# Optimizing a Trainium2 kernel written in Bass

```python
import numpy as np
import jax
import jax.numpy as jnp

def _softmax(x, axis=-1):
    return jax.nn.softmax(x, axis=axis)

def _gelu(x):
    return jax.nn.gelu(x, approximate=True)

def _silu(x):
    return jax.nn.silu(x)

def _sigmoid(x):
    return jax.nn.sigmoid(x)

def _layernorm(x, axis=-1, eps=1e-05):
    m = jnp.mean(x, axis=axis, keepdims=True)
    v = jnp.var(x, axis=axis, keepdims=True)
    return (x - m) / jnp.sqrt(v + eps)

def _scatter_add(tgt, idx, src, axis=0):
    return tgt.at[idx].add(src)

def _segment_sum(src, seg, n):
    return jax.ops.segment_sum(src, seg, n)
kernel_name = 'mk_cond_resid_d4_seqx_r8_d594d1'

def setup_inputs(seed: int=0):
    np.random.seed(seed)
    _w = jnp.asarray

    def _rec_inputs():
        import jax
        import jax.numpy as jnp
        _rk = jax.random.key(seed)
        x = -7.109e-05 + 0.9999 * jax.random.normal(jax.random.fold_in(_rk, 1), (64, 32, 256), jnp.float32)
        _lenS = 32 - jax.random.randint(jax.random.fold_in(_rk, 7), (64,), 0, max(1, 32 // 4) + 1, jnp.int32)
        _lenS2 = 32 - jax.random.randint(jax.random.fold_in(_rk, 8), (64,), 0, max(1, 32 // 4) + 1, jnp.int32)
        itok_B_1_198 = jax.random.randint(jax.random.fold_in(_rk, 11), (64,), 1, 199, jnp.int32)
        itok_Bx257_0_4111 = jax.random.randint(jax.random.fold_in(_rk, 12), (64, 257), 0, 514, jnp.int32)
        itok_B_37_3939 = jax.random.randint(jax.random.fold_in(_rk, 13), (64,), 37, 3940, jnp.int32)
        itok_B_0_3 = jax.random.randint(jax.random.fold_in(_rk, 14), (64,), 0, 4, jnp.int32)
        itok_B_0_7 = jax.random.randint(jax.random.fold_in(_rk, 15), (64,), 0, 8, jnp.int32)
        return (x, itok_B_1_198, itok_Bx257_0_4111, itok_B_37_3939, itok_B_0_3, itok_B_0_7)
    x, itok_B_1_198, itok_Bx257_0_4111, itok_B_37_3939, itok_B_0_3, itok_B_0_7 = _rec_inputs()

    def _L0_cond_setup():
        import jax, jax.numpy as jnp
        import numpy as np
        B, C, T = (128, 32, 256)
        S, D = (200, 32)
        key = jax.random.key(seed)
        k1, k2, k3 = jax.random.split(key, 3)
        x = jax.random.normal(k1, (B, C, T), dtype=jnp.float32)
        conditions = jax.random.randint(k2, (B,), 0, S, dtype=jnp.int64)
        weights = jax.random.normal(k3, (S, C, D), dtype=jnp.float32) / jnp.sqrt(jnp.float32(C))
        return {'x': x, 'conditions': conditions, 'weights': weights}
    _L0_cond_all = _L0_cond_setup()
    _L0_cond_in = {k: v for k, v in _L0_cond_all.items() if k in ('weights',)}
    del _L0_cond_all

    def _L1_cond_setup():
        import jax, jax.numpy as jnp
        import numpy as np
        H, G, HD = (8, 4, 32)
        GSZ = H // G
        BLOCK = 16
        WINDOW = 128
        SCALE = 256.0 ** (-0.5)
        EPS = 1e-06
        THETA = 10000.0
        B, T, D = (16, 4, 256)
        NBLK = 257

        def _rms(x, scale):
            var = jnp.mean(x * x, axis=-1, keepdims=True)
            return x * jax.lax.rsqrt(var + EPS) * (1.0 + scale)

        def _rope(x, pos):
            half = HD // 2
            inv = 1.0 / THETA ** (jnp.arange(half, dtype=jnp.float32) / half)
            ang = pos[:, :, None].astype(jnp.float32) * inv
            cos = jnp.cos(ang)[:, None, :, :]
            sin = jnp.sin(ang)[:, None, :, :]
            x1, x2 = (x[..., :half], x[..., half:])
            return jnp.concatenate([x1 * cos - x2 * sin, x2 * cos + x1 * sin], axis=-1)
        key = jax.random.key(seed)
        ks = jax.random.split(key, 10)
        inv_d = 1.0 / np.sqrt(D)
        return {'x': jax.random.normal(ks[0], (B, T, D), jnp.float32), 'Wq': jax.random.normal(ks[1], (H * HD, D), jnp.float32) * inv_d, 'Wk': jax.random.normal(ks[2], (G * HD, D), jnp.float32) * inv_d, 'Wv': jax.random.normal(ks[3], (G * HD, D), jnp.float32) * inv_d, 'Wo': jax.random.normal(ks[4], (D, H * HD), jnp.float32) * inv_d, 'q_norm_scale': jax.random.normal(ks[5], (HD,), jnp.float32) * 0.02, 'k_norm_scale': jax.random.normal(ks[6], (HD,), jnp.float32) * 0.02, 'k_blocks': jax.random.normal(ks[7], (B * NBLK, G, BLOCK, HD), jnp.float32), 'v_blocks': jax.random.normal(ks[8], (B * NBLK, G, BLOCK, HD), jnp.float32), 'block_tables': jnp.arange(B * NBLK, dtype=jnp.int32).reshape(B, NBLK), 'kv_lens': jax.random.randint(ks[9], (B,), 0, 512, dtype=jnp.int32)}
    _L1_cond_all = _L1_cond_setup()
    _L1_cond_in = {k: v for k, v in _L1_cond_all.items() if k in ('Wq', 'Wk', 'Wv', 'Wo', 'q_norm_scale', 'k_norm_scale', 'k_blocks', 'v_blocks')}
    del _L1_cond_all

    def _L2_cond_setup():
        import jax, jax.numpy as jnp
        import numpy as np
        B, S, D_IN, D_OUT, R, E = (8, 256, 256, 256, 16, 4)
        key = jax.random.key(seed)
        ks = jax.random.split(key, 7)
        x = jax.random.normal(ks[0], (B, S, D_IN), dtype=jnp.float32)
        W_base = jax.random.normal(ks[1], (D_OUT, D_IN), dtype=jnp.float32) * 0.02
        Wt = jax.random.normal(ks[2], (D_IN, D_IN), dtype=jnp.float32) * 0.02
        A = jax.random.normal(ks[3], (E, R, D_IN), dtype=jnp.float32) * 0.02
        B_w = jax.random.normal(ks[4], (E, D_OUT, R), dtype=jnp.float32) * 0.02
        Wp = jax.random.normal(ks[5], (D_OUT, D_OUT), dtype=jnp.float32) * 0.02
        scaling = jnp.ones((E,), dtype=jnp.float32)
        adapter_idx = jax.random.randint(ks[6], (B,), 0, E)
        return {'x': x, 'W_base': W_base, 'Wt': Wt, 'A': A, 'B_w': B_w, 'Wp': Wp, 'scaling': scaling, 'adapter_idx': adapter_idx}
    _L2_cond_all = _L2_cond_setup()
    _L2_cond_in = {k: v for k, v in _L2_cond_all.items() if k in ('W_base', 'Wt', 'A', 'B_w', 'Wp', 'scaling')}
    del _L2_cond_all

    def _L3_cond_setup():
        import jax, jax.numpy as jnp
        import numpy as np
        B, C, D, T, N_SUBJECTS = (128, 32, 32, 256, 8)
        key = jax.random.key(seed)
        kx, ks, kw = jax.random.split(key, 3)
        x = jax.random.normal(kx, (B, C, T), dtype=jnp.float32)
        subjects = jax.random.randint(ks, (B,), 0, N_SUBJECTS, dtype=jnp.int64)
        weights = jax.random.normal(kw, (N_SUBJECTS, C, D), dtype=jnp.float32) * (1.0 / C ** 0.5)
        return {'x': x, 'subjects': subjects, 'weights': weights}
    _L3_cond_all = _L3_cond_setup()
    _L3_cond_in = {k: v for k, v in _L3_cond_all.items() if k in ('weights',)}
    del _L3_cond_all
    return {'x': x, 'itok_B_1_198': itok_B_1_198, 'itok_Bx257_0_4111': itok_Bx257_0_4111, 'itok_B_37_3939': itok_B_37_3939, 'itok_B_0_3': itok_B_0_3, 'itok_B_0_7': itok_B_0_7, 'L0_cond_weights': _L0_cond_in['weights'], 'L1_cond_Wq': _L1_cond_in['Wq'], 'L1_cond_Wk': _L1_cond_in['Wk'], 'L1_cond_Wv': _L1_cond_in['Wv'], 'L1_cond_Wo': _L1_cond_in['Wo'], 'L1_cond_q_norm_scale': _L1_cond_in['q_norm_scale'], 'L1_cond_k_norm_scale': _L1_cond_in['k_norm_scale'], 'L1_cond_k_blocks': _L1_cond_in['k_blocks'], 'L1_cond_v_blocks': _L1_cond_in['v_blocks'], 'L2_cond_W_base': _L2_cond_in['W_base'], 'L2_cond_Wt': _L2_cond_in['Wt'], 'L2_cond_A': _L2_cond_in['A'], 'L2_cond_B_w': _L2_cond_in['B_w'], 'L2_cond_Wp': _L2_cond_in['Wp'], 'L2_cond_scaling': _L2_cond_in['scaling'], 'L3_cond_weights': _L3_cond_in['weights']}

def reference(x, itok_B_1_198, itok_Bx257_0_4111, itok_B_37_3939, itok_B_0_3, itok_B_0_7, L0_cond_weights, L1_cond_Wq, L1_cond_Wk, L1_cond_Wv, L1_cond_Wo, L1_cond_q_norm_scale, L1_cond_k_norm_scale, L1_cond_k_blocks, L1_cond_v_blocks, L2_cond_W_base, L2_cond_Wt, L2_cond_A, L2_cond_B_w, L2_cond_Wp, L2_cond_scaling, L3_cond_weights):
    import jax
    import jax.numpy as jnp

    def _L0_cond_ref(x, conditions, weights):
        import jax, jax.numpy as jnp
        import numpy as np
        B, C, T = (128, 32, 256)
        S, D = (200, 32)
        w = weights[conditions]
        return jnp.einsum('bct,bcd->bdt', x, w)

    def _L1_cond_ref(x, Wq, Wk, Wv, Wo, q_norm_scale, k_norm_scale, k_blocks, v_blocks, block_tables, kv_lens):
        import jax, jax.numpy as jnp
        import numpy as np
        H, G, HD = (8, 4, 32)
        GSZ = H // G
        BLOCK = 16
        WINDOW = 128
        SCALE = 256.0 ** (-0.5)
        EPS = 1e-06
        THETA = 10000.0
        B, T, D = (16, 4, 256)
        NBLK = 257

        def _rms(x, scale):
            var = jnp.mean(x * x, axis=-1, keepdims=True)
            return x * jax.lax.rsqrt(var + EPS) * (1.0 + scale)

        def _rope(x, pos):
            half = HD // 2
            inv = 1.0 / THETA ** (jnp.arange(half, dtype=jnp.float32) / half)
            ang = pos[:, :, None].astype(jnp.float32) * inv
            cos = jnp.cos(ang)[:, None, :, :]
            sin = jnp.sin(ang)[:, None, :, :]
            x1, x2 = (x[..., :half], x[..., half:])
            return jnp.concatenate([x1 * cos - x2 * sin, x2 * cos + x1 * sin], axis=-1)
        Bx, Tx, _ = x.shape
        q = jnp.einsum('btd,od->bto', x, Wq).reshape(Bx, Tx, H, HD).transpose(0, 2, 1, 3)
        k = jnp.einsum('btd,od->bto', x, Wk).reshape(Bx, Tx, G, HD).transpose(0, 2, 1, 3)
        v = jnp.einsum('btd,od->bto', x, Wv).reshape(Bx, Tx, G, HD).transpose(0, 2, 1, 3)
        q = _rms(q, q_norm_scale)
        k = _rms(k, k_norm_scale)
        pos = kv_lens[:, None] + jnp.arange(Tx, dtype=jnp.int32)
        q = _rope(q, pos)
        k = _rope(k, pos)
        slot = pos // BLOCK
        off = pos % BLOCK
        blk = jnp.take_along_axis(block_tables, slot, axis=1)
        k_blocks = k_blocks.at[blk, :, off, :].set(k.transpose(0, 2, 1, 3))
        v_blocks = v_blocks.at[blk, :, off, :].set(v.transpose(0, 2, 1, 3))
        k_all = k_blocks[block_tables].transpose(0, 2, 1, 3, 4).reshape(Bx, G, -1, HD)
        v_all = v_blocks[block_tables].transpose(0, 2, 1, 3, 4).reshape(Bx, G, -1, HD)
        S = k_all.shape[2]
        qg = q.reshape(Bx, G, GSZ, Tx, HD)
        scores = jnp.einsum('bghtd,bgsd->bghts', qg, k_all) * SCALE
        kpos = jnp.arange(S, dtype=jnp.int32)
        allowed = (kpos[None, None, :] <= pos[:, :, None]) & (kpos[None, None, :] > pos[:, :, None] - WINDOW)
        scores = jnp.where(allowed[:, None, None, :, :], scores, -jnp.inf)
        p = jax.nn.softmax(scores, axis=-1)
        o = jnp.einsum('bghts,bgsd->bghtd', p, v_all).reshape(Bx, H, Tx, HD)
        o = o.transpose(0, 2, 1, 3).reshape(Bx, Tx, H * HD)
        return jnp.einsum('bto,do->btd', o, Wo)

    def _L2_cond_ref(x, W_base, Wt, A, B_w, Wp, scaling, adapter_idx):
        import jax, jax.numpy as jnp
        import numpy as np
        B, S, D_IN, D_OUT, R, E = (8, 256, 256, 256, 16, 4)
        base = jnp.einsum('bsi,oi->bso', x, W_base)
        h = jnp.einsum('bsi,ji->bsj', x, Wt)
        Ab = A[adapter_idx]
        Bb = B_w[adapter_idx]
        sc = scaling[adapter_idx]
        z = jnp.einsum('bsj,brj->bsr', h, Ab)
        l = jnp.einsum('bsr,bor->bso', z, Bb)
        lora_out = jnp.einsum('bso,po->bsp', l, Wp) * sc[:, None, None]
        return base + lora_out

    def _L3_cond_ref(x, subjects, weights):
        import jax, jax.numpy as jnp
        import numpy as np
        B, C, D, T, N_SUBJECTS = (128, 32, 32, 256, 8)
        w = weights[subjects]
        out = jnp.einsum('bct,bcd->bdt', x, w)
        return out
    x = x + _L0_cond_ref(x, itok_B_1_198, L0_cond_weights)
    x = x + _L1_cond_ref(x, L1_cond_Wq, L1_cond_Wk, L1_cond_Wv, L1_cond_Wo, L1_cond_q_norm_scale, L1_cond_k_norm_scale, L1_cond_k_blocks, L1_cond_v_blocks, itok_Bx257_0_4111, itok_B_37_3939)
    x = x + _L2_cond_ref(x, L2_cond_W_base, L2_cond_Wt, L2_cond_A, L2_cond_B_w, L2_cond_Wp, L2_cond_scaling, itok_B_0_3)
    x = x + _L3_cond_ref(x, itok_B_0_7, L3_cond_weights)
    return x

_drawn_inputs = setup_inputs


def setup_inputs(seed=0):
    import zlib

    import numpy as np

    out = dict(_drawn_inputs(seed))
    spreads = {'L2_cond_scaling': (1.0, 0.6)}
    factors = {'L1_cond_Wk': 9.447,
     'L1_cond_q_norm_scale': 26.242,
     'L1_cond_k_norm_scale': 64.0,
     'L1_cond_k_blocks': 2.985,
     'L2_cond_Wt': 8.0,
     'L2_cond_A': 8.0,
     'L2_cond_B_w': 8.0,
     'L2_cond_Wp': 8.0}
    for name, (base, spread) in spreads.items():
        noise = np.random.default_rng([zlib.crc32(name.encode()), seed]).standard_normal(out[name].shape)
        drawn = base * np.exp(spread * noise) if base else spread * noise
        out[name] = jnp.asarray(drawn.astype(out[name].dtype))
    for name, factor in factors.items():
        out[name] = (out[name] * factor).astype(out[name].dtype)
    return out
```

```python
from contextlib import ExitStack

import numpy as np
import concourse.bass as bass
from concourse import mybir

ALU = mybir.AluOpType
ACT = mybir.ActivationFunctionType
AX_X = mybir.AxisListType.X
F32 = mybir.dt.float32
BF16 = mybir.dt.bfloat16
I32 = mybir.dt.int32

B, TOK, D = 64, 32, 256
H, G, HD = 8, 4, 32
GSZ = H // G
BLOCK, NBLK, NPOOL = 16, 257, 4112
WINDOW = 128
SCALE = 256.0 ** -0.5
EPS = 1e-6
THETA = 10000.0
E, R = 4, 16
NB = 128 // TOK
NT = B // NB
ROW = 2 * G * HD
BACK = WINDOW // BLOCK
OWN = 3
SPAN = BACK + OWN
SEGS = OWN * B
R4 = WINDOW // 4
Q2 = 18
NKB = 4 * R4
NK = NKB + 2 * Q2
KW = 180
BIG = float(2 ** 20)
NEG = -1e30
PI = float(np.pi)
MAGIC = 1.5 * 2.0 ** 23

_COLS = [("ident", 128), ("slot", NBLK), ("span", SPAN), ("m4", 36), ("m8", 24), ("m16", 48),
         ("later", OWN * B * OWN), ("seg1", OWN), ("tok", TOK), ("inv", HD // 2),
         ("backpos", NKB), ("ownpos", 2 * Q2), ("adapter", 1), ("batch", NB)]
COL = {}
_at = 0
for _n, _w in _COLS:
    COL[_n] = (_at, _at + _w)
    _at += _w
NCONST = _at


def constants():
    c = np.zeros((128, NCONST), np.float32)

    def put(name, value):
        a, b = COL[name]
        c[:, a:b] = np.broadcast_to(value, (128, b - a))

    put("ident", np.eye(128, dtype=np.float32))
    put("slot", np.arange(NBLK))
    put("span", np.arange(SPAN) - BACK)
    put("m4", np.arange(36) % 4)
    put("m8", np.arange(24) % 8)
    put("m16", np.arange(48) % 16)
    late = np.zeros((128, OWN, B, OWN), np.float32)
    for j in range(OWN):
        late[:, j] = (OWN * np.arange(128) + j)[:, None, None] > (OWN * np.arange(B)[:, None] + np.arange(OWN))
    put("later", late.reshape(128, -1))
    put("seg1", np.arange(128)[:, None] + B * np.arange(OWN) + 1)
    put("tok", np.arange(TOK))
    half = HD // 2
    put("inv", np.float32(1.0) / np.float32(THETA) ** (np.arange(half, dtype=np.float32) / np.float32(half)))
    put("backpos", (4 * np.arange(R4)[None, :] + np.arange(4)[:, None]).reshape(-1))
    put("ownpos", (2 * np.arange(Q2)[None, :] + np.arange(2)[:, None]).reshape(-1))
    put("adapter", (np.arange(128) // R)[:, None])
    put("batch", (np.arange(128) // TOK)[:, None] == np.arange(NB))
    return c


def at_step(h, u, lag):
    return 2 * h + (u - lag), h + (u - lag) // 2, (u - lag) % 2


def valid(t):
    return not isinstance(t, int) or 0 <= t < NT


def reused(t):
    return not isinstance(t, int) or t >= 2


def steps(eng, body, total, first, last):
    for i in range(first):
        body(i // 2, i % 2)
    with eng.Fori(first // 2, last // 2) as h:
        body(h, 0)
        body(h, 1)
    for i in range(last, total):
        body(i // 2, i % 2)


def build(nc, x, cond, table, kv_lens, adapter, subject, w0, wqkv, wo, qscale, kscale, pool,
          wbase, wt, at, bt, wp, scaling, w3, consts, out):
    half = HD // 2
    table_i = table
    merged = nc.dram_tensor("merged", [SEGS * BLOCK, ROW], F32).ap()
    blocks_d = nc.dram_tensor("blocks_scratch", [B, SPAN], F32).ap()
    pool_rows4 = pool.rearrange("(r f) n -> r (f n)", f=4)
    pool_blocks = pool.rearrange("(r f) n -> r (f n)", f=BLOCK)
    merged_rows4 = merged.rearrange("(r f) n -> r (f n)", f=4)
    merged_rows2 = merged.rearrange("(r f) n -> r (f n)", f=2)
    merged_blocks = merged.rearrange("(r f) n -> r (f n)", f=BLOCK)

    with ExitStack() as ctx:
        def sb(name, shape, dt=F32):
            return ctx.enter_context(nc.sbuf_tensor(name, shape, dt))

        def sem(name):
            return ctx.enter_context(nc.semaphore(name))

        con = sb("con", [128, NCONST])

        def cc(name, p=128):
            a, b = COL[name]
            return con[0:p, a:b]

        ident = cc("ident")
        identb = sb("identb", [128, 128], BF16)
        xall = sb("xall", [128, NT, D])
        qT = sb("qT", [128, NT, H * TOK])
        big = sb("big", [128, OWN * BLOCK * ROW])
        wqkv_sb = sb("wqkv_sb", [128, 2, 512])
        wo_sb = sb("wo_sb", [128, 2, D])
        wbase_sb = sb("wbase_sb", [128, 2, D])
        wt_sb = sb("wt_sb", [128, 2, D])
        at_sb = sb("at_sb", [128, 2, E * R])
        bt_sb = sb("bt_sb", [128, 2, E * R])
        wp_sb = sb("wp_sb", [128, 2, D])
        aw = sb("aw", [128, 2, E * R])
        bw = sb("bw", [E * R, D])
        w0bd = sb("w0bd", [128, 2, 128])
        w3bd = sb("w3bd", [128, 2, 128])
        qsc = sb("qsc", [128, HD])
        ksc = sb("ksc", [128, HD])
        cond_sb = sb("cond_sb", [1, B], I32)
        subj_sb = sb("subj_sb", [1, B], I32)
        adp_i = sb("adp_i", [E * R, B], I32)
        adp_f = sb("adp_f", [E * R, B])
        scal = sb("scal", [E * R, 1])
        zscale = sb("zscale", [E * R, B])
        idx = sb("idx", [128, 4, NT], I32)
        row_now = sb("row_now", [128, 4, 2], I32)
        pos_now = sb("pos_now", [128, 2, 2])
        pos3 = sb("pos3", [128, 3, NT])
        kt_rope = sb("kt_rope", [128, 2048])
        ropeC = kt_rope[:, 0:1024].rearrange("p (t k d) -> p t k d", t=NT, k=2)
        ropeS = kt_rope[:, 1024:2048].rearrange("p (t k d) -> p t k d", t=NT, k=2)
        kT = kt_rope[:, 0:2 * G * KW].rearrange("p (a g k) -> p a g k", a=2, g=G)
        mask = sb("mask", [128, 2, NK], BF16)
        work = sb("work", [128, 6480])

        used = [0]

        def carve(*shape):
            n = int(np.prod(shape))
            v = work[:, used[0]:used[0] + n]
            used[0] += n
            names = "abcd"[:len(shape)]
            if len(shape) == 1:
                return v
            return v.rearrange(f"p ({' '.join(names)}) -> p {' '.join(names)}",
                               **{k: s for k, s in zip(names, shape)})

        x1s = carve(2, D)
        x1T = carve(2, 2, 128)
        kqs = carve(2, 384)
        sq = carve(2, 384)
        ropeA = carve(2, 384)
        ropeB = carve(2, 384)
        rsum = carve(2, 384)
        kvrow = carve(2, ROW)
        qrot = carve(2, D)
        qrT = carve(2, D)
        ss = carve(2, 12)
        rt = carve(2, 12)
        rinv = carve(2, 12)
        used[0] = 0
        prob = carve(2, H, KW)
        pT = carve(2, 6, H * TOK)

        stage = big[0:B, :].rearrange("p (j n) -> p j n", j=OWN)
        vbd = big[:, 0:6144].rearrange("p (a f g c) -> p a f g c", a=2, f=6, g=G)
        qbd = big[:, 6144:8192].rearrange("p (a h c) -> p a h c", a=2, h=H)
        own = big[:, 8192:9216].rearrange("p (a n) -> p a n", a=2)
        kvb = big[:, 9216:11264].rearrange("p (a n) -> p a n", a=2)

        mx = sb("mx", [128, 2, H])
        nmx = sb("nmx", [128, 2, H])
        den = sb("den", [128, 2, H])
        rden = sb("rden", [128, 2, H])
        oraw = sb("oraw", [128, D])
        onrm = sb("onrm", [128, D])
        onT = sb("onT", [128, 2, 128])
        x2s = sb("x2s", [128, 2, D])
        x2T = sb("x2T", [128, 2, 128])
        zm = sb("zm", [E * R, 128])
        x3s = sb("x3s", [128, 2, D])
        x4s = sb("x4s", [128, 2, D])

        blk_i = sb("blk_i", [B, SPAN], I32)
        more = sb("more", [B, 192 + 288])

        scratch = sb("scratch", [B, 4096])
        sused = [0]

        def scr(n, p=B):
            v = scratch[0:p, sused[0]:sused[0] + n]
            sused[0] += n
            return v

        kv_i = scr(1).bitcast(I32)
        tab_i = scr(NBLK).bitcast(I32)
        kvf = scr(1)
        tabf = scr(NBLK)
        off0 = scr(1)
        slot0 = scr(1)
        target = scr(SPAN)
        pick = x2s[0:B, :, :].rearrange('p k n -> p (k n)')[:, 0:NBLK]
        blk = scr(SPAN)
        bits = scr(4)
        rest = scr(4)
        allblk = scr(B * SPAN)
        eq = [scr(B * SPAN) for _ in range(OWN)]
        el = [v[0:B, 0:B * OWN] for v in (oraw, onrm, more)]
        cover = more[:, 416:467].rearrange("p (j n) -> p j n", j=OWN)
        dead = scr(OWN * 17).rearrange("p (j n) -> p j n", j=OWN)
        canon_seg = scr(OWN)
        canon = scr(SPAN)
        cmiss = scr(SPAN)
        cidx = scr(SPAN)
        rows4 = scr(72).rearrange("p (k m) -> p k m", k=2)
        rows4b = scr(66).rearrange("p (k m) -> p k m", k=2)
        tmp4 = scr(66).rearrange("p (k m) -> p k m", k=2)
        rows2 = scr(24)
        rows2b = scr(24)
        tmp2 = scr(24)
        rows1 = scr(48)
        rows1b = scr(48)
        tmp1 = scr(48)
        idxf = more[:, 192:320].rearrange("p (k r) -> p k r", k=4)
        posf = more[:, 320:416].rearrange("p (k r) -> p k r", k=3)
        lim = scr(1)
        ang = x4s[:, 0, :].rearrange("p (t d) -> p t d", t=NT)
        turn = x4s[:, 1, :].rearrange("p (t d) -> p t d", t=NT)
        redu = x2s[:, :, :].rearrange("p k (t d) -> p k t d", t=NT)
        trig = x3s[:, :, :].rearrange("p k (t d) -> p k t d", t=NT)

        bank = [ctx.enter_context(nc.psum_tensor(f"bank{i}", [128, 512], F32)) for i in range(8)]
        ps_l0 = [bank[0], bank[1]]
        ps_xT = [bank[2], bank[3]]
        ps_qkv = [bank[4], bank[5]]
        ps_idx = bank[6]
        ps_pre = bank[7]
        ps_sc = bank[0:3]
        ps_o = bank[3]
        ps_t = bank[4]
        ps_wo = bank[5][:, 0:D]
        ps_l3 = bank[7][:, 128:128 + D]
        ps_l2 = bank[6][:, 0:D]
        ps_z = bank[7][0:E * R, 0:128]
        HEADS = [range(0, 3), range(3, 6), range(6, 8)]

        s_small, s_con, s_w = sem("s_small"), sem("s_con"), sem("s_w")
        s_x = [sem(f"s_x{i}") for i in range(4)]
        s_w0 = [sem("s_w0a"), sem("s_w0b")]
        s_w3 = [sem("s_w3a"), sem("s_w3b")]
        s_zero = sem("s_zero")
        s_ix = sem("s_ix")
        s_blkd, s_blkr = sem("s_blkd"), sem("s_blkr")
        s_ipe = sem("s_ipe")
        s_idx = sem("s_idx")
        s_trig, s_rope = sem("s_trig"), sem("s_rope")
        s_pre, s_prec = sem("s_pre"), sem("s_prec")
        s_stage = [sem(f"s_stage{j}") for j in range(OWN)]
        s_init = sem("s_init")
        s_cache = [sem("s_cachea"), sem("s_cacheb")]
        l0_done, x1_done, x1_saved = sem("l0_done"), sem("x1_done"), sem("x1_saved")
        xT_done, xT_copied, qkv_done = sem("xT_done"), sem("xT_copied"), sem("qkv_done")
        kq_copied, v_copied, sq_done = sem("kq_copied"), sem("v_copied"), sem("sq_done")
        ss_done, rt_done, rinv_done = sem("ss_done"), sem("rt_done"), sem("rinv_done")
        prods_done, rsum_done, krow_done = sem("prods_done"), sem("rsum_done"), sem("krow_done")
        qrot_done, qT_done = sem("qrot_done"), sem("qT_done")
        s_scat = [sem("s_scata"), sem("s_scatb")]
        s_merge = [sem("s_mergea"), sem("s_mergeb")]
        s_own = [sem("s_owna"), sem("s_ownb")]
        kT_part, kT_done = sem("kT_part"), sem("kT_done")
        qbd_done, mask_done, vbd_done = sem("qbd_done"), sem("mask_done"), sem("vbd_done")
        sc_done, mx_done, nmx_done, exp_done = sem("sc_done"), sem("mx_done"), sem("nmx_done"), sem("exp_done")
        pT_done, pv_done, oraw_done, rden_done = sem("pT_done"), sem("pv_done"), sem("oraw_done"), sem("rden_done")
        onrm_done, onT_done, onT_copied = sem("onrm_done"), sem("onT_done"), sem("onT_copied")
        wo_done, x2_done, x2T_done, x2T_copied = sem("wo_done"), sem("x2_done"), sem("x2T_done"), sem("x2T_copied")
        z_done, zm_done, l2_done, x3_done = sem("z_done"), sem("zm_done"), sem("l2_done"), sem("x3_done")
        l3_done, x4_done = sem("l3_done"), sem("x4_done")
        s_out = [sem("s_outa"), sem("s_outb")]
        s_pad, s_big = sem("s_pad"), sem("s_big")
        row1_copied, row4_copied, rowm_copied, pos_copied = (
            sem("row1_copied"), sem("row4_copied"), sem("rowm_copied"), sem("pos_copied"))
        qrT_done = sem("qrT_done")
        desc_init, desc_scat, desc_cache, desc_fetch = sem("desc_init"), sem("desc_scat"), sem("desc_cache"), sem("desc_fetch")

        ZEROED = 2
        P1 = (20, 6, 16)
        P2 = (NT + 3, 6, 14)

        block = ctx.enter_context(nc.Block())

        @block.sync
        def _(sp):
            sp.dma_start(kv_i, kv_lens).then_inc(s_small, 16)
            sp.dma_start(tab_i, table_i).then_inc(s_small, 16)
            sp.dma_start(con[:, :], consts).then_inc(s_con, 16)
            sp.dma_start(cond_sb[:, :], cond).then_inc(s_w, 16)
            sp.dma_start(subj_sb[:, :], subject).then_inc(s_w, 16)
            xv = x.rearrange("(t p) n -> p t n", p=128)
            for i in range(4):
                sp.dma_start(xall[:, 4 * i:4 * i + 4, :], xv[:, 4 * i:4 * i + 4, :]).then_inc(s_x[i], 16)
            sp.wait_ge(s_blkd, 16)
            sp.dma_start(allblk, blocks_d.rearrange("b i -> (b i)").unsqueeze(0).broadcast_to([B, B * SPAN])
                         ).then_inc(s_blkr, 16)
            sp.wait_ge(s_w, 16 * 13)
            sp.wait_ge(s_zero, ZEROED)

            def diagonal(t, p, weights, numbers, buf, signal):
                for b in range(NB):
                    n = sp.value_load(numbers[0:1, bass.ds(t * NB + b, 1)], min_val=0, max_val=weights.shape[0] - 1)
                    sp.dma_start(buf[32 * b:32 * b + 32, p, 32 * b:32 * b + 32],
                                 weights[bass.ds(n, 1), :, :].rearrange("o c d -> (o c) d")).then_inc(signal[p], 16)

            def phase1(h, u):
                t, k, p = at_step(h, u, 0)
                if valid(t):
                    if reused(t):
                        sp.wait_ge(l0_done, t - 1)
                    diagonal(t, p, w0, cond_sb, w0bd, s_w0)

            steps(sp, phase1, NT, 2, NT)

            def phase2(h, u):
                t, k, p = at_step(h, u, 0)
                if valid(t):
                    if reused(t):
                        sp.wait_ge(l3_done, t - 1)
                    diagonal(t, p, w3, subj_sb, w3bd, s_w3)
                t, k, p = at_step(h, u, 1)
                if valid(t):
                    sp.wait_ge(x4_done, t + 1)
                    sp.dma_start(out[bass.ds(t * 128, 128), :], x4s[:, p, :]).then_inc(s_out[p], 16)

            steps(sp, phase2, NT + 1, 4, 14)
            for p in range(2):
                sp.wait_ge(s_out[p], 16 * (NT // 2))

        @block.gpsimd
        def _(pl):
            tick = pl.alloc_register("tick")
            pl.reg_mov(tick, 0)

            def wait(signal, n):
                if not isinstance(n, int):
                    pl.reg_mov(tick, n)
                    n = pl.snap(tick)
                    pl.wait_ge(s_idx, 4)
                pl.wait_ge(signal, n)

            pl.memset(w0bd[:, :, :], 0.0).then_inc(s_zero, 1)
            pl.memset(w3bd[:, :, :], 0.0).then_inc(s_zero, 1)

            wait(s_idx, 1)
            for j in range(OWN):
                pl.indirect_dma_start(
                    out=stage[:, j, :], out_offset=None, in_=pool_blocks,
                    in_offset=bass.IndirectOffsetOnAxis(ap=blk_i[:, BACK + j:BACK + j + 1], axis=0),
                    bounds_check=NPOOL - 1, oob_is_err=False, engine_sem=desc_init).then_inc(s_stage[j], 16)
                wait(desc_init, j + 1)

            wait(s_w, 16 * 13)
            pl.tensor_scalar(ksc[:, :], ksc[:, :], 1.0, None, ALU.add).then_inc(s_rope, 1)
            pl.tensor_scalar(qsc[:, :], qsc[:, :], 1.0, None, ALU.add).then_inc(s_rope, 1)
            wait(s_rope, 2)
            wait(s_trig, 2)
            for i, scl in enumerate((ksc, qsc)):
                for lo in range(2):
                    mine = scl[:, half * lo:half * lo + half].unsqueeze(1).broadcast_to([128, NT, half])
                    other = scl[:, half - half * lo:HD - half * lo].unsqueeze(1).broadcast_to([128, NT, half])
                    pl.tensor_tensor(ropeC[:, :, i, half * lo:half * lo + half], trig[:, 1], mine,
                                     ALU.mult).then_inc(s_rope, 1)
                    pl.tensor_tensor(ropeS[:, :, i, half * lo:half * lo + half], trig[:, 0], other,
                                     ALU.mult).then_inc(s_rope, 1)
            wait(s_rope, 10)
            for i in range(2):
                v = ropeS[:, :, i, 0:half]
                pl.tensor_scalar(v, v, -1.0, None, ALU.mult).then_inc(s_rope, 1)
            wait(s_rope, 12)

            def cached(t, p):
                pl.tensor_copy(row_now[:, 0, p:p + 1], idx[:, 0, bass.ds(t, 1)]).then_inc(row4_copied, 1)
                wait(row4_copied, t + 1)
                pl.indirect_dma_start(
                    out=kvb[:, p, :], out_offset=None, in_=pool_rows4,
                    in_offset=bass.IndirectOffsetOnAxis(ap=row_now[:, 0, p:p + 1], axis=0),
                    bounds_check=4 * NPOOL - 1, oob_is_err=False, engine_sem=desc_cache).then_inc(s_cache[p], 16)
                wait(desc_cache, t + 1)

            def phase1(h, u):
                t, k, p = at_step(h, u, 0)
                if valid(t):
                    wait(x1_done, t + 1)
                    pl.tensor_copy(xall[:, t, :], x1s[:, p, :]).then_inc(x1_saved, 1)
                t, k, p = at_step(h, u, 2)
                if valid(t):
                    wait(kq_copied, t + 1)
                    if reused(t):
                        wait(rsum_done, t - 1)
                    for i, (a, n) in enumerate(((0, G), (128, H))):
                        src = kqs[:, p, a:a + n * HD].rearrange("p (n d) -> p n d", d=HD)
                        da = ropeA[:, p, a:a + n * HD].rearrange("p (n d) -> p n d", d=HD)
                        db = ropeB[:, p, a:a + n * HD].rearrange("p (n d) -> p n d", d=HD)
                        c = ropeC[:, bass.ds(t, 1), i, :].broadcast_to([128, n, HD])
                        s_lo = ropeS[:, bass.ds(t, 1), i, 0:half].broadcast_to([128, n, half])
                        s_hi = ropeS[:, bass.ds(t, 1), i, half:HD].broadcast_to([128, n, half])
                        pl.tensor_tensor(da, src, c, ALU.mult).then_inc(prods_done, 1)
                        pl.tensor_tensor(db[:, :, 0:half], src[:, :, half:HD], s_lo, ALU.mult).then_inc(prods_done, 1)
                        pl.tensor_tensor(db[:, :, half:HD], src[:, :, 0:half], s_hi, ALU.mult).then_inc(prods_done, 1)
                t, k, p = at_step(h, u, 3)
                if valid(t):
                    wait(krow_done, t + 1)
                    wait(v_copied, t + 1)
                    if isinstance(t, int) and t == 0:
                        wait(s_idx, 4)
                        wait(s_init, 16 * OWN)
                    if reused(t):
                        wait(s_scat[p], 16 * k)
                    pl.tensor_copy(row_now[:, 3, p:p + 1], idx[:, 3, bass.ds(t, 1)]).then_inc(row1_copied, 1)
                    wait(row1_copied, t + 1)
                    pl.indirect_dma_start(
                        out=merged, out_offset=bass.IndirectOffsetOnAxis(ap=row_now[:, 3, p:p + 1], axis=0),
                        in_=kvrow[:, p, :], in_offset=None,
                        bounds_check=SEGS * BLOCK - 1, oob_is_err=False, engine_sem=desc_scat).then_inc(s_scat[p], 16)
                    wait(desc_scat, t + 1)
                if isinstance(h, int) and 2 * h + u == 4:
                    wait(s_init, 16 * OWN)
                    wait(s_idx, 4)
                    pl.memset(own, 0.0).then_inc(s_big, 1)
                    cached(0, 0)
                    cached(1, 1)

            steps(pl, phase1, *P1)

            for p in range(2):
                wait(s_scat[p], 16 * (NT // 2))
            wait(s_big, 1)

            def fetch(t, k, p):
                pl.tensor_copy(row_now[:, 1:3, p:p + 1], idx[:, 1:3, bass.ds(t, 1)]).then_inc(rowm_copied, 1)
                wait(rowm_copied, t + 1)
                wait(s_cache[p], 16 * (k + 1))
                pl.indirect_dma_start(
                    out=kvb[:, p, :], out_offset=None, in_=merged_rows4,
                    in_offset=bass.IndirectOffsetOnAxis(ap=row_now[:, 1, p:p + 1], axis=0),
                    bounds_check=SEGS * 4 - 1, oob_is_err=False, engine_sem=desc_fetch).then_inc(s_merge[p], 16)
                wait(desc_fetch, 2 * t + 1)
                pl.indirect_dma_start(
                    out=own[:, p, :], out_offset=None, in_=merged_rows2,
                    in_offset=bass.IndirectOffsetOnAxis(ap=row_now[:, 2, p:p + 1], axis=0),
                    bounds_check=SEGS * 8 - 1, oob_is_err=False, engine_sem=desc_fetch).then_inc(s_own[p], 16)
                wait(desc_fetch, 2 * t + 2)

            fetch(0, 0, 0)
            wait(qT_done, NT)
            for p in range(2):
                pl.memset(prob[:, p, :, NK:KW], 0.0).then_inc(s_pad, 1)

            def phase2(h, u):
                t1, k1, p1 = at_step(h, u, -1)
                if valid(t1):
                    if reused(t1):
                        wait(kT_done, t1 - 1)
                        wait(vbd_done, 8 * (t1 - 1))
                    fetch(t1, k1, p1)
                t, k, p = at_step(h, u, 0)
                if valid(t):
                    if reused(t):
                        wait(sc_done, 3 * (t - 1))
                    pl.tensor_copy(pos_now[:, :, p:p + 1], pos3[:, 0:2, bass.ds(t, 1)]).then_inc(pos_copied, 1)
                    wait(pos_copied, t + 1)
                    pl.tensor_scalar(mask[:, p, 0:NKB], cc("backpos"), pos_now[:, 0, p:p + 1], NEG,
                                     ALU.is_lt, ALU.mult).then_inc(mask_done, 1)
                    pl.tensor_scalar(mask[:, p, NKB:NK], cc("ownpos"), pos_now[:, 1, p:p + 1], NEG,
                                     ALU.is_gt, ALU.mult).then_inc(mask_done, 1)
                    wait(s_merge[p], 16 * (k + 1))
                    wait(s_own[p], 16 * (k + 1))
                    if reused(t):
                        wait(pv_done, t - 1)
                    old = kvb[:, p, :].rearrange("p (f k g d) -> p f k g d", f=4, k=2, g=G)
                    new = own[:, p, :].rearrange("p (f k g d) -> p f k g d", f=2, k=2, g=G)
                    for b in range(NB):
                        only = con[:, COL["batch"][0] + b:COL["batch"][0] + b + 1]
                        pl.tensor_scalar(vbd[:, p, 0:4, :, 32 * b:32 * b + 32], old[:, :, 1], only, None,
                                         ALU.mult).then_inc(vbd_done, 1)
                        pl.tensor_scalar(vbd[:, p, 4:6, :, 32 * b:32 * b + 32], new[:, :, 1], only, None,
                                         ALU.mult).then_inc(vbd_done, 1)
                t2, k2, p2 = at_step(h, u, -2)
                if valid(t2):
                    wait(kT_done, t2 - 1)
                    wait(vbd_done, 8 * (t2 - 1))
                    cached(t2, p2)

            steps(pl, phase2, NT, 4, 14)

        @block.scalar
        def _(act):
            for dst, src in ((qsc[:, :], qscale.broadcast_to([128, HD])), (ksc[:, :], kscale.broadcast_to([128, HD])),
                             (adp_i[:, :], adapter.broadcast_to([E * R, B])), (scal[:, :], scaling),
                             (wqkv_sb[:, :, :], wqkv.rearrange("(c p) n -> p c n", p=128)),
                             (at_sb[:, :, :], at.rearrange("(c p) n -> p c n", p=128)),
                             (wt_sb[:, :, :], wt.rearrange("(c p) n -> p c n", p=128)),
                             (bt_sb[:, :, :], bt.rearrange("(c p) n -> p c n", p=128)),
                             (wp_sb[:, :, :], wp.rearrange("(c p) n -> p c n", p=128)),
                             (wo_sb[:, :, :], wo.rearrange("(c p) n -> p c n", p=128)),
                             (wbase_sb[:, :, :], wbase.rearrange("(c p) n -> p c n", p=128))):
                act.dma_start(dst, src).then_inc(s_w, 16)
            act.wait_ge(s_con, 16)
            act.copy(identb[:, :], ident).then_inc(s_prec, 1)
            act.wait_ge(s_ix, 13 + SPAN)
            act.dma_start(blocks_d, blk).then_inc(s_blkd, 16)
            act.wait_ge(s_idx, 3)
            for i in range(2):
                act.activation(trig[:, i], redu[:, i], ACT.Sin).then_inc(s_trig, 1)
            for j in range(OWN):
                act.wait_ge(s_stage[j], 16)
                act.dma_start(merged_blocks[B * j:B * j + B, :], stage[:, j, :]).then_inc(s_init, 16)
            act.wait_ge(s_pre, 1)
            act.copy(aw[:, :, :], ps_pre[:, 0:128].rearrange("p (c n) -> p c n", c=2)).then_inc(s_prec, 1)
            act.copy(bw[:, :], ps_pre[0:E * R, 128:384]).then_inc(s_prec, 1)

            def phase1(h, u):
                t, k, p = at_step(h, u, 1)
                if valid(t):
                    act.wait_ge(xT_done, t + 1)
                    if reused(t):
                        act.wait_ge(qkv_done, t - 1)
                    act.copy(x1T[:, p], ps_xT[p][:, 0:256].rearrange("p (c n) -> p c n", c=2)
                             ).then_inc(xT_copied, 1)
                t, k, p = at_step(h, u, 2)
                if valid(t):
                    act.wait_ge(qkv_done, t + 1)
                    if reused(t):
                        act.wait_ge(prods_done, 6 * (t - 1))
                    act.copy(kqs[:, p, :], ps_qkv[p][:, 0:384]).then_inc(kq_copied, 1)
                    if reused(t):
                        act.wait_ge(ss_done, t - 1)
                    act.activation(sq[:, p, :], ps_qkv[p][:, 0:384], ACT.Square).then_inc(sq_done, 1)
                    if reused(t):
                        act.wait_ge(s_scat[p], 16 * k)
                    act.copy(kvrow[:, p, 128:256], ps_qkv[p][:, 384:512]).then_inc(v_copied, 1)
                t, k, p = at_step(h, u, 3)
                if valid(t):
                    act.wait_ge(ss_done, t + 1)
                    if reused(t):
                        act.wait_ge(rinv_done, t - 1)
                    act.activation(rt[:, p, :], ss[:, p, :], ACT.Sqrt).then_inc(rt_done, 1)
                t, k, p = at_step(h, u, 4)
                if valid(t):
                    act.wait_ge(qrT_done, t + 1)
                    act.copy(qT[:, bass.ds(t, 1), :].rearrange("p o n -> p (o n)"), qrT[:, p, :]).then_inc(qT_done, 1)

            steps(act, phase1, *P1)
            act.wait_ge(s_pad, 2)
            act.wait_ge(s_init, 16 * OWN)
            act.wait_ge(qT_done, NT)

            def phase2(h, u):
                t, k, p = at_step(h, u, 0)
                t2, k2, p2 = at_step(h, u, 2)
                if valid(t2):
                    act.wait_ge(onT_done, t2 + 1)
                    act.copy(onT[:, :, :], ps_t[:, 0:256].rearrange("p (c n) -> p c n", c=2)
                             ).then_inc(onT_copied, 1)
                if valid(t):
                    if reused(t):
                        act.wait_ge(sc_done, 3 * (t - 1))
                    for b in range(NB):
                        only = con[:, COL["batch"][0] + b:COL["batch"][0] + b + 1]
                        act.activation(qbd[:, p, :, 32 * b:32 * b + 32],
                                       qT[:, bass.ds(t, 1), :].rearrange("p o (h c) -> p (o h) c", h=H),
                                       ACT.Copy, scale=only).then_inc(qbd_done, 1)
                for i in range(3):
                    if i == 1 and valid(t2):
                        act.wait_ge(x2T_done, t2 + 1)
                        act.copy(x2T[:, :, :], ps_t[:, 256:512].rearrange("p (c n) -> p c n", c=2)
                                 ).then_inc(x2T_copied, 1)
                    if valid(t):
                        if i == 0 and reused(t):
                            act.wait_ge(pT_done, 3 * (t - 1))
                        act.wait_ge(nmx_done, 3 * t + i + 1)
                        for j, hd in enumerate(HEADS[i]):
                            act.activation(prob[:, p, hd, 0:NK], ps_sc[i][:, j * NK:j * NK + NK], ACT.Exp,
                                           bias=nmx[:, p, hd:hd + 1], scale=SCALE,
                                           accum_out=den[:, p, hd:hd + 1]).then_inc(exp_done, 1)

            steps(act, phase2, *P2)

        @block.vector
        def _(ve):
            count = [0]

            def link(ins):
                count[0] += 1
                ins.then_inc(s_ix, 1)
                ve.wait_ge(s_ix, count[0])

            ve.wait_ge(s_small, 32)
            ve.wait_ge(s_con, 16)
            link(ve.tensor_copy(kvf, kv_i))
            link(ve.tensor_copy(tabf, tab_i))
            link(ve.tensor_scalar(slot0, kvf, 1.0 / BLOCK, -7.5 / BLOCK, ALU.mult, ALU.add))
            link(ve.tensor_scalar(slot0, slot0, MAGIC, None, ALU.add))
            link(ve.tensor_scalar(slot0, slot0, -MAGIC, None, ALU.add))
            link(ve.scalar_tensor_tensor(out=off0, in0=slot0, scalar=-float(BLOCK), in1=kvf,
                                         op0=ALU.mult, op1=ALU.add))
            link(ve.tensor_scalar(target, cc("span", B), slot0, None, ALU.add))
            for i in range(SPAN):
                link(ve.scalar_tensor_tensor(out=pick, in0=cc("slot", B), scalar=target[:, i:i + 1], in1=tabf,
                                             op0=ALU.is_equal, op1=ALU.mult, accum_out=blk[:, i:i + 1]))
            link(ve.tensor_scalar(bits[:, 0:1], off0, 8.0, None, ALU.is_ge))
            link(ve.scalar_tensor_tensor(out=rest[:, 0:1], in0=bits[:, 0:1], scalar=-8.0, in1=off0,
                                         op0=ALU.mult, op1=ALU.add))
            link(ve.tensor_scalar(bits[:, 1:2], rest[:, 0:1], 4.0, None, ALU.is_ge))
            link(ve.scalar_tensor_tensor(out=rest[:, 1:2], in0=bits[:, 1:2], scalar=-4.0, in1=rest[:, 0:1],
                                         op0=ALU.mult, op1=ALU.add))
            link(ve.tensor_scalar(bits[:, 2:3], rest[:, 1:2], 2.0, None, ALU.is_ge))
            link(ve.scalar_tensor_tensor(out=bits[:, 3:4], in0=bits[:, 2:3], scalar=-2.0, in1=rest[:, 1:2],
                                         op0=ALU.mult, op1=ALU.add))
            assert count[0] == 13 + SPAN
            ve.tensor_copy(blk_i[:, :], blk).then_inc(s_idx, 1)

            link(ve.tensor_scalar(posf[:, 2, :], cc("tok", B), kvf, None, ALU.add))
            link(ve.tensor_scalar(posf[:, 1, :], cc("tok", B), rest[:, 1:2], None, ALU.add))
            link(ve.tensor_tensor(lim, rest[:, 1:2], kvf, ALU.subtract))
            link(ve.tensor_scalar(lim, lim, float(WINDOW), None, ALU.add))
            link(ve.tensor_scalar(posf[:, 0, :], posf[:, 1, :], 1.0, lim, ALU.add, ALU.max))

            link(ve.tensor_scalar(cidx, blk, 4.0, None, ALU.mult))
            link(ve.tensor_tensor(rows4[:, 0, :].rearrange("p (i f) -> p i f", f=4),
                                  cidx[:, 0:9].unsqueeze(2).broadcast_to([B, 9, 4]),
                                  cc("m4", B).rearrange("p (i f) -> p i f", f=4), ALU.add))

            link(ve.tensor_scalar(cover[:, 0, :], cc("m16", B)[:, 0:17], off0, None, ALU.is_ge))
            link(ve.tensor_scalar(cover[:, 2, :], cc("m16", B)[:, 0:17], off0, None, ALU.is_lt))
            link(ve.memset(cover[:, 1, :], 1.0))
            link(ve.memset(cover[:, :, 16:17], 1.0))
            ve.wait_ge(s_blkr, 16)
            for j in range(OWN):
                link(ve.tensor_scalar(eq[j], allblk, blk[:, BACK + j:BACK + j + 1], None, ALU.is_equal))
            for j in range(OWN):
                a = COL["later"][0] + j * B * OWN
                link(ve.tensor_tensor(el[j].rearrange("p (b i) -> p b i", i=OWN),
                                      eq[j].rearrange("p (b i) -> p b i", i=SPAN)[:, :, BACK:SPAN],
                                      con[0:B, a:a + B * OWN].rearrange("p (b i) -> p b i", i=OWN), ALU.mult))
            ve.wait_ge(s_ipe, 1)
            link(ve.tensor_copy(dead, ps_idx[0:B, 0:51].rearrange("p (j n) -> p j n", j=OWN)))
            link(ve.tensor_scalar(canon_seg, dead[:, :, 16], 0.0, None, ALU.is_equal))
            link(ve.tensor_tensor(canon_seg, canon_seg, cc("seg1", B), ALU.mult))
            seg_ready = count[0]
            ve.wait_ge(s_ipe, 2)
            link(ve.tensor_copy(canon, ps_idx[0:B, 64:64 + SPAN]))
            link(ve.tensor_scalar(cmiss, canon, 0.0, BIG, ALU.is_equal, ALU.mult))
            link(ve.tensor_scalar(cidx, canon, 4.0, -4.0, ALU.mult, ALU.add))
            link(ve.tensor_tensor(cidx, cidx, cmiss, ALU.add))
            link(ve.tensor_tensor(rows4[:, 1, :].rearrange("p (i f) -> p i f", f=4),
                                  cidx[:, 0:9].unsqueeze(2).broadcast_to([B, 9, 4]),
                                  cc("m4", B).rearrange("p (i f) -> p i f", f=4), ALU.add))
            link(ve.tensor_scalar(cidx, canon, 8.0, -8.0, ALU.mult, ALU.add))
            link(ve.tensor_tensor(rows2.rearrange("p (i f) -> p i f", f=8),
                                  cidx[:, BACK:SPAN].unsqueeze(2).broadcast_to([B, OWN, 8]),
                                  cc("m8", B).rearrange("p (i f) -> p i f", f=8), ALU.add))
            link(ve.tensor_scalar(cidx, canon, 16.0, -16.0, ALU.mult, ALU.add))
            link(ve.tensor_tensor(rows1.rearrange("p (i f) -> p i f", f=16),
                                  cidx[:, BACK:SPAN].unsqueeze(2).broadcast_to([B, OWN, 16]),
                                  cc("m16", B).rearrange("p (i f) -> p i f", f=16), ALU.add))
            link(ve.tensor_scalar(dead, dead, 1.0, BIG, ALU.is_ge, ALU.mult))
            link(ve.tensor_tensor(rows1.rearrange("p (i f) -> p i f", f=16),
                                  rows1.rearrange("p (i f) -> p i f", f=16), dead[:, :, 0:16], ALU.add))
            link(ve.memset(idxf[:, :, :], BIG))

            def shift(dst, tmp, src, by, bit):
                n = dst.shape[-1]
                s0 = src[:, :, 0:n] if len(src.shape) == 3 else src[:, 0:n]
                s1 = src[:, :, by:by + n] if len(src.shape) == 3 else src[:, by:by + n]
                tm = tmp[:, :, 0:n] if len(src.shape) == 3 else tmp[:, 0:n]
                link(ve.tensor_tensor(tm, s1, s0, ALU.subtract))
                link(ve.scalar_tensor_tensor(out=dst, in0=tm, scalar=bits[:, bit:bit + 1], in1=s0,
                                             op0=ALU.mult, op1=ALU.add))

            shift(rows4b[:, :, 0:33], tmp4, rows4, 2, 0)
            shift(idxf[:, 0:2, :], tmp4, rows4b, 1, 1)
            shift(rows2b[:, 0:20], tmp2, rows2, 4, 0)
            shift(idxf[:, 2, 0:Q2], tmp2, rows2b, 2, 1)
            shift(rows1b[:, 0:39], tmp1, rows1, 8, 0)
            shift(rows1[:, 0:35], tmp1, rows1b, 4, 1)
            shift(rows1b[:, 0:33], tmp1, rows1, 2, 2)
            shift(idxf[:, 3, :], tmp1, rows1b, 1, 3)
            idx_ready = count[0]
            build.ready = (seg_ready, idx_ready)

            ve.wait_ge(s_ipe, 3)
            trI = ps_idx[:, 128:192].rearrange("p (t b) -> p b t", b=NB)
            trP = ps_idx[0:96, 192:256].rearrange("p (t b) -> p b t", b=NB)
            for b in range(NB):
                for kind in range(4):
                    link(ve.tensor_copy(idx[32 * b:32 * b + 32, kind, :], trI[32 * kind:32 * kind + 32, b, :]))
                for kind in range(3):
                    link(ve.tensor_copy(pos3[32 * b:32 * b + 32, kind, :], trP[32 * kind:32 * kind + 32, b, :]))
            ve.engine_nop().then_inc(s_idx, 1)

            link(ve.tensor_tensor(ang, pos3[:, 2, :].unsqueeze(2).broadcast_to([128, NT, half]),
                                  cc("inv").unsqueeze(1).broadcast_to([128, NT, half]), ALU.mult))
            c1 = float(np.float32(6.28125))
            c2 = float(np.float32(np.round((2 * np.pi - c1) * 2.0 ** 21) / 2.0 ** 21))
            c3 = float(np.float32(2 * np.pi - c1 - c2))
            for i in range(2):
                link(ve.tensor_scalar(turn, ang, 1.0 / (2 * PI), 0.25 * i, ALU.mult, ALU.add))
                link(ve.tensor_scalar(turn, turn, MAGIC, None, ALU.add))
                link(ve.tensor_scalar(turn, turn, -MAGIC, None, ALU.add))
                link(ve.scalar_tensor_tensor(out=redu[:, i], in0=turn, scalar=-c1, in1=ang, op0=ALU.mult, op1=ALU.add))
                link(ve.scalar_tensor_tensor(out=redu[:, i], in0=turn, scalar=-c2, in1=redu[:, i],
                                             op0=ALU.mult, op1=ALU.add))
                link(ve.scalar_tensor_tensor(out=redu[:, i], in0=turn, scalar=-c3, in1=redu[:, i],
                                             op0=ALU.mult, op1=ALU.add))
                link(ve.tensor_scalar(redu[:, i], redu[:, i], i * PI / 2, PI, ALU.add, ALU.min))
                link(ve.tensor_scalar(redu[:, i], redu[:, i], -PI, None, ALU.max))
            ve.engine_nop().then_inc(s_idx, 1)
            ve.wait_ge(s_w, 16 * 13)
            link(ve.tensor_copy(adp_f[:, :], adp_i[:, :]))
            link(ve.tensor_scalar(zscale[:, :], adp_f[:, :], cc("adapter", E * R), scal[:, 0:1],
                                  ALU.is_equal, ALU.mult))
            ve.wait_ge(s_trig, 2)
            ve.engine_nop().then_inc(s_idx, 1)

            def phase1(h, u):
                t, k, p = at_step(h, u, 0)
                if valid(t):
                    ve.wait_ge(l0_done, t + 1)
                    if reused(t):
                        ve.wait_ge(xT_done, t - 1)
                        ve.wait_ge(x1_saved, t - 1)
                    ve.tensor_tensor(x1s[:, p, :], xall[:, bass.ds(t, 1), :].rearrange("p o n -> p (o n)"),
                                     ps_l0[p][:, 0:D], ALU.add).then_inc(x1_done, 1)
                t, k, p = at_step(h, u, 2)
                if valid(t):
                    ve.wait_ge(sq_done, t + 1)
                    if reused(t):
                        ve.wait_ge(rt_done, t - 1)
                    ve.tensor_reduce(ss[:, p, :], sq[:, p, :].rearrange("p (n d) -> p n d", d=HD), AX_X,
                                     ALU.add).then_inc(kT_part, 1)
                    ve.wait_ge(kT_part, t + 1)
                    ve.tensor_scalar(ss[:, p, :], ss[:, p, :], 1.0 / HD, EPS, ALU.mult, ALU.add).then_inc(ss_done, 1)
                t, k, p = at_step(h, u, 3)
                if valid(t):
                    ve.wait_ge(rt_done, t + 1)
                    ve.reciprocal(rinv[:, p, :], rt[:, p, :]).then_inc(rinv_done, 1)
                    ve.wait_ge(prods_done, 6 * (t + 1))
                    ve.tensor_tensor(rsum[:, p, :], ropeA[:, p, :], ropeB[:, p, :], ALU.add).then_inc(rsum_done, 1)
                    ve.wait_ge(rinv_done, t + 1)
                    ve.wait_ge(rsum_done, t + 1)
                    if reused(t):
                        ve.wait_ge(s_scat[p], 16 * k)
                    ve.tensor_tensor(kvrow[:, p, 0:128].rearrange("p (n d) -> p n d", d=HD),
                                     rsum[:, p, 0:128].rearrange("p (n d) -> p n d", d=HD),
                                     rinv[:, p, 0:G].unsqueeze(2).broadcast_to([128, G, HD]),
                                     ALU.mult).then_inc(krow_done, 1)
                    ve.tensor_tensor(qrot[:, p, :].rearrange("p (n d) -> p n d", d=HD),
                                     rsum[:, p, 128:384].rearrange("p (n d) -> p n d", d=HD),
                                     rinv[:, p, G:12].unsqueeze(2).broadcast_to([128, H, HD]),
                                     ALU.mult).then_inc(qrot_done, 1)
                    ve.wait_ge(qrot_done, t + 1)
                    if reused(t):
                        ve.wait_ge(qT_done, t - 1)
                    ve.transpose(qrT[:, p, :], qrot[:, p, :]).then_inc(qrT_done, 1)

            steps(ve, phase1, *P1)

            def keys(t, k, p):
                ve.wait_ge(s_merge[p], 16 * (k + 1))
                ve.wait_ge(s_own[p], 16 * (k + 1))
                if reused(t):
                    ve.wait_ge(sc_done, 3 * (t - 1))
                old = kvb[:, p, :].rearrange("p (f k g d) -> p f k g d", f=4, k=2, g=G)
                new = own[:, p, :].rearrange("p (f k g d) -> p f k g d", f=2, k=2, g=G)
                ve.transpose(kT[:, p, :, 0:NKB].rearrange("p g (f r) -> p f g r", f=4), old[:, :, 0])
                ve.transpose(kT[:, p, :, NKB:NKB + 32], new[:, 0, 0]).then_inc(kT_part, 1)
                ve.wait_ge(kT_part, NT + t + 1)
                ve.transpose(kT[:, p, :, NKB + Q2:NKB + Q2 + 32], new[:, 1, 0]).then_inc(kT_done, 1)

            keys(0, 0, 0)
            ve.wait_ge(s_pad, 2)

            def maxima(t, p, i):
                a, n = HEADS[i][0], len(HEADS[i])
                ve.wait_ge(sc_done, 3 * t + i + 1)
                ve.tensor_reduce(mx[:, p, a:a + n], ps_sc[i][:, 0:n * NK].rearrange("p (n k) -> p n k", n=n),
                                 AX_X, ALU.max).then_inc(mx_done, 1)
                ve.wait_ge(mx_done, 3 * t + i + 1)
                ve.tensor_scalar(nmx[:, p, a:a + n], mx[:, p, a:a + n], -SCALE, None, ALU.mult).then_inc(nmx_done, 1)

            def phase2(h, u):
                t, k, p = at_step(h, u, 0)
                t2, k2, p2 = at_step(h, u, 2)
                t3, k3, p3 = at_step(h, u, 3)
                if valid(t2):
                    ve.wait_ge(pv_done, t2 + 1)
                    ve.transpose(oraw[:, :], ps_o[:, 0:256]).then_inc(oraw_done, 1)
                    ve.reciprocal(rden[:, p2, :], den[:, p2, :]).then_inc(rden_done, 1)
                    ve.wait_ge(oraw_done, t2 + 1)
                    ve.wait_ge(rden_done, t2 + 1)
                    ve.tensor_tensor(onrm[:, :].rearrange("p (n d) -> p n d", d=HD),
                                     oraw[:, :].rearrange("p (n d) -> p n d", d=HD),
                                     rden[:, p2, :].unsqueeze(2).broadcast_to([128, H, HD]),
                                     ALU.mult).then_inc(onrm_done, 1)
                if valid(t):
                    maxima(t, p, 0)
                if valid(t2):
                    ve.wait_ge(wo_done, t2 + 1)
                    ve.tensor_tensor(x2s[:, p2, :], xall[:, bass.ds(t2, 1), :].rearrange("p o n -> p (o n)"),
                                     ps_wo, ALU.add).then_inc(x2_done, 1)
                if valid(t):
                    maxima(t, p, 1)
                if valid(t3):
                    ve.wait_ge(l3_done, t3 + 1)
                    if reused(t3):
                        ve.wait_ge(s_out[p3], 16 * k3)
                    ve.tensor_tensor(x4s[:, p3, :], x3s[:, p3, :], ps_l3, ALU.add).then_inc(x4_done, 1)
                if valid(t):
                    maxima(t, p, 2)
                if valid(t2):
                    ve.wait_ge(z_done, t2 + 1)
                    ve.tensor_tensor(zm[:, :].rearrange("p (b c) -> p b c", b=NB),
                                     ps_z.rearrange("p (b c) -> p b c", b=NB),
                                     zscale[:, bass.ds(t2 * NB, NB)].unsqueeze(2).broadcast_to([E * R, NB, TOK]),
                                     ALU.mult).then_inc(zm_done, 1)
                t1, k1, p1 = at_step(h, u, -1)
                if valid(t1):
                    keys(t1, k1, p1)
                if valid(t):
                    if reused(t):
                        ve.wait_ge(pv_done, t - 1)
                    ve.wait_ge(exp_done, H * (t + 1))
                    for f0, f1, a in ((0, 4, 0), (4, 5, NKB), (5, 6, NKB + Q2)):
                        ve.transpose(pT[:, p, f0:f1, :].rearrange("p f (h c) -> p h f c", h=H),
                                     prob[:, p, :, a:a + 32 * (f1 - f0)].rearrange("p h (f c) -> p h f c", c=32)
                                     ).then_inc(pT_done, 1)
                if valid(t2):
                    ve.wait_ge(l2_done, t2 + 1)
                    ve.tensor_tensor(x3s[:, p2, :], x2s[:, p2, :], ps_l2, ALU.add).then_inc(x3_done, 1)

            steps(ve, phase2, *P2)

        @block.tensor
        def _(pe):
            seg_ready, idx_ready = build.ready
            pe.wait_ge(s_ix, seg_ready - 3)
            for i in range(OWN):
                for j in range(OWN):
                    mm = pe.matmul(ps_idx[0:B, 17 * i:17 * i + 17],
                                   el[j].rearrange("p (b i) -> p i b", i=OWN)[:, i], cover[:, j, :],
                                   start=(j == 0), stop=(j == OWN - 1))
            mm.then_inc(s_ipe, 1)
            pe.wait_ge(s_ix, seg_ready)
            for i in range(SPAN):
                for j in range(OWN):
                    mm = pe.matmul(ps_idx[0:B, 64 + i:65 + i], eq[j].rearrange("p (b i) -> p i b", i=SPAN)[:, i],
                                   canon_seg[:, j:j + 1], start=(j == 0), stop=(j == OWN - 1))
            mm.then_inc(s_ipe, 1)
            pe.wait_ge(s_w, 16 * 13)
            for m in range(2):
                for c in range(2):
                    pe.matmul(ps_pre[:, 64 * m:64 * m + 64], wt_sb[:, c, 128 * m:128 * m + 128], at_sb[:, c, :],
                              start=(c == 0), stop=(c == 1))
            for c in range(2):
                mm = pe.matmul(ps_pre[0:E * R, 128:384], bt_sb[:, c, :], wp_sb[:, c, :], start=(c == 0), stop=(c == 1))
            mm.then_inc(s_pre, 1)
            pe.wait_ge(s_ix, idx_ready)
            pe.transpose(ps_idx[:, 128:192], idxf.rearrange("p k r -> p (k r)"), con[0:B, 0:B])
            pe.transpose(ps_idx[0:96, 192:256], posf.rearrange("p k r -> p (k r)"), con[0:B, 0:B]).then_inc(s_ipe, 1)

            def phase1(h, u):
                t, k, p = at_step(h, u, 0)
                if valid(t):
                    if isinstance(t, int):
                        pe.wait_ge(s_x[t // 4], 16)
                    elif u == 0:
                        pass
                    pe.wait_ge(s_w0[p], 64 * (k + 1))
                    if reused(t):
                        pe.wait_ge(x1_done, t - 1)
                    pe.matmul(ps_l0[p][:, 0:D], w0bd[:, p, :],
                              xall[:, bass.ds(t, 1), :].rearrange("p o n -> p (o n)"),
                              start=True, stop=True).then_inc(l0_done, 1)
                t, k, p = at_step(h, u, 1)
                if valid(t):
                    pe.wait_ge(x1_done, t + 1)
                    if reused(t):
                        pe.wait_ge(xT_copied, t - 1)
                    for c in range(2):
                        mm = pe.transpose(ps_xT[p][:, 128 * c:128 * c + 128], x1s[:, p, 128 * c:128 * c + 128], ident)
                    mm.then_inc(xT_done, 1)
                t, k, p = at_step(h, u, 2)
                if valid(t):
                    pe.wait_ge(xT_copied, t + 1)
                    if reused(t):
                        pe.wait_ge(kq_copied, t - 1)
                        pe.wait_ge(sq_done, t - 1)
                        pe.wait_ge(v_copied, t - 1)
                    for c in range(2):
                        mm = pe.matmul(ps_qkv[p][:, :], x1T[:, p, c, :], wqkv_sb[:, c, :], start=(c == 0), stop=(c == 1))
                    mm.then_inc(qkv_done, 1)

            for i in range(4):
                pe.wait_ge(s_x[i], 16)
            steps(pe, phase1, *P1)

            pe.wait_ge(kq_copied, NT)
            pe.wait_ge(sq_done, NT)
            pe.wait_ge(v_copied, NT)
            pe.wait_ge(s_idx, 4)
            pe.wait_ge(s_prec, 3)

            def scores(t, p, i):
                if i == 0:
                    pe.wait_ge(kT_done, t + 1)
                    pe.wait_ge(qbd_done, NB * (t + 1))
                    pe.wait_ge(mask_done, 2 * (t + 1))
                if not isinstance(t, int) or t >= 1:
                    pe.wait_ge(exp_done, H * t - H + HEADS[i][-1] + 1)
                n = len(HEADS[i])
                pe.matmul(ps_sc[i][:, 0:n * NK], identb[:, :],
                          mask[:, p, :].unsqueeze(1).broadcast_to([128, n, NK]), start=True, stop=False,
                          skip_group_check=True)
                for j, hd in enumerate(HEADS[i]):
                    mm = pe.matmul(ps_sc[i][:, j * NK:j * NK + NK], qbd[:, p, hd, :], kT[:, p, hd // GSZ, 0:NK],
                                   start=False, stop=(j == n - 1), skip_group_check=True)
                mm.then_inc(sc_done, 1)

            def weighted(t, p, groups):
                if groups[0] == 0:
                    pe.wait_ge(pT_done, 3 * (t + 1))
                    pe.wait_ge(vbd_done, 8 * (t + 1))
                    if not isinstance(t, int) or t >= 1:
                        pe.wait_ge(oraw_done, t)
                for g in groups:
                    for f in range(6):
                        mm = pe.matmul(ps_o[:, 64 * g:64 * g + 64], vbd[:, p, f, g, :], pT[:, p, f, 64 * g:64 * g + 64],
                                       start=(f == 0), stop=(f == 5))
                if groups[-1] == G - 1:
                    mm.then_inc(pv_done, 1)

            def phase2(h, u):
                t, k, p = at_step(h, u, 0)
                t1, k1, p1 = at_step(h, u, 1)
                t2, k2, p2 = at_step(h, u, 2)
                t3, k3, p3 = at_step(h, u, 3)
                if valid(t2):
                    pe.wait_ge(onrm_done, t2 + 1)
                    for c in range(2):
                        mm = pe.transpose(ps_t[:, 128 * c:128 * c + 128], onrm[:, 128 * c:128 * c + 128], ident)
                    mm.then_inc(onT_done, 1)
                if valid(t):
                    scores(t, p, 0)
                if valid(t2):
                    pe.wait_ge(onT_copied, t2 + 1)
                    for c in range(2):
                        mm = pe.matmul(ps_wo, onT[:, c, :], wo_sb[:, c, :], start=(c == 0), stop=(c == 1))
                    mm.then_inc(wo_done, 1)
                if valid(t3):
                    pe.wait_ge(x3_done, t3 + 1)
                    pe.wait_ge(s_w3[p3], 64 * (k3 + 1))
                    pe.matmul(ps_l3, w3bd[:, p3, :], x3s[:, p3, :], start=True, stop=True).then_inc(l3_done, 1)
                if valid(t):
                    scores(t, p, 1)
                if valid(t2):
                    pe.wait_ge(x2_done, t2 + 1)
                    for c in range(2):
                        mm = pe.transpose(ps_t[:, 256 + 128 * c:384 + 128 * c], x2s[:, p2, 128 * c:128 * c + 128], ident)
                    mm.then_inc(x2T_done, 1)
                if valid(t):
                    scores(t, p, 2)
                if valid(t2):
                    pe.wait_ge(x2T_copied, t2 + 1)
                    if not isinstance(t2, int) or t2 >= 1:
                        pe.wait_ge(x4_done, t2)
                    for c in range(2):
                        mm = pe.matmul(ps_z, aw[:, c, :], x2T[:, c, :], start=(c == 0), stop=(c == 1))
                    mm.then_inc(z_done, 1)
                    for c in range(2):
                        pe.matmul(ps_l2, x2T[:, c, :], wbase_sb[:, c, :], start=(c == 0), stop=False)
                if valid(t1):
                    weighted(t1, p1, [0, 1])
                if valid(t2):
                    pe.wait_ge(zm_done, t2 + 1)
                    pe.matmul(ps_l2, zm[:, :], bw[:, :], start=False, stop=True).then_inc(l2_done, 1)
                if valid(t1):
                    weighted(t1, p1, [2, 3])

            steps(pe, phase2, *P2)


def kernel(**inputs):
    import concourse.bacc as _bacc
    from concourse.bass_utils import run_bass_kernel_spmd as _run

    a = {k: np.asarray(v) for k, v in inputs.items()}
    kb, vb = a["L1_cond_k_blocks"], a["L1_cond_v_blocks"]
    pool = np.stack([kb.transpose(0, 2, 1, 3), vb.transpose(0, 2, 1, 3)], axis=2).reshape(NPOOL * BLOCK, ROW)
    arrays = {
        "x": a["x"].reshape(B * TOK, D),
        "cond": a["itok_B_1_198"].reshape(1, B),
        "table": a["itok_Bx257_0_4111"],
        "kv_lens": a["itok_B_37_3939"].reshape(B, 1),
        "adapter": a["itok_B_0_3"].reshape(1, B),
        "subject": a["itok_B_0_7"].reshape(1, B),
        "w0": a["L0_cond_weights"],
        "wqkv": np.concatenate([a["L1_cond_Wk"], a["L1_cond_Wq"], a["L1_cond_Wv"]], axis=0).T,
        "wo": a["L1_cond_Wo"].T,
        "qscale": a["L1_cond_q_norm_scale"].reshape(1, HD),
        "kscale": a["L1_cond_k_norm_scale"].reshape(1, HD),
        "pool": pool,
        "wbase": a["L2_cond_W_base"].T,
        "wt": a["L2_cond_Wt"],
        "at": a["L2_cond_A"].reshape(E * R, D).T,
        "bt": a["L2_cond_B_w"].transpose(1, 0, 2).reshape(D, E * R),
        "wp": a["L2_cond_Wp"].T,
        "scaling": np.repeat(a["L2_cond_scaling"], R).reshape(E * R, 1),
        "w3": a["L3_cond_weights"],
        "consts": constants(),
    }
    nc = _bacc.Bacc("TRN2", target_bir_lowering=False, num_devices=1)
    arrays = {f"in_{k}": np.ascontiguousarray(v) for k, v in arrays.items()}
    args = [nc.dram_tensor(k, v.shape, mybir.dt.from_np(v.dtype), kind="ExternalInput").ap()
            for k, v in arrays.items()]
    out = nc.dram_tensor("out", (B * TOK, D), F32, kind="ExternalOutput").ap()
    build(nc, *args, out)
    r = _run(nc, [arrays], core_ids=[0])
    return r.results[0]["out"].reshape(B, TOK, D)
```

```python
from contextlib import ExitStack

import numpy as np
import concourse.bass as bass
from concourse import mybir

ALU = mybir.AluOpType
ACT = mybir.ActivationFunctionType
AX_X = mybir.AxisListType.X
AX_XY = mybir.AxisListType.XY
F32 = mybir.dt.float32
BF16 = mybir.dt.bfloat16
I32 = mybir.dt.int32

B, TOK, D = 64, 32, 256
H, G, HD = 8, 4, 32
GSZ = H // G
BLOCK, NBLK, NPOOL = 16, 257, 4112
WINDOW = 128
SCALE = 256.0 ** -0.5
EPS = 1e-6
THETA = 10000.0
E, R = 4, 16
NB = 128 // TOK
NT = B // NB
ROW = 2 * G * HD
BACK = WINDOW // BLOCK
OWN = 3
SPAN = BACK + OWN
SEGS = OWN * B
R4 = WINDOW // 4
Q2 = 18
NKB = 4 * R4
NK = NKB + 2 * Q2
KW = 180
RING = 4
BIG = float(2 ** 20)
NEG = -1e30
PI = float(np.pi)
MAGIC = 1.5 * 2.0 ** 23

_COLS = [("ident", 128), ("slot", NBLK), ("span", SPAN), ("m4", 36), ("m8", 24), ("m16", 48),
         ("later", OWN * B * OWN), ("seg1", OWN), ("tok", TOK), ("inv", HD // 2),
         ("backpos", NKB), ("ownpos", 2 * Q2), ("adapter", 1), ("batch", NB)]
COL = {}
_at = 0
for _n, _w in _COLS:
    COL[_n] = (_at, _at + _w)
    _at += _w
NCONST = _at


def constants():
    c = np.zeros((128, NCONST), np.float32)

    def put(name, value):
        a, b = COL[name]
        c[:, a:b] = np.broadcast_to(value, (128, b - a))

    put("ident", np.eye(128, dtype=np.float32))
    put("slot", np.arange(NBLK))
    put("span", np.arange(SPAN) - BACK)
    put("m4", np.arange(36) % 4)
    put("m8", np.arange(24) % 8)
    put("m16", np.arange(48) % 16)
    late = np.zeros((128, OWN, B, OWN), np.float32)
    for j in range(OWN):
        late[:, j] = (OWN * np.arange(128) + j)[:, None, None] > (OWN * np.arange(B)[:, None] + np.arange(OWN))
    put("later", late.reshape(128, -1))
    put("seg1", np.arange(128)[:, None] + B * np.arange(OWN) + 1)
    put("tok", np.arange(TOK))
    half = HD // 2
    put("inv", np.float32(1.0) / np.float32(THETA) ** (np.arange(half, dtype=np.float32) / np.float32(half)))
    put("backpos", (4 * np.arange(R4)[None, :] + np.arange(4)[:, None]).reshape(-1))
    put("ownpos", (2 * np.arange(Q2)[None, :] + np.arange(2)[:, None]).reshape(-1))
    put("adapter", (np.arange(128) // R)[:, None])
    put("batch", (np.arange(128) // TOK)[:, None] == np.arange(NB))
    return c


def at_step(h, u, lag):
    return 2 * h + (u - lag), h + (u - lag) // 2, (u - lag) % 2


def at_step4(h, u, lag):
    return 4 * h + (u - lag), 2 * h + (u - lag) // 2, (u - lag) % 2, (u - lag) % 4, h + (u - lag) // 4


def valid(t):
    return not isinstance(t, int) or 0 <= t < NT


def reused(t):
    return not isinstance(t, int) or t >= 2


def steps(eng, body, total, first, last, group=2):
    for i in range(first):
        body(i // group, i % group)
    with eng.Fori(first // group, last // group) as h:
        for u in range(group):
            body(h, u)
    for i in range(last, total):
        body(i // group, i % group)


def build(nc, x, cond, table, kv_lens, adapter, subject, w0, wqkv, wo, qscale, kscale, pool,
          wbase, wt, at, bt, wp, scaling, w3, consts, out):
    half = HD // 2
    table_i = table
    merged = nc.dram_tensor("merged", [SEGS * BLOCK, ROW], F32).ap()
    blocks_d = nc.dram_tensor("blocks_scratch", [B, SPAN], F32).ap()
    pool_rows4 = pool.rearrange("(r f) n -> r (f n)", f=4)
    pool_blocks = pool.rearrange("(r f) n -> r (f n)", f=BLOCK)
    merged_rows4 = merged.rearrange("(r f) n -> r (f n)", f=4)
    merged_rows2 = merged.rearrange("(r f) n -> r (f n)", f=2)
    merged_blocks = merged.rearrange("(r f) n -> r (f n)", f=BLOCK)

    with ExitStack() as ctx:
        def sb(name, shape, dt=F32):
            return ctx.enter_context(nc.sbuf_tensor(name, shape, dt))

        def sem(name):
            return ctx.enter_context(nc.semaphore(name))

        con = sb("con", [128, NCONST])

        def cc(name, p=128):
            a, b = COL[name]
            return con[0:p, a:b]

        ident = cc("ident")
        identb = sb("identb", [128, 128], BF16)
        xall = sb("xall", [128, NT, D])
        qT = sb("qT", [128, NT, H * TOK])
        big = sb("big", [128, OWN * BLOCK * ROW])
        wqkv_sb = sb("wqkv_sb", [128, 2, 512])
        wo_sb = sb("wo_sb", [128, 2, D])
        wbase_sb = sb("wbase_sb", [128, 2, D])
        wt_sb = sb("wt_sb", [128, 2, D])
        at_sb = sb("at_sb", [128, 2, E * R])
        bt_sb = sb("bt_sb", [128, 2, E * R])
        wp_sb = sb("wp_sb", [128, 2, D])
        aw = sb("aw", [128, 2, E * R])
        bw = sb("bw", [E * R, D])
        w0bd = sb("w0bd", [128, 2, 128])
        w3bd = sb("w3bd", [128, 2, 128])
        qsc = sb("qsc", [128, HD])
        ksc = sb("ksc", [128, HD])
        cond_sb = sb("cond_sb", [1, B], I32)
        subj_sb = sb("subj_sb", [1, B], I32)
        adp_i = sb("adp_i", [E * R, B], I32)
        adp_f = sb("adp_f", [E * R, B])
        scal = sb("scal", [E * R, 1])
        zscale = sb("zscale", [E * R, B])
        idx = sb("idx", [128, 4, NT], I32)
        row_now = sb("row_now", [128, 4, RING], I32)
        pos_now = sb("pos_now", [128, 2, 2])
        pos3 = sb("pos3", [128, 3, NT])
        kt_rope = sb("kt_rope", [128, 3072])
        ropeC = kt_rope[:, 0:1536].rearrange("p (t a k d) -> p t a k d", t=NT, a=2, k=3)
        ropeS = kt_rope[:, 1536:3072].rearrange("p (t a k d) -> p t a k d", t=NT, a=2, k=3)
        kT = kt_rope[:, 0:2 * G * KW].rearrange("p (a g k) -> p a g k", a=2, g=G)
        mask = sb("mask", [128, 2, NK], BF16)
        work = sb("work", [128, 6480])

        used = [0]

        def carve(*shape):
            n = int(np.prod(shape))
            v = work[:, used[0]:used[0] + n]
            used[0] += n
            names = "abcd"[:len(shape)]
            if len(shape) == 1:
                return v
            return v.rearrange(f"p ({' '.join(names)}) -> p {' '.join(names)}",
                               **{k: s for k, s in zip(names, shape)})

        x1s = carve(2, D)
        x1T = carve(2, 2, 128)
        kqs = carve(2, 384)
        sq = carve(2, 384)
        ropeA = carve(2, 384)
        ropeB = carve(2, 384)
        rsum = carve(2, 384)
        kvrow = carve(2, ROW)
        qrot = carve(2, D)
        qrT = carve(2, D)
        ss = carve(2, 12)
        rt = carve(2, 12)
        rinv = carve(2, 12)
        used[0] = 0
        prob = carve(2, H, KW)
        pT = carve(2, 6, H * TOK)

        stage = big[0:B, :].rearrange("p (j n) -> p j n", j=OWN)
        vbd = big[:, 0:6144].rearrange("p (a f g c) -> p a f g c", a=2, f=6, g=G)
        qbd = big[:, 6144:8192].rearrange("p (a h c) -> p a h c", a=2, h=H)
        own = sb("own", [128, RING, 2 * ROW])
        kvb = big[:, 8192:12288].rearrange("p (a n) -> p a n", a=RING)

        mx = sb("mx", [128, 2, H])
        nmx = sb("nmx", [128, 2, H])
        den = sb("den", [128, 2, H])
        rden = sb("rden", [128, 2, H])
        oraw = sb("oraw", [128, D])
        onrm = sb("onrm", [128, D])
        onT = sb("onT", [128, 2, 128])
        x2s = sb("x2s", [128, 2, D])
        x2T = sb("x2T", [128, 2, 128])
        zm = sb("zm", [E * R, 128])
        x3s = sb("x3s", [128, 2, D])
        x4s = sb("x4s", [128, 2, D])

        blk_i = sb("blk_i", [B, SPAN], I32)
        more = sb("more", [B, 192 + 288])

        scratch = sb("scratch", [B, 4096])
        sused = [0]

        def scr(n, p=B):
            v = scratch[0:p, sused[0]:sused[0] + n]
            sused[0] += n
            return v

        kv_i = scr(1).bitcast(I32)
        tab_i = scr(NBLK).bitcast(I32)
        kvf = scr(1)
        tabf = scr(NBLK)
        off0 = scr(1)
        slot0 = scr(1)
        target = scr(SPAN)
        pick = x2s[0:B, :, :].rearrange('p k n -> p (k n)')[:, 0:NBLK]
        blk = scr(SPAN)
        bits = scr(4)
        rest = scr(4)
        allblk = scr(B * SPAN)
        eq = [scr(B * SPAN) for _ in range(OWN)]
        el = [v[0:B, 0:B * OWN] for v in (oraw, onrm, more)]
        cover = more[:, 416:467].rearrange("p (j n) -> p j n", j=OWN)
        dead = scr(OWN * 17).rearrange("p (j n) -> p j n", j=OWN)
        canon_seg = scr(OWN)
        canon = scr(SPAN)
        cmiss = scr(SPAN)
        cidx = scr(SPAN)
        rows4 = scr(72).rearrange("p (k m) -> p k m", k=2)
        rows4b = scr(66).rearrange("p (k m) -> p k m", k=2)
        tmp4 = scr(66).rearrange("p (k m) -> p k m", k=2)
        rows2 = scr(24)
        rows2b = scr(24)
        tmp2 = scr(24)
        rows1 = scr(48)
        rows1b = scr(48)
        tmp1 = scr(48)
        idxf = more[:, 192:320].rearrange("p (k r) -> p k r", k=4)
        posf = more[:, 320:416].rearrange("p (k r) -> p k r", k=3)
        lim = scr(1)
        ang = x4s[:, 0, :].rearrange("p (t d) -> p t d", t=NT)
        turn = x4s[:, 1, :].rearrange("p (t d) -> p t d", t=NT)
        redu = x2s[:, :, :].rearrange("p k (t d) -> p k t d", t=NT)
        trig = x3s[:, :, :].rearrange("p k (t d) -> p k t d", t=NT)

        bank = [ctx.enter_context(nc.psum_tensor(f"bank{i}", [128, 512], F32)) for i in range(8)]
        ps_l0 = [bank[0], bank[1]]
        ps_xT = [bank[2], bank[3]]
        ps_qkv = [bank[4], bank[5]]
        ps_idx = bank[6]
        ps_pre = bank[7]
        ps_sc = bank[0:3]
        ps_o = bank[3]
        ps_t = bank[4]
        ps_wo = bank[5][:, 0:D]
        ps_l3 = bank[7][:, 128:128 + D]
        ps_l2 = bank[6][:, 0:D]
        ps_z = bank[7][0:E * R, 0:128]
        HEADS = [range(0, 3), range(3, 6), range(6, 8)]

        s_small, s_con, s_w = sem("s_small"), sem("s_con"), sem("s_w")
        s_x = [sem(f"s_x{i}") for i in range(4)]
        s_w0 = [sem("s_w0a"), sem("s_w0b")]
        s_w3 = [sem("s_w3a"), sem("s_w3b")]
        s_zero = sem("s_zero")
        s_ix = sem("s_ix")
        s_blkd, s_blkr = sem("s_blkd"), sem("s_blkr")
        s_ipe = sem("s_ipe")
        s_idx = sem("s_idx")
        s_trig, s_rope = sem("s_trig"), sem("s_rope")
        s_pre, s_prec = sem("s_pre"), sem("s_prec")
        s_stage = [sem(f"s_stage{j}") for j in range(OWN)]
        s_init = sem("s_init")
        s_cache = [sem(f"s_cache{i}") for i in range(RING)]
        l0_done, x1_done, x1_saved = sem("l0_done"), sem("x1_done"), sem("x1_saved")
        xT_done, xT_copied, qkv_done = sem("xT_done"), sem("xT_copied"), sem("qkv_done")
        kq_copied, v_copied, sq_done = sem("kq_copied"), sem("v_copied"), sem("sq_done")
        ss_done, rt_done, rinv_done = sem("ss_done"), sem("rt_done"), sem("rinv_done")
        prods_done, rsum_done, krow_done = sem("prods_done"), sem("rsum_done"), sem("krow_done")
        qrot_done, qT_done = sem("qrot_done"), sem("qT_done")
        s_scat = [sem("s_scata"), sem("s_scatb")]
        s_merge = [sem(f"s_merge{i}") for i in range(RING)]
        s_own = [sem(f"s_own{i}") for i in range(RING)]
        kT_part, kT_done = sem("kT_part"), sem("kT_done")
        qbd_done, mask_done, vold_done, vnew_done = sem("qbd_done"), sem("mask_done"), sem("vold_done"), sem("vnew_done")
        sc_done, mx_done, nmx_done, exp_done = sem("sc_done"), sem("mx_done"), sem("nmx_done"), sem("exp_done")
        pT_done, pv_done, oraw_done, rden_done = sem("pT_done"), sem("pv_done"), sem("oraw_done"), sem("rden_done")
        onrm_done, onT_done, onT_copied = sem("onrm_done"), sem("onT_done"), sem("onT_copied")
        wo_done, x2_done, x2T_done, x2T_copied = sem("wo_done"), sem("x2_done"), sem("x2T_done"), sem("x2T_copied")
        z_done, zm_done, l2_done, x3_done = sem("z_done"), sem("zm_done"), sem("l2_done"), sem("x3_done")
        l3_done, x4_done = sem("l3_done"), sem("x4_done")
        s_out = [sem("s_outa"), sem("s_outb")]
        s_pad, s_big = sem("s_pad"), sem("s_big")
        row1_copied, row4_copied, rowm_copied, pos_copied = (
            sem("row1_copied"), sem("row4_copied"), sem("rowm_copied"), sem("pos_copied"))
        qrT_done, cross_done = sem("qrT_done"), sem("cross_done")
        desc_init, desc_scat, desc_cache, desc_fetch = sem("desc_init"), sem("desc_scat"), sem("desc_cache"), sem("desc_fetch")

        ZEROED = 2
        P1 = (20, 6, 16)
        P2 = (NT + 3, 6, 14)
        P2R = (NT + 3, 4, 12, RING)

        block = ctx.enter_context(nc.Block())

        @block.sync
        def _(sp):
            sp.dma_start(kv_i, kv_lens).then_inc(s_small, 16)
            sp.dma_start(tab_i, table_i).then_inc(s_small, 16)
            sp.dma_start(con[:, :], consts).then_inc(s_con, 16)
            sp.dma_start(cond_sb[:, :], cond).then_inc(s_w, 16)
            sp.dma_start(subj_sb[:, :], subject).then_inc(s_w, 16)
            xv = x.rearrange("(t p) n -> p t n", p=128)
            for i in range(4):
                sp.dma_start(xall[:, 4 * i:4 * i + 4, :], xv[:, 4 * i:4 * i + 4, :]).then_inc(s_x[i], 16)
            sp.wait_ge(s_blkd, 16)
            sp.dma_start(allblk, blocks_d.rearrange("b i -> (b i)").unsqueeze(0).broadcast_to([B, B * SPAN])
                         ).then_inc(s_blkr, 16)
            sp.wait_ge(s_w, 16 * 13)
            sp.wait_ge(s_zero, ZEROED)

            def diagonal(t, p, weights, numbers, buf, signal):
                for b in range(NB):
                    n = sp.value_load(numbers[0:1, bass.ds(t * NB + b, 1)], min_val=0, max_val=weights.shape[0] - 1)
                    sp.dma_start(buf[32 * b:32 * b + 32, p, 32 * b:32 * b + 32],
                                 weights[bass.ds(n, 1), :, :].rearrange("o c d -> (o c) d")).then_inc(signal[p], 16)

            def phase1(h, u):
                t, k, p = at_step(h, u, 0)
                if valid(t):
                    if reused(t):
                        sp.wait_ge(l0_done, t - 1)
                    diagonal(t, p, w0, cond_sb, w0bd, s_w0)

            steps(sp, phase1, NT, 2, NT)

            def phase2(h, u):
                t, k, p = at_step(h, u, 0)
                if valid(t):
                    if reused(t):
                        sp.wait_ge(l3_done, t - 1)
                    diagonal(t, p, w3, subj_sb, w3bd, s_w3)
                t, k, p = at_step(h, u, 1)
                if valid(t):
                    sp.wait_ge(x4_done, t + 1)
                    sp.dma_start(out[bass.ds(t * 128, 128), :], x4s[:, p, :]).then_inc(s_out[p], 16)

            steps(sp, phase2, NT + 1, 4, 14)
            for p in range(2):
                sp.wait_ge(s_out[p], 16 * (NT // 2))

        @block.gpsimd
        def _(pl):
            tick = pl.alloc_register("tick")
            pl.reg_mov(tick, 0)

            def wait(signal, n):
                if not isinstance(n, int):
                    pl.reg_mov(tick, n)
                    n = pl.snap(tick)
                    pl.wait_ge(s_idx, 4)
                pl.wait_ge(signal, n)

            pl.memset(w0bd[:, :, :], 0.0).then_inc(s_zero, 1)
            pl.memset(w3bd[:, :, :], 0.0).then_inc(s_zero, 1)
            pl.memset(own[:, :, :], 0.0).then_inc(s_big, 1)

            wait(s_idx, 1)
            for j in range(OWN):
                pl.indirect_dma_start(
                    out=stage[:, j, :], out_offset=None, in_=pool_blocks,
                    in_offset=bass.IndirectOffsetOnAxis(ap=blk_i[:, BACK + j:BACK + j + 1], axis=0),
                    bounds_check=NPOOL - 1, oob_is_err=False, engine_sem=desc_init).then_inc(s_stage[j], 16)
                wait(desc_init, j + 1)

            wait(s_w, 16 * 13)
            pl.tensor_scalar(ksc[:, :], ksc[:, :], 1.0, None, ALU.add).then_inc(s_rope, 1)
            pl.tensor_scalar(qsc[:, :], qsc[:, :], 1.0, None, ALU.add).then_inc(s_rope, 1)
            wait(s_rope, 2)
            wait(s_trig, 2)
            for lo in range(2):
                for scl, k0, k1 in ((ksc, 0, 1), (qsc, 1, 3)):
                    n = k1 - k0
                    pl.tensor_tensor(
                        ropeC[:, :, lo, k0:k1, :], trig[:, 1].unsqueeze(2).broadcast_to([128, NT, n, half]),
                        scl[:, half * lo:half * lo + half].unsqueeze(1).unsqueeze(1).broadcast_to([128, NT, n, half]),
                        ALU.mult).then_inc(s_rope, 1)
            wait(s_rope, 6)

            def cached(t, r):
                pl.tensor_copy(row_now[:, 0, r:r + 1], idx[:, 0, bass.ds(t, 1)]).then_inc(row4_copied, 1)
                wait(row4_copied, t + 1)
                pl.indirect_dma_start(
                    out=kvb[:, r, :], out_offset=None, in_=pool_rows4,
                    in_offset=bass.IndirectOffsetOnAxis(ap=row_now[:, 0, r:r + 1], axis=0),
                    bounds_check=4 * NPOOL - 1, oob_is_err=False, engine_sem=desc_cache).then_inc(s_cache[r], 16)
                wait(desc_cache, t + 1)

            def phase1(h, u):
                t, k, p = at_step(h, u, 2)
                if valid(t):
                    wait(kq_copied, t + 1)
                    if reused(t):
                        wait(rsum_done, t - 1)
                    c = ropeC[:, bass.ds(t, 1)].rearrange("p o a k d -> p (o a k) d")
                    pl.tensor_tensor(ropeA[:, p, :].rearrange("p (k n d) -> p k n d", k=6, d=half),
                                     kqs[:, p, :].rearrange("p (k n d) -> p k n d", k=6, d=half),
                                     c.unsqueeze(2).broadcast_to([128, 6, G, half]), ALU.mult).then_inc(prods_done, 1)
                t, k, p = at_step(h, u, 3)
                if valid(t):
                    wait(krow_done, t + 1)
                    wait(v_copied, t + 1)
                    if isinstance(t, int) and t == 0:
                        wait(s_idx, 4)
                        wait(s_init, 16 * OWN)
                    if reused(t):
                        wait(s_scat[p], 16 * k)
                    pl.tensor_copy(row_now[:, 3, p:p + 1], idx[:, 3, bass.ds(t, 1)]).then_inc(row1_copied, 1)
                    wait(row1_copied, t + 1)
                    pl.indirect_dma_start(
                        out=merged, out_offset=bass.IndirectOffsetOnAxis(ap=row_now[:, 3, p:p + 1], axis=0),
                        in_=kvrow[:, p, :], in_offset=None,
                        bounds_check=SEGS * BLOCK - 1, oob_is_err=False, engine_sem=desc_scat).then_inc(s_scat[p], 16)
                    wait(desc_scat, t + 1)
                if isinstance(h, int) and 2 * h + u == 4:
                    wait(s_init, 16 * OWN)
                    wait(s_idx, 4)
                    for r in range(RING):
                        cached(r, r)

            steps(pl, phase1, *P1)

            for p in range(2):
                wait(s_scat[p], 16 * (NT // 2))
            wait(s_big, 1)

            def fetch(t, r, n):
                pl.tensor_copy(row_now[:, 1:3, r:r + 1], idx[:, 1:3, bass.ds(t, 1)]).then_inc(rowm_copied, 1)
                wait(rowm_copied, t + 1)
                wait(s_cache[r], 16 * (n + 1))
                pl.indirect_dma_start(
                    out=kvb[:, r, :], out_offset=None, in_=merged_rows4,
                    in_offset=bass.IndirectOffsetOnAxis(ap=row_now[:, 1, r:r + 1], axis=0),
                    bounds_check=SEGS * 4 - 1, oob_is_err=False, engine_sem=desc_fetch).then_inc(s_merge[r], 16)
                wait(desc_fetch, 2 * t + 1)
                pl.indirect_dma_start(
                    out=own[:, r, :], out_offset=None, in_=merged_rows2,
                    in_offset=bass.IndirectOffsetOnAxis(ap=row_now[:, 2, r:r + 1], axis=0),
                    bounds_check=SEGS * 8 - 1, oob_is_err=False, engine_sem=desc_fetch).then_inc(s_own[r], 16)
                wait(desc_fetch, 2 * t + 2)

            def masks(t, p):
                pl.tensor_copy(pos_now[:, :, p:p + 1], pos3[:, 0:2, bass.ds(t, 1)]).then_inc(pos_copied, 1)
                wait(pos_copied, t + 1)
                pl.tensor_scalar(mask[:, p, 0:NKB], cc("backpos"), pos_now[:, 0, p:p + 1], NEG,
                                 ALU.is_lt, ALU.mult).then_inc(mask_done, 1)
                pl.tensor_scalar(mask[:, p, NKB:NK], cc("ownpos"), pos_now[:, 1, p:p + 1], NEG,
                                 ALU.is_gt, ALU.mult).then_inc(mask_done, 1)

            fetch(0, 0, 0)
            fetch(1, 1, 0)
            wait(qT_done, NT)
            for p in range(2):
                pl.memset(prob[:, p, :, NK:KW], 0.0).then_inc(s_pad, 1)
            masks(0, 0)

            def phase2(h, u):
                t, k, p, r, n = at_step4(h, u, -1)
                if valid(t):
                    if reused(t):
                        wait(sc_done, 3 * (t - 1))
                    masks(t, p)
                t, k, p, r, n = at_step4(h, u, -2)
                if valid(t):
                    if not isinstance(t, int) or t >= RING:
                        wait(kT_done, t - 3)
                        wait(vnew_done, NB * (t - 3))
                    fetch(t, r, n)
                t, k, p, r, n = at_step4(h, u, -4)
                if valid(t):
                    wait(kT_done, t - 3)
                    wait(vold_done, NB * (t - 3))
                    cached(t, r)

            steps(pl, phase2, NT, *P2R[1:])

        @block.scalar
        def _(act):
            for dst, src in ((qsc[:, :], qscale.broadcast_to([128, HD])), (ksc[:, :], kscale.broadcast_to([128, HD])),
                             (adp_i[:, :], adapter.broadcast_to([E * R, B])), (scal[:, :], scaling),
                             (wqkv_sb[:, :, :], wqkv.rearrange("(c p) n -> p c n", p=128)),
                             (at_sb[:, :, :], at.rearrange("(c p) n -> p c n", p=128)),
                             (wt_sb[:, :, :], wt.rearrange("(c p) n -> p c n", p=128)),
                             (bt_sb[:, :, :], bt.rearrange("(c p) n -> p c n", p=128)),
                             (wp_sb[:, :, :], wp.rearrange("(c p) n -> p c n", p=128)),
                             (wo_sb[:, :, :], wo.rearrange("(c p) n -> p c n", p=128)),
                             (wbase_sb[:, :, :], wbase.rearrange("(c p) n -> p c n", p=128))):
                act.dma_start(dst, src).then_inc(s_w, 16)
            act.wait_ge(s_con, 16)
            act.copy(identb[:, :], ident).then_inc(s_prec, 1)
            act.wait_ge(s_ix, 13 + SPAN)
            act.dma_start(blocks_d, blk).then_inc(s_blkd, 16)
            act.wait_ge(s_idx, 3)
            for i in range(2):
                act.activation(trig[:, i], redu[:, i], ACT.Sin).then_inc(s_trig, 1)
            for j in range(OWN):
                act.wait_ge(s_stage[j], 16)
                act.dma_start(merged_blocks[B * j:B * j + B, :], stage[:, j, :]).then_inc(s_init, 16)
            act.wait_ge(s_pre, 1)
            act.copy(aw[:, :, :], ps_pre[:, 0:128].rearrange("p (c n) -> p c n", c=2)).then_inc(s_prec, 1)
            act.copy(bw[:, :], ps_pre[0:E * R, 128:384]).then_inc(s_prec, 1)

            def phase1(h, u):
                t, k, p = at_step(h, u, 0)
                if valid(t):
                    act.wait_ge(x1_done, t + 1)
                    act.copy(xall[:, bass.ds(t, 1), :].rearrange("p o n -> p (o n)"), x1s[:, p, :]
                             ).then_inc(x1_saved, 1)
                t, k, p = at_step(h, u, 1)
                if valid(t):
                    act.wait_ge(xT_done, t + 1)
                    if reused(t):
                        act.wait_ge(qkv_done, t - 1)
                    act.copy(x1T[:, p], ps_xT[p][:, 0:256].rearrange("p (c n) -> p c n", c=2)
                             ).then_inc(xT_copied, 1)
                t, k, p = at_step(h, u, 2)
                if valid(t):
                    act.wait_ge(qkv_done, t + 1)
                    if reused(t):
                        act.wait_ge(prods_done, t - 1)
                        act.wait_ge(rsum_done, t - 1)
                    act.copy(kqs[:, p, :], ps_qkv[p][:, 0:384]).then_inc(kq_copied, 1)
                    if reused(t):
                        act.wait_ge(ss_done, t - 1)
                    act.activation(sq[:, p, :], ps_qkv[p][:, 0:384], ACT.Square).then_inc(sq_done, 1)
                    if reused(t):
                        act.wait_ge(s_scat[p], 16 * k)
                    act.copy(kvrow[:, p, 128:256], ps_qkv[p][:, 384:512]).then_inc(v_copied, 1)
                t, k, p = at_step(h, u, 3)
                if valid(t):
                    act.wait_ge(ss_done, t + 1)
                    if reused(t):
                        act.wait_ge(rinv_done, t - 1)
                    act.activation(rt[:, p, :], ss[:, p, :], ACT.Sqrt).then_inc(rt_done, 1)
                t, k, p = at_step(h, u, 4)
                if valid(t):
                    act.wait_ge(qrT_done, t + 1)
                    act.copy(qT[:, bass.ds(t, 1), :].rearrange("p o n -> p (o n)"), qrT[:, p, :]).then_inc(qT_done, 1)

            steps(act, phase1, *P1)
            act.wait_ge(s_pad, 2)
            act.wait_ge(s_init, 16 * OWN)
            act.wait_ge(qT_done, NT)

            def queries(t, p):
                if reused(t):
                    act.wait_ge(sc_done, 3 * (t - 1))
                for b in range(NB):
                    only = con[:, COL["batch"][0] + b:COL["batch"][0] + b + 1]
                    act.activation(qbd[:, p, :, 32 * b:32 * b + 32],
                                   qT[:, bass.ds(t, 1), :].rearrange("p o (h c) -> p (o h) c", h=H),
                                   ACT.Copy, scale=only).then_inc(qbd_done, 1)

            queries(0, 0)

            def phase2(h, u):
                t, k, p, r, n = at_step4(h, u, 0)
                t2, k2, p2, _, _ = at_step4(h, u, 2)
                if valid(t2):
                    act.wait_ge(onT_done, t2 + 1)
                    act.copy(onT[:, :, :], ps_t[:, 0:256].rearrange("p (c n) -> p c n", c=2)
                             ).then_inc(onT_copied, 1)
                for i in range(3):
                    if i == 1 and valid(t2):
                        act.wait_ge(x2T_done, t2 + 1)
                        act.copy(x2T[:, :, :], ps_t[:, 256:512].rearrange("p (c n) -> p c n", c=2)
                                 ).then_inc(x2T_copied, 1)
                    if valid(t):
                        if i == 0 and reused(t):
                            act.wait_ge(pT_done, 3 * (t - 1))
                        act.wait_ge(nmx_done, 3 * t + i + 1)
                        for j, hd in enumerate(HEADS[i]):
                            act.activation(prob[:, p, hd, 0:NK], ps_sc[i][:, j * NK:j * NK + NK], ACT.Exp,
                                           bias=nmx[:, p, hd:hd + 1], scale=SCALE,
                                           accum_out=den[:, p, hd:hd + 1]).then_inc(exp_done, 1)
                if valid(t):
                    act.wait_ge(s_own[r], 16 * (n + 1))
                    if reused(t):
                        act.wait_ge(pv_done, t - 1)
                    new = own[:, r, :].rearrange("p (f k g d) -> p f k g d", f=2, k=2, g=G)
                    for b in range(NB):
                        act.activation(vbd[:, p, 4:6, :, 32 * b:32 * b + 32], new[:, :, 1], ACT.Copy,
                                       scale=con[:, COL["batch"][0] + b:COL["batch"][0] + b + 1]).then_inc(vnew_done, 1)
                t1, _, p1, _, _ = at_step4(h, u, -1)
                if valid(t1):
                    queries(t1, p1)

            steps(act, phase2, *P2R)

        @block.vector
        def _(ve):
            count = [0]

            def link(ins):
                count[0] += 1
                ins.then_inc(s_ix, 1)
                ve.wait_ge(s_ix, count[0])

            ve.wait_ge(s_small, 32)
            ve.wait_ge(s_con, 16)
            link(ve.tensor_copy(kvf, kv_i))
            link(ve.tensor_copy(tabf, tab_i))
            link(ve.tensor_scalar(slot0, kvf, 1.0 / BLOCK, -7.5 / BLOCK, ALU.mult, ALU.add))
            link(ve.tensor_scalar(slot0, slot0, MAGIC, None, ALU.add))
            link(ve.tensor_scalar(slot0, slot0, -MAGIC, None, ALU.add))
            link(ve.scalar_tensor_tensor(out=off0, in0=slot0, scalar=-float(BLOCK), in1=kvf,
                                         op0=ALU.mult, op1=ALU.add))
            link(ve.tensor_scalar(target, cc("span", B), slot0, None, ALU.add))
            for i in range(SPAN):
                link(ve.scalar_tensor_tensor(out=pick, in0=cc("slot", B), scalar=target[:, i:i + 1], in1=tabf,
                                             op0=ALU.is_equal, op1=ALU.mult, accum_out=blk[:, i:i + 1]))
            link(ve.tensor_scalar(bits[:, 0:1], off0, 8.0, None, ALU.is_ge))
            link(ve.scalar_tensor_tensor(out=rest[:, 0:1], in0=bits[:, 0:1], scalar=-8.0, in1=off0,
                                         op0=ALU.mult, op1=ALU.add))
            link(ve.tensor_scalar(bits[:, 1:2], rest[:, 0:1], 4.0, None, ALU.is_ge))
            link(ve.scalar_tensor_tensor(out=rest[:, 1:2], in0=bits[:, 1:2], scalar=-4.0, in1=rest[:, 0:1],
                                         op0=ALU.mult, op1=ALU.add))
            link(ve.tensor_scalar(bits[:, 2:3], rest[:, 1:2], 2.0, None, ALU.is_ge))
            link(ve.scalar_tensor_tensor(out=bits[:, 3:4], in0=bits[:, 2:3], scalar=-2.0, in1=rest[:, 1:2],
                                         op0=ALU.mult, op1=ALU.add))
            assert count[0] == 13 + SPAN
            ve.tensor_copy(blk_i[:, :], blk).then_inc(s_idx, 1)

            link(ve.tensor_scalar(posf[:, 2, :], cc("tok", B), kvf, None, ALU.add))
            link(ve.tensor_scalar(posf[:, 1, :], cc("tok", B), rest[:, 1:2], None, ALU.add))
            link(ve.tensor_tensor(lim, rest[:, 1:2], kvf, ALU.subtract))
            link(ve.tensor_scalar(lim, lim, float(WINDOW), None, ALU.add))
            link(ve.tensor_scalar(posf[:, 0, :], posf[:, 1, :], 1.0, lim, ALU.add, ALU.max))

            link(ve.tensor_scalar(cidx, blk, 4.0, None, ALU.mult))
            link(ve.tensor_tensor(rows4[:, 0, :].rearrange("p (i f) -> p i f", f=4),
                                  cidx[:, 0:9].unsqueeze(2).broadcast_to([B, 9, 4]),
                                  cc("m4", B).rearrange("p (i f) -> p i f", f=4), ALU.add))

            link(ve.tensor_scalar(cover[:, 0, :], cc("m16", B)[:, 0:17], off0, None, ALU.is_ge))
            link(ve.tensor_scalar(cover[:, 2, :], cc("m16", B)[:, 0:17], off0, None, ALU.is_lt))
            link(ve.memset(cover[:, 1, :], 1.0))
            link(ve.memset(cover[:, :, 16:17], 1.0))
            ve.wait_ge(s_blkr, 16)
            for j in range(OWN):
                link(ve.tensor_scalar(eq[j], allblk, blk[:, BACK + j:BACK + j + 1], None, ALU.is_equal))
            for j in range(OWN):
                a = COL["later"][0] + j * B * OWN
                link(ve.tensor_tensor(el[j].rearrange("p (b i) -> p b i", i=OWN),
                                      eq[j].rearrange("p (b i) -> p b i", i=SPAN)[:, :, BACK:SPAN],
                                      con[0:B, a:a + B * OWN].rearrange("p (b i) -> p b i", i=OWN), ALU.mult))
            ve.wait_ge(s_ipe, 1)
            link(ve.tensor_copy(dead, ps_idx[0:B, 0:51].rearrange("p (j n) -> p j n", j=OWN)))
            link(ve.tensor_scalar(canon_seg, dead[:, :, 16], 0.0, None, ALU.is_equal))
            link(ve.tensor_tensor(canon_seg, canon_seg, cc("seg1", B), ALU.mult))
            seg_ready = count[0]
            ve.wait_ge(s_ipe, 2)
            link(ve.tensor_copy(canon, ps_idx[0:B, 64:64 + SPAN]))
            link(ve.tensor_scalar(cmiss, canon, 0.0, BIG, ALU.is_equal, ALU.mult))
            link(ve.tensor_scalar(cidx, canon, 4.0, -4.0, ALU.mult, ALU.add))
            link(ve.tensor_tensor(cidx, cidx, cmiss, ALU.add))
            link(ve.tensor_tensor(rows4[:, 1, :].rearrange("p (i f) -> p i f", f=4),
                                  cidx[:, 0:9].unsqueeze(2).broadcast_to([B, 9, 4]),
                                  cc("m4", B).rearrange("p (i f) -> p i f", f=4), ALU.add))
            link(ve.tensor_scalar(cidx, canon, 8.0, -8.0, ALU.mult, ALU.add))
            link(ve.tensor_tensor(rows2.rearrange("p (i f) -> p i f", f=8),
                                  cidx[:, BACK:SPAN].unsqueeze(2).broadcast_to([B, OWN, 8]),
                                  cc("m8", B).rearrange("p (i f) -> p i f", f=8), ALU.add))
            link(ve.tensor_scalar(cidx, canon, 16.0, -16.0, ALU.mult, ALU.add))
            link(ve.tensor_tensor(rows1.rearrange("p (i f) -> p i f", f=16),
                                  cidx[:, BACK:SPAN].unsqueeze(2).broadcast_to([B, OWN, 16]),
                                  cc("m16", B).rearrange("p (i f) -> p i f", f=16), ALU.add))
            link(ve.tensor_scalar(dead, dead, 1.0, BIG, ALU.is_ge, ALU.mult))
            link(ve.tensor_tensor(rows1.rearrange("p (i f) -> p i f", f=16),
                                  rows1.rearrange("p (i f) -> p i f", f=16), dead[:, :, 0:16], ALU.add))
            link(ve.memset(idxf[:, :, :], BIG))

            def shift(dst, tmp, src, by, bit):
                n = dst.shape[-1]
                s0 = src[:, :, 0:n] if len(src.shape) == 3 else src[:, 0:n]
                s1 = src[:, :, by:by + n] if len(src.shape) == 3 else src[:, by:by + n]
                tm = tmp[:, :, 0:n] if len(src.shape) == 3 else tmp[:, 0:n]
                link(ve.tensor_tensor(tm, s1, s0, ALU.subtract))
                link(ve.scalar_tensor_tensor(out=dst, in0=tm, scalar=bits[:, bit:bit + 1], in1=s0,
                                             op0=ALU.mult, op1=ALU.add))

            shift(rows4b[:, :, 0:33], tmp4, rows4, 2, 0)
            shift(idxf[:, 0:2, :], tmp4, rows4b, 1, 1)
            shift(rows2b[:, 0:20], tmp2, rows2, 4, 0)
            shift(idxf[:, 2, 0:Q2], tmp2, rows2b, 2, 1)
            shift(rows1b[:, 0:39], tmp1, rows1, 8, 0)
            shift(rows1[:, 0:35], tmp1, rows1b, 4, 1)
            shift(rows1b[:, 0:33], tmp1, rows1, 2, 2)
            shift(idxf[:, 3, :], tmp1, rows1b, 1, 3)
            idx_ready = count[0]
            build.ready = (seg_ready, idx_ready)

            ve.wait_ge(s_ipe, 3)
            trI = ps_idx[:, 128:192].rearrange("p (t b) -> p b t", b=NB)
            trP = ps_idx[0:96, 192:256].rearrange("p (t b) -> p b t", b=NB)
            for b in range(NB):
                for kind in range(4):
                    link(ve.tensor_copy(idx[32 * b:32 * b + 32, kind, :], trI[32 * kind:32 * kind + 32, b, :]))
                for kind in range(3):
                    link(ve.tensor_copy(pos3[32 * b:32 * b + 32, kind, :], trP[32 * kind:32 * kind + 32, b, :]))
            ve.engine_nop().then_inc(s_idx, 1)

            link(ve.tensor_tensor(ang, pos3[:, 2, :].unsqueeze(2).broadcast_to([128, NT, half]),
                                  cc("inv").unsqueeze(1).broadcast_to([128, NT, half]), ALU.mult))
            c1 = float(np.float32(6.28125))
            c2 = float(np.float32(np.round((2 * np.pi - c1) * 2.0 ** 21) / 2.0 ** 21))
            c3 = float(np.float32(2 * np.pi - c1 - c2))
            for i in range(2):
                link(ve.tensor_scalar(turn, ang, 1.0 / (2 * PI), 0.25 * i, ALU.mult, ALU.add))
                link(ve.tensor_scalar(turn, turn, MAGIC, None, ALU.add))
                link(ve.tensor_scalar(turn, turn, -MAGIC, None, ALU.add))
                link(ve.scalar_tensor_tensor(out=redu[:, i], in0=turn, scalar=-c1, in1=ang, op0=ALU.mult, op1=ALU.add))
                link(ve.scalar_tensor_tensor(out=redu[:, i], in0=turn, scalar=-c2, in1=redu[:, i],
                                             op0=ALU.mult, op1=ALU.add))
                link(ve.scalar_tensor_tensor(out=redu[:, i], in0=turn, scalar=-c3, in1=redu[:, i],
                                             op0=ALU.mult, op1=ALU.add))
                link(ve.tensor_scalar(redu[:, i], redu[:, i], i * PI / 2, PI, ALU.add, ALU.min))
                link(ve.tensor_scalar(redu[:, i], redu[:, i], -PI, None, ALU.max))
            ve.engine_nop().then_inc(s_idx, 1)
            ve.wait_ge(s_w, 16 * 13)
            link(ve.tensor_copy(adp_f[:, :], adp_i[:, :]))
            link(ve.tensor_scalar(zscale[:, :], adp_f[:, :], cc("adapter", E * R), scal[:, 0:1],
                                  ALU.is_equal, ALU.mult))
            ve.wait_ge(s_rope, 2)
            ve.wait_ge(s_trig, 2)
            for lo in range(2):
                for k, scl in enumerate((ksc, qsc, qsc)):
                    link(ve.scalar_tensor_tensor(
                        out=ropeS[:, :, lo, k, :], in0=trig[:, 0], scalar=2.0 * lo - 1.0,
                        in1=scl[:, half - half * lo:HD - half * lo].unsqueeze(1).broadcast_to([128, NT, half]),
                        op0=ALU.mult, op1=ALU.mult))
            ve.engine_nop().then_inc(s_idx, 1)

            def phase1(h, u):
                t, k, p = at_step(h, u, 0)
                if valid(t):
                    ve.wait_ge(l0_done, t + 1)
                    if reused(t):
                        ve.wait_ge(xT_done, t - 1)
                        ve.wait_ge(x1_saved, t - 1)
                    ve.tensor_tensor(x1s[:, p, :], xall[:, bass.ds(t, 1), :].rearrange("p o n -> p (o n)"),
                                     ps_l0[p][:, 0:D], ALU.add).then_inc(x1_done, 1)
                t, k, p = at_step(h, u, 2)
                if valid(t):
                    ve.wait_ge(sq_done, t + 1)
                    if reused(t):
                        ve.wait_ge(rt_done, t - 1)
                    ve.tensor_reduce(ss[:, p, :], sq[:, p, :].rearrange("p (a n d) -> p n a d", a=2, d=half), AX_XY,
                                     ALU.add).then_inc(kT_part, 1)
                    ve.wait_ge(kT_part, t + 1)
                    ve.tensor_scalar(ss[:, p, :], ss[:, p, :], 1.0 / HD, EPS, ALU.mult, ALU.add).then_inc(ss_done, 1)
                    ve.wait_ge(kq_copied, t + 1)
                    sn = ropeS[:, bass.ds(t, 1)].rearrange("p o a k d -> p (o a k) d")
                    for lo in range(2):
                        ve.tensor_tensor(
                            ropeB[:, p, 192 * lo:192 * lo + 192].rearrange("p (k n d) -> p k n d", k=3, d=half),
                            kqs[:, p, 192 - 192 * lo:384 - 192 * lo].rearrange("p (k n d) -> p k n d", k=3, d=half),
                            sn[:, 3 * lo:3 * lo + 3].unsqueeze(2).broadcast_to([128, 3, G, half]),
                            ALU.mult).then_inc(cross_done, 1)
                t, k, p = at_step(h, u, 3)
                if valid(t):
                    ve.wait_ge(rt_done, t + 1)
                    ve.reciprocal(rinv[:, p, :], rt[:, p, :]).then_inc(rinv_done, 1)
                    ve.wait_ge(prods_done, t + 1)
                    ve.wait_ge(cross_done, 2 * (t + 1))
                    ve.tensor_tensor(rsum[:, p, :], ropeA[:, p, :], ropeB[:, p, :], ALU.add).then_inc(rsum_done, 1)
                    ve.wait_ge(rinv_done, t + 1)
                    ve.wait_ge(rsum_done, t + 1)
                    if reused(t):
                        ve.wait_ge(s_scat[p], 16 * k)
                    halves = rsum[:, p, :].rearrange("p (a n d) -> p a n d", a=2, d=half)
                    ve.tensor_tensor(kvrow[:, p, 0:128].rearrange("p (n a d) -> p a n d", a=2, d=half),
                                     halves[:, :, 0:G, :],
                                     rinv[:, p, 0:G].unsqueeze(1).unsqueeze(3).broadcast_to([128, 2, G, half]),
                                     ALU.mult).then_inc(krow_done, 1)
                    ve.tensor_tensor(qrot[:, p, :].rearrange("p (n a d) -> p a n d", a=2, d=half),
                                     halves[:, :, G:12, :],
                                     rinv[:, p, G:12].unsqueeze(1).unsqueeze(3).broadcast_to([128, 2, H, half]),
                                     ALU.mult).then_inc(qrot_done, 1)
                    ve.wait_ge(qrot_done, t + 1)
                    if reused(t):
                        ve.wait_ge(qT_done, t - 1)
                    ve.transpose(qrT[:, p, :], qrot[:, p, :]).then_inc(qrT_done, 1)

            steps(ve, phase1, *P1)

            def keys(t, p, r, n):
                ve.wait_ge(s_merge[r], 16 * (n + 1))
                ve.wait_ge(s_own[r], 16 * (n + 1))
                if reused(t):
                    ve.wait_ge(sc_done, 3 * (t - 1))
                old = kvb[:, r, :].rearrange("p (f k g d) -> p f k g d", f=4, k=2, g=G)
                new = own[:, r, :].rearrange("p (f k g d) -> p f k g d", f=2, k=2, g=G)
                ve.transpose(kT[:, p, :, 0:NKB].rearrange("p g (f r) -> p f g r", f=4), old[:, :, 0])
                ve.transpose(kT[:, p, :, NKB:NKB + 32], new[:, 0, 0]).then_inc(kT_part, 1)
                ve.wait_ge(kT_part, NT + t + 1)
                ve.transpose(kT[:, p, :, NKB + Q2:NKB + Q2 + 32], new[:, 1, 0]).then_inc(kT_done, 1)

            def values(t, p, r, n):
                if reused(t):
                    ve.wait_ge(pv_done, t - 1)
                old = kvb[:, r, :].rearrange("p (f k g d) -> p f k g d", f=4, k=2, g=G)
                for b in range(NB):
                    ve.tensor_scalar(vbd[:, p, 0:4, :, 32 * b:32 * b + 32], old[:, :, 1],
                                     con[:, COL["batch"][0] + b:COL["batch"][0] + b + 1], None,
                                     ALU.mult).then_inc(vold_done, 1)

            keys(0, 0, 0, 0)
            ve.wait_ge(s_pad, 2)

            def maxima(t, p, i):
                a, n = HEADS[i][0], len(HEADS[i])
                ve.wait_ge(sc_done, 3 * t + i + 1)
                ve.tensor_reduce(mx[:, p, a:a + n], ps_sc[i][:, 0:n * NK].rearrange("p (n k) -> p n k", n=n),
                                 AX_X, ALU.max).then_inc(mx_done, 1)
                ve.wait_ge(mx_done, 3 * t + i + 1)
                ve.tensor_scalar(nmx[:, p, a:a + n], mx[:, p, a:a + n], -SCALE, None, ALU.mult).then_inc(nmx_done, 1)

            def phase2(h, u):
                t, k, p, r, n = at_step4(h, u, 0)
                t2, k2, p2, _, _ = at_step4(h, u, 2)
                t3, k3, p3, _, _ = at_step4(h, u, 3)
                if valid(t2):
                    ve.wait_ge(pv_done, t2 + 1)
                    ve.transpose(oraw[:, :], ps_o[:, 0:256]).then_inc(oraw_done, 1)
                    ve.reciprocal(rden[:, p2, :], den[:, p2, :]).then_inc(rden_done, 1)
                    ve.wait_ge(oraw_done, t2 + 1)
                    ve.wait_ge(rden_done, t2 + 1)
                    ve.tensor_tensor(onrm[:, :].rearrange("p (n d) -> p n d", d=HD),
                                     oraw[:, :].rearrange("p (n d) -> p n d", d=HD),
                                     rden[:, p2, :].unsqueeze(2).broadcast_to([128, H, HD]),
                                     ALU.mult).then_inc(onrm_done, 1)
                if valid(t):
                    maxima(t, p, 0)
                    maxima(t, p, 1)
                if valid(t2):
                    ve.wait_ge(wo_done, t2 + 1)
                    ve.tensor_tensor(x2s[:, p2, :], xall[:, bass.ds(t2, 1), :].rearrange("p o n -> p (o n)"),
                                     ps_wo, ALU.add).then_inc(x2_done, 1)
                if valid(t):
                    maxima(t, p, 2)
                if valid(t3):
                    ve.wait_ge(l3_done, t3 + 1)
                    if reused(t3):
                        ve.wait_ge(s_out[p3], 16 * k3)
                    ve.tensor_tensor(x4s[:, p3, :], x3s[:, p3, :], ps_l3, ALU.add).then_inc(x4_done, 1)
                if valid(t):
                    values(t, p, r, n)
                if valid(t2):
                    ve.wait_ge(z_done, t2 + 1)
                    ve.tensor_tensor(zm[:, :].rearrange("p (b c) -> p b c", b=NB),
                                     ps_z.rearrange("p (b c) -> p b c", b=NB),
                                     zscale[:, bass.ds(t2 * NB, NB)].unsqueeze(2).broadcast_to([E * R, NB, TOK]),
                                     ALU.mult).then_inc(zm_done, 1)
                t1, _, p1, r1, n1 = at_step4(h, u, -1)
                if valid(t1):
                    keys(t1, p1, r1, n1)
                if valid(t):
                    if reused(t):
                        ve.wait_ge(pv_done, t - 1)
                    ve.wait_ge(exp_done, H * (t + 1))
                    for f0, f1, a in ((0, 4, 0), (4, 5, NKB), (5, 6, NKB + Q2)):
                        ve.transpose(pT[:, p, f0:f1, :].rearrange("p f (h c) -> p h f c", h=H),
                                     prob[:, p, :, a:a + 32 * (f1 - f0)].rearrange("p h (f c) -> p h f c", c=32)
                                     ).then_inc(pT_done, 1)
                if valid(t2):
                    ve.wait_ge(l2_done, t2 + 1)
                    ve.tensor_tensor(x3s[:, p2, :], x2s[:, p2, :], ps_l2, ALU.add).then_inc(x3_done, 1)

            steps(ve, phase2, *P2R)

        @block.tensor
        def _(pe):
            seg_ready, idx_ready = build.ready
            pe.wait_ge(s_ix, seg_ready - 3)
            for i in range(OWN):
                for j in range(OWN):
                    mm = pe.matmul(ps_idx[0:B, 17 * i:17 * i + 17],
                                   el[j].rearrange("p (b i) -> p i b", i=OWN)[:, i], cover[:, j, :],
                                   start=(j == 0), stop=(j == OWN - 1))
            mm.then_inc(s_ipe, 1)
            pe.wait_ge(s_ix, seg_ready)
            for i in range(SPAN):
                for j in range(OWN):
                    mm = pe.matmul(ps_idx[0:B, 64 + i:65 + i], eq[j].rearrange("p (b i) -> p i b", i=SPAN)[:, i],
                                   canon_seg[:, j:j + 1], start=(j == 0), stop=(j == OWN - 1))
            mm.then_inc(s_ipe, 1)
            pe.wait_ge(s_w, 16 * 13)
            for m in range(2):
                for c in range(2):
                    pe.matmul(ps_pre[:, 64 * m:64 * m + 64], wt_sb[:, c, 128 * m:128 * m + 128], at_sb[:, c, :],
                              start=(c == 0), stop=(c == 1))
            for c in range(2):
                mm = pe.matmul(ps_pre[0:E * R, 128:384], bt_sb[:, c, :], wp_sb[:, c, :], start=(c == 0), stop=(c == 1))
            mm.then_inc(s_pre, 1)
            pe.wait_ge(s_ix, idx_ready)
            pe.transpose(ps_idx[:, 128:192], idxf.rearrange("p k r -> p (k r)"), con[0:B, 0:B])
            pe.transpose(ps_idx[0:96, 192:256], posf.rearrange("p k r -> p (k r)"), con[0:B, 0:B]).then_inc(s_ipe, 1)

            def phase1(h, u):
                t, k, p = at_step(h, u, 0)
                if valid(t):
                    if isinstance(t, int):
                        pe.wait_ge(s_x[t // 4], 16)
                    elif u == 0:
                        pass
                    pe.wait_ge(s_w0[p], 64 * (k + 1))
                    if reused(t):
                        pe.wait_ge(x1_done, t - 1)
                    pe.matmul(ps_l0[p][:, 0:D], w0bd[:, p, :],
                              xall[:, bass.ds(t, 1), :].rearrange("p o n -> p (o n)"),
                              start=True, stop=True).then_inc(l0_done, 1)
                t, k, p = at_step(h, u, 1)
                if valid(t):
                    pe.wait_ge(x1_done, t + 1)
                    if reused(t):
                        pe.wait_ge(xT_copied, t - 1)
                    for c in range(2):
                        mm = pe.transpose(ps_xT[p][:, 128 * c:128 * c + 128], x1s[:, p, 128 * c:128 * c + 128], ident)
                    mm.then_inc(xT_done, 1)
                t, k, p = at_step(h, u, 2)
                if valid(t):
                    pe.wait_ge(xT_copied, t + 1)
                    if reused(t):
                        pe.wait_ge(kq_copied, t - 1)
                        pe.wait_ge(sq_done, t - 1)
                        pe.wait_ge(v_copied, t - 1)
                    for c in range(2):
                        mm = pe.matmul(ps_qkv[p][:, :], x1T[:, p, c, :], wqkv_sb[:, c, :], start=(c == 0), stop=(c == 1))
                    mm.then_inc(qkv_done, 1)

            for i in range(4):
                pe.wait_ge(s_x[i], 16)
            steps(pe, phase1, *P1)

            pe.wait_ge(kq_copied, NT)
            pe.wait_ge(sq_done, NT)
            pe.wait_ge(v_copied, NT)
            pe.wait_ge(s_idx, 4)
            pe.wait_ge(s_prec, 3)

            def scores(t, p, i):
                if i == 0:
                    pe.wait_ge(kT_done, t + 1)
                    pe.wait_ge(qbd_done, NB * (t + 1))
                    pe.wait_ge(mask_done, 2 * (t + 1))
                if not isinstance(t, int) or t >= 1:
                    pe.wait_ge(exp_done, H * t - H + HEADS[i][-1] + 1)
                n = len(HEADS[i])
                pe.matmul(ps_sc[i][:, 0:n * NK], identb[:, :],
                          mask[:, p, :].unsqueeze(1).broadcast_to([128, n, NK]), start=True, stop=False,
                          skip_group_check=True)
                for j, hd in enumerate(HEADS[i]):
                    mm = pe.matmul(ps_sc[i][:, j * NK:j * NK + NK], qbd[:, p, hd, :], kT[:, p, hd // GSZ, 0:NK],
                                   start=False, stop=(j == n - 1), skip_group_check=True)
                mm.then_inc(sc_done, 1)

            def weighted(t, p, groups):
                if groups[0] == 0:
                    pe.wait_ge(pT_done, 3 * (t + 1))
                    pe.wait_ge(vold_done, NB * (t + 1))
                    pe.wait_ge(vnew_done, NB * (t + 1))
                    if not isinstance(t, int) or t >= 1:
                        pe.wait_ge(oraw_done, t)
                for g in groups:
                    for f in range(6):
                        mm = pe.matmul(ps_o[:, 64 * g:64 * g + 64], vbd[:, p, f, g, :], pT[:, p, f, 64 * g:64 * g + 64],
                                       start=(f == 0), stop=(f == 5))
                if groups[-1] == G - 1:
                    mm.then_inc(pv_done, 1)

            def phase2(h, u):
                t, k, p = at_step(h, u, 0)
                t1, k1, p1 = at_step(h, u, 1)
                t2, k2, p2 = at_step(h, u, 2)
                t3, k3, p3 = at_step(h, u, 3)
                if valid(t):
                    scores(t, p, 0)
                if valid(t2):
                    pe.wait_ge(onrm_done, t2 + 1)
                    for c in range(2):
                        mm = pe.transpose(ps_t[:, 128 * c:128 * c + 128], onrm[:, 128 * c:128 * c + 128], ident)
                    mm.then_inc(onT_done, 1)
                if valid(t):
                    scores(t, p, 1)
                if valid(t2):
                    pe.wait_ge(onT_copied, t2 + 1)
                    for c in range(2):
                        mm = pe.matmul(ps_wo, onT[:, c, :], wo_sb[:, c, :], start=(c == 0), stop=(c == 1))
                    mm.then_inc(wo_done, 1)
                if valid(t):
                    scores(t, p, 2)
                if valid(t3):
                    pe.wait_ge(x3_done, t3 + 1)
                    pe.wait_ge(s_w3[p3], 64 * (k3 + 1))
                    pe.matmul(ps_l3, w3bd[:, p3, :], x3s[:, p3, :], start=True, stop=True).then_inc(l3_done, 1)
                if valid(t1):
                    weighted(t1, p1, [0])
                if valid(t2):
                    pe.wait_ge(x2_done, t2 + 1)
                    for c in range(2):
                        mm = pe.transpose(ps_t[:, 256 + 128 * c:384 + 128 * c], x2s[:, p2, 128 * c:128 * c + 128], ident)
                    mm.then_inc(x2T_done, 1)
                if valid(t1):
                    weighted(t1, p1, [1])
                if valid(t2):
                    pe.wait_ge(x2T_copied, t2 + 1)
                    if not isinstance(t2, int) or t2 >= 1:
                        pe.wait_ge(x4_done, t2)
                    for c in range(2):
                        mm = pe.matmul(ps_z, aw[:, c, :], x2T[:, c, :], start=(c == 0), stop=(c == 1))
                    mm.then_inc(z_done, 1)
                    for c in range(2):
                        pe.matmul(ps_l2, x2T[:, c, :], wbase_sb[:, c, :], start=(c == 0), stop=False)
                if valid(t1):
                    weighted(t1, p1, [2])
                if valid(t2):
                    pe.wait_ge(zm_done, t2 + 1)
                    pe.matmul(ps_l2, zm[:, :], bw[:, :], start=False, stop=True).then_inc(l2_done, 1)
                if valid(t1):
                    weighted(t1, p1, [3])

            steps(pe, phase2, *P2)


def kernel(**inputs):
    import concourse.bacc as _bacc
    from concourse.bass_utils import run_bass_kernel_spmd as _run

    a = {k: np.asarray(v) for k, v in inputs.items()}
    kb, vb = a["L1_cond_k_blocks"], a["L1_cond_v_blocks"]
    pool = np.stack([kb.transpose(0, 2, 1, 3), vb.transpose(0, 2, 1, 3)], axis=2).reshape(NPOOL * BLOCK, ROW)
    arrays = {
        "x": a["x"].reshape(B * TOK, D),
        "cond": a["itok_B_1_198"].reshape(1, B),
        "table": a["itok_Bx257_0_4111"],
        "kv_lens": a["itok_B_37_3939"].reshape(B, 1),
        "adapter": a["itok_B_0_3"].reshape(1, B),
        "subject": a["itok_B_0_7"].reshape(1, B),
        "w0": a["L0_cond_weights"],
        "wqkv": np.concatenate([
            np.concatenate([a["L1_cond_Wk"], a["L1_cond_Wq"]], axis=0).reshape(G + H, 2, HD // 2, D)
            .transpose(1, 0, 2, 3).reshape((G + H) * HD, D), a["L1_cond_Wv"]], axis=0).T,
        "wo": a["L1_cond_Wo"].T,
        "qscale": a["L1_cond_q_norm_scale"].reshape(1, HD),
        "kscale": a["L1_cond_k_norm_scale"].reshape(1, HD),
        "pool": pool,
        "wbase": a["L2_cond_W_base"].T,
        "wt": a["L2_cond_Wt"],
        "at": a["L2_cond_A"].reshape(E * R, D).T,
        "bt": a["L2_cond_B_w"].transpose(1, 0, 2).reshape(D, E * R),
        "wp": a["L2_cond_Wp"].T,
        "scaling": np.repeat(a["L2_cond_scaling"], R).reshape(E * R, 1),
        "w3": a["L3_cond_weights"],
        "consts": constants(),
    }
    nc = _bacc.Bacc("TRN2", target_bir_lowering=False, num_devices=1)
    arrays = {f"in_{k}": np.ascontiguousarray(v) for k, v in arrays.items()}
    args = [nc.dram_tensor(k, v.shape, mybir.dt.from_np(v.dtype), kind="ExternalInput").ap()
            for k, v in arrays.items()]
    out = nc.dram_tensor("out", (B * TOK, D), F32, kind="ExternalOutput").ap()
    build(nc, *args, out)
    r = _run(nc, [arrays], core_ids=[0])
    return r.results[0]["out"].reshape(B, TOK, D)
```

```python
from contextlib import ExitStack

import numpy as np
import concourse.bass as bass
from concourse import mybir

ALU = mybir.AluOpType
ACT = mybir.ActivationFunctionType
AX_X = mybir.AxisListType.X
AX_XY = mybir.AxisListType.XY
F32 = mybir.dt.float32
BF16 = mybir.dt.bfloat16
I32 = mybir.dt.int32

B, TOK, D = 64, 32, 256
H, G, HD = 8, 4, 32
GSZ = H // G
BLOCK, NBLK, NPOOL = 16, 257, 4112
WINDOW = 128
SCALE = 256.0 ** -0.5
EPS = 1e-6
THETA = 10000.0
E, R = 4, 16
NB = 128 // TOK
NT = B // NB
ROW = 2 * G * HD
BACK = WINDOW // BLOCK
OWN = 3
SPAN = BACK + OWN
SEGS = OWN * B
R4 = WINDOW // 4
Q2 = 18
NKB = 4 * R4
NK = NKB + 2 * Q2
KW = 180
RING = 4
BIG = float(2 ** 20)
NEG = -1e30
PI = float(np.pi)
MAGIC = 1.5 * 2.0 ** 23

_COLS = [("ident", 128), ("slot", NBLK), ("span", SPAN), ("m4", 36), ("m8", 24), ("m16", 48),
         ("later", OWN * B * OWN), ("seg1", OWN), ("tok", TOK), ("inv", HD // 2),
         ("backpos", NKB), ("ownpos", 2 * Q2), ("adapter", 1), ("batch", NB), ("rowtok", 1),
         ("place", NB), ("tile", NT)]
COL = {}
_at = 0
for _n, _w in _COLS:
    COL[_n] = (_at, _at + _w)
    _at += _w
NCONST = _at


def constants():
    c = np.zeros((128, NCONST), np.float32)

    def put(name, value):
        a, b = COL[name]
        c[:, a:b] = np.broadcast_to(value, (128, b - a))

    put("ident", np.eye(128, dtype=np.float32))
    put("slot", np.arange(NBLK))
    put("span", np.arange(SPAN) - BACK)
    put("m4", np.arange(36) % 4)
    put("m8", np.arange(24) % 8)
    put("m16", np.arange(48) % 16)
    late = np.zeros((128, OWN, B, OWN), np.float32)
    for j in range(OWN):
        late[:, j] = (OWN * np.arange(128) + j)[:, None, None] > (OWN * np.arange(B)[:, None] + np.arange(OWN))
    put("later", late.reshape(128, -1))
    put("seg1", np.arange(128)[:, None] + B * np.arange(OWN) + 1)
    put("tok", np.arange(TOK))
    half = HD // 2
    put("inv", np.float32(1.0) / np.float32(THETA) ** (np.arange(half, dtype=np.float32) / np.float32(half)))
    put("backpos", (4 * np.arange(R4)[None, :] + np.arange(4)[:, None]).reshape(-1))
    put("ownpos", (2 * np.arange(Q2)[None, :] + np.arange(2)[:, None]).reshape(-1))
    put("adapter", (np.arange(128) // R)[:, None])
    put("rowtok", (np.arange(128) % TOK)[:, None])
    put("place", (np.arange(128) % NB)[:, None] == np.arange(NB))
    put("tile", (np.arange(128) // NB)[:, None] == np.arange(NT))
    put("batch", (np.arange(128) // TOK)[:, None] == np.arange(NB))
    return c


def at_step(h, u, lag):
    return 2 * h + (u - lag), h + (u - lag) // 2, (u - lag) % 2


def at_step4(h, u, lag):
    return 4 * h + (u - lag), 2 * h + (u - lag) // 2, (u - lag) % 2, (u - lag) % 4, h + (u - lag) // 4


def valid(t):
    return not isinstance(t, int) or 0 <= t < NT


def reused(t):
    return not isinstance(t, int) or t >= 2


def steps(eng, body, total, first, last, group=2):
    for i in range(first):
        body(i // group, i % group)
    with eng.Fori(first // group, last // group) as h:
        for u in range(group):
            body(h, u)
    for i in range(last, total):
        body(i // group, i % group)


def build(nc, x, table, kv_lens, of_rows, adapter, subject, w0, wqkv, wo, qscale, kscale, pool,
          wbase, wt, at, bt, wp, scaling, w3, consts, out):
    half = HD // 2
    table_i = table
    w0_rows = w0.rearrange("n c d -> (n c) d")
    merged = nc.dram_tensor("merged", [SEGS * BLOCK, ROW], F32).ap()
    blocks_d = nc.dram_tensor("blocks_scratch", [B, SPAN], F32).ap()
    pool_rows4 = pool.rearrange("(r f) n -> r (f n)", f=4)
    pool_blocks = pool.rearrange("(r f) n -> r (f n)", f=BLOCK)
    merged_rows4 = merged.rearrange("(r f) n -> r (f n)", f=4)
    merged_rows2 = merged.rearrange("(r f) n -> r (f n)", f=2)
    merged_blocks = merged.rearrange("(r f) n -> r (f n)", f=BLOCK)

    with ExitStack() as ctx:
        def sb(name, shape, dt=F32):
            return ctx.enter_context(nc.sbuf_tensor(name, shape, dt))

        def sem(name):
            return ctx.enter_context(nc.semaphore(name))

        con = sb("con", [128, NCONST])

        def cc(name, p=128):
            a, b = COL[name]
            return con[0:p, a:b]

        ident = cc("ident")
        identb = sb("identb", [128, 128], BF16)
        xin = sb("xin", [128, RING, D])
        yall = sb("yall", [128, NT, D])
        zx = sb("zx", [E * R, NT, 128])
        qT = sb("qT", [128, NT, H * TOK])
        big = sb("big", [128, OWN * BLOCK * ROW])
        wqkv_sb = sb("wqkv_sb", [128, 2, 512])
        wbase_sb = sb("wbase_sb", [128, 2, D])
        wt_sb = sb("wt_sb", [128, 2, D])
        at_sb = sb("at_sb", [128, 2, E * R])
        bt_sb = sb("bt_sb", [128, 2, E * R])
        wp_sb = sb("wp_sb", [128, 2, D])
        wo_rows = sb("wo_rows", [128, 2, D])
        aw = sb("aw", [128, 2, E * R])
        aow = sb("aow", [128, 2, E * R])
        wob = sb("wob", [128, 2, D])
        bw = sb("bw", [E * R, D])
        w0c = sb("w0c", [128, NT, TOK])
        w0_i = sb("w0_i", [128, NT], I32)
        w0_f = sb("w0_f", [128, NT])
        w0i = sb("w0i", [128, 2, 128])
        w3bd = sb("w3bd", [128, 2, 128])
        qsc = sb("qsc", [128, HD])
        ksc = sb("ksc", [128, HD])
        subj_sb = sb("subj_sb", [1, B], I32)
        adp_i = sb("adp_i", [E * R, B], I32)
        adp_f = sb("adp_f", [E * R, B])
        scal = sb("scal", [E * R, 1])
        zscale = sb("zscale", [E * R, B])
        idx = sb("idx", [128, 4, NT], I32)
        row_now = sb("row_now", [128, 4, RING], I32)
        pos_now = sb("pos_now", [128, 2, 2])
        pos3 = sb("pos3", [128, 2, NT])
        row_i = sb("row_i", [128, 2, NT], I32)
        rowpos = sb("rowpos", [128, NT])
        kt_rope = sb("kt_rope", [128, 3072])
        ropeC = kt_rope[:, 0:1536].rearrange("p (t a k d) -> p t a k d", t=NT, a=2, k=3)
        ropeS = kt_rope[:, 1536:3072].rearrange("p (t a k d) -> p t a k d", t=NT, a=2, k=3)
        kT = kt_rope[:, 0:2 * G * KW].rearrange("p (a g k) -> p a g k", a=2, g=G)
        mask = sb("mask", [128, 2, NK], BF16)
        work = sb("work", [128, 7008])

        used = [0]

        def carve(*shape):
            n = int(np.prod(shape))
            v = work[:, used[0]:used[0] + n]
            used[0] += n
            names = "abcd"[:len(shape)]
            if len(shape) == 1:
                return v
            return v.rearrange(f"p ({' '.join(names)}) -> p {' '.join(names)}",
                               **{k: s for k, s in zip(names, shape)})

        x1T = carve(2, 2, 128)
        kqs = carve(2, 384)
        sq = carve(2, 384)
        ropeA = carve(2, 384)
        ropeB = carve(2, 384)
        rsum = carve(2, 384)
        kvrow = carve(RING, ROW)
        qrot = carve(2, D)
        qrT = carve(2, D)
        ss = carve(2, 12)
        rt = carve(2, 12)
        rinv = carve(2, 12)
        used[0] = 0
        prob = carve(2, H, KW)
        pT = carve(2, 6, H * TOK)

        stage = big[0:B, :].rearrange("p (j n) -> p j n", j=OWN)
        vbd = big[:, 0:6144].rearrange("p (a f g c) -> p a f g c", a=2, f=6, g=G)
        qbd = big[:, 6144:8192].rearrange("p (a h c) -> p a h c", a=2, h=H)
        own = sb("own", [128, RING, 2 * ROW])
        kvb = big[:, 8192:12288].rearrange("p (a n) -> p a n", a=RING)

        mx = sb("mx", [128, 2, H])
        nmx = sb("nmx", [128, 2, H])
        den = sb("den", [128, 2, H])
        rden = sb("rden", [128, 2, H])
        oraw = sb("oraw", [128, D])
        onrm = sb("onrm", [128, D])
        onT = sb("onT", [128, 2, 128])
        early = sb("early", [128, 2, D])
        zs = sb("zs", [E * R, 128])
        zm = sb("zm", [E * R, 128])
        x3s = sb("x3s", [128, 2, D])
        x4s = sb("x4s", [128, 2, D])

        blk_i = sb("blk_i", [B, SPAN], I32)
        more = sb("more", [B, 192 + 288])

        scratch = sb("scratch", [B, 4096])
        sused = [0]

        def scr(n, p=B):
            v = scratch[0:p, sused[0]:sused[0] + n]
            sused[0] += n
            return v

        kv_i = scr(1).bitcast(I32)
        tab_i = scr(NBLK).bitcast(I32)
        kvf = scr(1)
        tabf = scr(NBLK)
        off0 = scr(1)
        slot0 = scr(1)
        target = scr(SPAN)
        pick = early[0:B, :, :].rearrange('p k n -> p (k n)')[:, 0:NBLK]
        blk = scr(SPAN)
        bits = scr(4)
        rest = scr(4)
        allblk = scr(B * SPAN)
        eq = [scr(B * SPAN // 2).bitcast(BF16) for _ in range(OWN)]
        el = [scr(B * OWN // 2).bitcast(BF16) for _ in range(OWN)]
        cover = scr(OWN * 9).bitcast(BF16)[:, 0:OWN * 17].rearrange("p (j n) -> p j n", j=OWN)
        canon_b = scr(2).bitcast(BF16)[:, 0:OWN]
        spread = scr(6 * 128).rearrange("p (k b r) -> p k b r", k=6, b=NB)
        dead = scr(OWN * 17).rearrange("p (j n) -> p j n", j=OWN)
        canon_seg = scr(OWN)
        canon = scr(SPAN)
        cmiss = scr(SPAN)
        cidx = scr(SPAN)
        rows4 = scr(72).rearrange("p (k m) -> p k m", k=2)
        rows4b = scr(66).rearrange("p (k m) -> p k m", k=2)
        tmp4 = scr(66).rearrange("p (k m) -> p k m", k=2)
        rows2 = scr(24)
        rows2b = scr(24)
        tmp2 = scr(24)
        rows1 = scr(48)
        rows1b = scr(48)
        tmp1 = scr(48)
        idxf = more[:, 192:320].rearrange("p (k r) -> p k r", k=4)
        posf = more[:, 320:384].rearrange("p (k r) -> p k r", k=2)
        lists = more[:, 192:384].rearrange("p (k r) -> p k r", k=6)
        lim = scr(1)
        ang = x4s[:, 0, :].rearrange("p (t d) -> p t d", t=NT)
        turn = x4s[:, 1, :].rearrange("p (t d) -> p t d", t=NT)
        redu = early[:, :, :].rearrange("p k (t d) -> p k t d", t=NT)
        trig = x3s[:, :, :].rearrange("p k (t d) -> p k t d", t=NT)

        bank = [ctx.enter_context(nc.psum_tensor(f"bank{i}", [128, 512], F32)) for i in range(8)]
        ps_xT = [bank[0], bank[1]]
        ps_y = [bank[2], bank[3]]
        ps_wob = bank[3]
        ps_qkv = [bank[4], bank[5]]
        ps_idx = bank[6]
        ps_pre = bank[7]
        ps_sc = bank[0:3]
        ps_o = bank[3]
        ps_t = bank[4]
        ps_z = bank[5][0:E * R, 0:128]
        ps_l2 = bank[6][:, 0:D]
        ps_l3 = bank[7][:, 0:D]
        HEADS = [range(0, 3), range(3, 6), range(6, 8)]

        s_small, s_con, s_w = sem("s_small"), sem("s_con"), sem("s_w")
        s_rowi, s_num = sem("s_rowi"), sem("s_num")
        s_x = [sem(f"s_x{i}") for i in range(RING)]
        s_wb, s_pre2 = sem("s_wb"), sem("s_pre2")
        s_w0 = [sem(f"s_w0{i}") for i in range(RING)]
        s_w3 = [sem("s_w3a"), sem("s_w3b")]
        s_zero = sem("s_zero")
        s_ix = sem("s_ix")
        s_blkd, s_blkr = sem("s_blkd"), sem("s_blkr")
        s_ipe = sem("s_ipe")
        s_blk = sem("s_blk")
        s_redu = sem("s_redu")
        s_same = sem("s_same")
        s_canon = sem("s_canon")
        s_lists = sem("s_lists")
        s_rows = sem("s_rows")
        s_trig, s_rope = sem("s_trig"), sem("s_rope")
        s_pre, s_prec = sem("s_pre"), sem("s_prec")
        s_stage = [sem(f"s_stage{j}") for j in range(OWN)]
        s_init = sem("s_init")
        s_cache = [sem(f"s_cache{i}") for i in range(RING)]
        w0i_done, y_done, y_copied, zx_copied = sem("w0i_done"), sem("y_done"), sem("y_copied"), sem("zx_copied")
        xT_done, xT_copied, qkv_done = sem("xT_done"), sem("xT_copied"), sem("qkv_done")
        kq_copied, v_copied, sq_done = sem("kq_copied"), sem("v_copied"), sem("sq_done")
        ss_done, rt_done, rinv_done = sem("ss_done"), sem("rt_done"), sem("rinv_done")
        prods_done, rsum_done, krow_done = sem("prods_done"), sem("rsum_done"), sem("krow_done")
        qrot_done, qT_done = sem("qrot_done"), sem("qT_done")
        s_scat = [sem(f"s_scat{i}") for i in range(RING)]
        s_merge = [sem(f"s_merge{i}") for i in range(RING)]
        s_own = [sem(f"s_own{i}") for i in range(RING)]
        kT_part, kT_done = sem("kT_part"), sem("kT_done")
        qbd_done, mask_done, vold_done, vnew_done = sem("qbd_done"), sem("mask_done"), sem("vold_done"), sem("vnew_done")
        sc_done, mx_done, nmx_done, exp_done = sem("sc_done"), sem("mx_done"), sem("nmx_done"), sem("exp_done")
        pT_done, pv_done, oraw_done, rden_done = sem("pT_done"), sem("pv_done"), sem("oraw_done"), sem("rden_done")
        onrm_done, onT_done, onT_copied = sem("onrm_done"), sem("onT_done"), sem("onT_copied")
        z_done, zs_done, zm_done, l2_done, x3_done = sem("z_done"), sem("zs_done"), sem("zm_done"), sem("l2_done"), sem("x3_done")
        l3_done, x4_done = sem("l3_done"), sem("x4_done")
        s_out = [sem("s_outa"), sem("s_outb")]
        s_pad, s_big = sem("s_pad"), sem("s_big")
        row1_copied, row4_copied, rowm_copied, pos_copied = (
            sem("row1_copied"), sem("row4_copied"), sem("rowm_copied"), sem("pos_copied"))
        qrT_done, cross_done = sem("qrT_done"), sem("cross_done")
        desc_w0, s_w0i = sem("desc_w0"), sem("s_w0i")
        desc_init, desc_scat, desc_cache, desc_fetch = sem("desc_init"), sem("desc_scat"), sem("desc_cache"), sem("desc_fetch")

        ZEROED = 2
        P1 = (NT + 5, 8, 16, RING)
        P2 = (NT + 2, 4, 14)
        P2R = (NT + 2, 4, 12, RING)

        block = ctx.enter_context(nc.Block())

        @block.sync
        def _(sp):
            sp.dma_start(kv_i, kv_lens).then_inc(s_small, 16)
            sp.dma_start(tab_i, table_i).then_inc(s_small, 16)
            sp.dma_start(con[:, :], consts).then_inc(s_con, 16)
            sp.dma_start(row_i[:, :, :].rearrange("p k t -> p (k t)"), of_rows).then_inc(s_rowi, 16)
            sp.dma_start(subj_sb[:, :], subject).then_inc(s_num, 16)

            def phase1(h, u):
                t, k, p, r, n = at_step4(h, u, 0)
                if valid(t):
                    if not isinstance(t, int) or t >= RING:
                        sp.wait_ge(xT_done, t - 3)
                    sp.dma_start(xin[:, r, :], x[bass.ds(t * 128, 128), :]).then_inc(s_x[r], 16)

            steps(sp, phase1, NT, 4, NT, RING)

            sp.wait_ge(s_num, 16 * 5)
            sp.wait_ge(s_zero, ZEROED)

            def diagonal(t, p, weights, numbers, buf, signal):
                for b in range(NB):
                    n = sp.value_load(numbers[0:1, bass.ds(t * NB + b, 1)], min_val=0, max_val=weights.shape[0] - 1)
                    sp.dma_start(buf[32 * b:32 * b + 32, p, 32 * b:32 * b + 32],
                                 weights[bass.ds(n, 1), :, :].rearrange("o c d -> (o c) d")).then_inc(signal[p], 16)

            def phase2(h, u):
                t, k, p = at_step(h, u, 0)
                if valid(t):
                    if reused(t):
                        sp.wait_ge(l3_done, t - 1)
                    diagonal(t, p, w3, subj_sb, w3bd, s_w3)
                t, k, p = at_step(h, u, 1)
                if valid(t):
                    sp.wait_ge(x4_done, t + 1)
                    sp.dma_start(out[bass.ds(t * 128, 128), :], x4s[:, p, :]).then_inc(s_out[p], 16)

            steps(sp, phase2, NT + 1, 4, 14)
            for p in range(2):
                sp.wait_ge(s_out[p], 16 * (NT // 2))

        @block.gpsimd
        def _(pl):
            tick = pl.alloc_register("tick")
            pl.reg_mov(tick, 0)

            def wait(signal, n):
                if not isinstance(n, int):
                    pl.reg_mov(tick, n)
                    n = pl.snap(tick)
                    pl.wait_ge(s_rows, 1)
                pl.wait_ge(signal, n)

            pl.memset(w0i[:, :, :], 0.0).then_inc(s_zero, 1)
            pl.memset(w3bd[:, :, :], 0.0).then_inc(s_zero, 1)
            pl.memset(own[:, :, :], 0.0).then_inc(s_big, 1)

            def l0_weights(t):
                pl.indirect_dma_start(
                    out=w0c[:, t, :], out_offset=None, in_=w0_rows,
                    in_offset=bass.IndirectOffsetOnAxis(ap=w0_i[:, t:t + 1], axis=0),
                    bounds_check=w0_rows.shape[0] - 1, oob_is_err=False, engine_sem=desc_w0).then_inc(s_w0[t // 4], 16)
                wait(desc_w0, t + 1)

            wait(s_w0i, 1)
            for t in range(0, 6):
                l0_weights(t)

            wait(s_blk, 1)
            for j in range(OWN):
                pl.indirect_dma_start(
                    out=stage[:, j, :], out_offset=None, in_=pool_blocks,
                    in_offset=bass.IndirectOffsetOnAxis(ap=blk_i[:, BACK + j:BACK + j + 1], axis=0),
                    bounds_check=NPOOL - 1, oob_is_err=False, engine_sem=desc_init).then_inc(s_stage[j], 16)
                wait(desc_init, j + 1)

            wait(s_num, 16 * 5)
            pl.tensor_scalar(ksc[:, :], ksc[:, :], 1.0, None, ALU.add).then_inc(s_rope, 1)
            pl.tensor_scalar(qsc[:, :], qsc[:, :], 1.0, None, ALU.add).then_inc(s_rope, 1)
            wait(s_w, 16 * 7)
            for c in range(2):
                pl.tensor_tensor(wbase_sb[:, c, 128 * c:128 * c + 128], wbase_sb[:, c, 128 * c:128 * c + 128],
                                 ident, ALU.add).then_inc(s_wb, 1)
            for t in range(6, 9):
                l0_weights(t)
            wait(s_rope, 2)
            wait(s_trig, 2)
            for lo in range(2):
                for scl, k0, k1 in ((ksc, 0, 1), (qsc, 1, 3)):
                    n = k1 - k0
                    pl.tensor_tensor(
                        ropeC[:, :, lo, k0:k1, :], trig[:, 1].unsqueeze(2).broadcast_to([128, NT, n, half]),
                        scl[:, half * lo:half * lo + half].unsqueeze(1).unsqueeze(1).broadcast_to([128, NT, n, half]),
                        ALU.mult).then_inc(s_rope, 1)
            wait(s_rope, 6)
            for t in range(9, NT):
                l0_weights(t)

            def cached(t, r):
                pl.tensor_copy(row_now[:, 0, r:r + 1], idx[:, 0, bass.ds(t, 1)]).then_inc(row4_copied, 1)
                wait(row4_copied, t + 1)
                pl.indirect_dma_start(
                    out=kvb[:, r, :], out_offset=None, in_=pool_rows4,
                    in_offset=bass.IndirectOffsetOnAxis(ap=row_now[:, 0, r:r + 1], axis=0),
                    bounds_check=4 * NPOOL - 1, oob_is_err=False, engine_sem=desc_cache).then_inc(s_cache[r], 16)
                wait(desc_cache, t + 1)

            def masks(t, p):
                pl.tensor_copy(pos_now[:, :, p:p + 1], pos3[:, 0:2, bass.ds(t, 1)]).then_inc(pos_copied, 1)
                wait(pos_copied, t + 1)
                pl.tensor_scalar(mask[:, p, 0:NKB], cc("backpos"), pos_now[:, 0, p:p + 1], NEG,
                                 ALU.is_lt, ALU.mult).then_inc(mask_done, 1)
                pl.tensor_scalar(mask[:, p, NKB:NK], cc("ownpos"), pos_now[:, 1, p:p + 1], NEG,
                                 ALU.is_gt, ALU.mult).then_inc(mask_done, 1)

            def phase1(h, u):
                t, k, p, r, n = at_step4(h, u, 3)
                if valid(t):
                    wait(kq_copied, t + 1)
                    if reused(t):
                        wait(rsum_done, t - 1)
                    c = ropeC[:, bass.ds(t, 1)].rearrange("p o a k d -> p (o a k) d")
                    pl.tensor_tensor(ropeA[:, p, :].rearrange("p (k n d) -> p k n d", k=6, d=half),
                                     kqs[:, p, :].rearrange("p (k n d) -> p k n d", k=6, d=half),
                                     c.unsqueeze(2).broadcast_to([128, 6, G, half]), ALU.mult).then_inc(prods_done, 1)
                t, k, p, r, n = at_step4(h, u, 4)
                if valid(t):
                    if isinstance(t, int) and t == 0:
                        wait(s_rows, 1)
                        wait(s_init, 16 * OWN)
                    pl.tensor_copy(row_now[:, 3, r:r + 1], idx[:, 3, bass.ds(t, 1)]).then_inc(row1_copied, 1)
                    wait(row1_copied, t + 1)
                    wait(v_copied, t + 1)
                    wait(krow_done, t + 1)
                    pl.indirect_dma_start(
                        out=merged, out_offset=bass.IndirectOffsetOnAxis(ap=row_now[:, 3, r:r + 1], axis=0),
                        in_=kvrow[:, r, :], in_offset=None,
                        bounds_check=SEGS * BLOCK - 1, oob_is_err=False, engine_sem=desc_scat).then_inc(s_scat[r], 16)
                    wait(desc_scat, t + 1)
                if isinstance(h, int) and 4 <= 4 * h + u < 4 + RING:
                    cached(4 * h + u - 4, u % RING)
                if isinstance(h, int) and NT <= 4 * h + u < NT + 2:
                    masks(4 * h + u - NT, u % 2)

            steps(pl, phase1, *P1)

            wait(qT_done, NT)
            for p in range(2):
                pl.memset(prob[:, p, :, NK:KW], 0.0).then_inc(s_pad, 1)
            wait(s_big, 1)
            for r in range(RING):
                wait(s_scat[r], 16 * (NT // RING))

            def fetch(t, r, n):
                pl.tensor_copy(row_now[:, 1:3, r:r + 1], idx[:, 1:3, bass.ds(t, 1)]).then_inc(rowm_copied, 1)
                wait(rowm_copied, t + 1)
                wait(s_cache[r], 16 * (n + 1))
                pl.indirect_dma_start(
                    out=kvb[:, r, :], out_offset=None, in_=merged_rows4,
                    in_offset=bass.IndirectOffsetOnAxis(ap=row_now[:, 1, r:r + 1], axis=0),
                    bounds_check=SEGS * 4 - 1, oob_is_err=False, engine_sem=desc_fetch).then_inc(s_merge[r], 16)
                wait(desc_fetch, 2 * t + 1)
                pl.indirect_dma_start(
                    out=own[:, r, :], out_offset=None, in_=merged_rows2,
                    in_offset=bass.IndirectOffsetOnAxis(ap=row_now[:, 2, r:r + 1], axis=0),
                    bounds_check=SEGS * 8 - 1, oob_is_err=False, engine_sem=desc_fetch).then_inc(s_own[r], 16)
                wait(desc_fetch, 2 * t + 2)

            fetch(0, 0, 0)
            fetch(1, 1, 0)

            def phase2(h, u):
                t, k, p, r, n = at_step4(h, u, -1)
                if valid(t) and reused(t):
                    wait(sc_done, 3 * (t - 1))
                    masks(t, p)
                t, k, p, r, n = at_step4(h, u, -2)
                if valid(t):
                    if not isinstance(t, int) or t >= RING:
                        wait(kT_done, t - 3)
                        wait(vnew_done, NB * (t - 3))
                    fetch(t, r, n)
                t, k, p, r, n = at_step4(h, u, -4)
                if valid(t):
                    wait(kT_done, t - 3)
                    wait(vold_done, NB * (t - 3))
                    cached(t, r)

            steps(pl, phase2, NT, *P2R[1:])

        @block.scalar
        def _(act):
            for dst, src in ((qsc[:, :], qscale.broadcast_to([128, HD])), (ksc[:, :], kscale.broadcast_to([128, HD])),
                             (adp_i[:, :], adapter.broadcast_to([E * R, B])), (scal[:, :], scaling)):
                act.dma_start(dst, src).then_inc(s_num, 16)
            for dst, src in ((wqkv_sb[:, :, :], wqkv.rearrange("(c p) n -> p c n", p=128)),
                             (at_sb[:, :, :], at.rearrange("(c p) n -> p c n", p=128)),
                             (wt_sb[:, :, :], wt.rearrange("(c p) n -> p c n", p=128)),
                             (bt_sb[:, :, :], bt.rearrange("(c p) n -> p c n", p=128)),
                             (wp_sb[:, :, :], wp.rearrange("(c p) n -> p c n", p=128)),
                             (wo_rows[:, :, :], wo.rearrange("(c p) n -> p c n", p=128)),
                             (wbase_sb[:, :, :], wbase.rearrange("(c p) n -> p c n", p=128))):
                act.dma_start(dst, src).then_inc(s_w, 16)
            act.wait_ge(s_con, 16)
            act.copy(identb[:, :], ident).then_inc(s_prec, 1)
            act.wait_ge(s_blk, 1)
            act.dma_start(blocks_d, blk).then_inc(s_blkd, 16)
            act.wait_ge(s_blkd, 16)
            act.dma_start(allblk, blocks_d.rearrange("b i -> (b i)").unsqueeze(0).broadcast_to([B, B * SPAN])
                          ).then_inc(s_blkr, 16)
            act.wait_ge(s_pre, 1)
            act.copy(aw[:, :, :], ps_pre[:, 0:128].rearrange("p (c n) -> p c n", c=2)).then_inc(s_prec, 1)
            act.copy(bw[:, :], ps_pre[0:E * R, 128:384]).then_inc(s_prec, 1)
            act.wait_ge(s_redu, 1)
            for i in range(2):
                act.activation(trig[:, i], redu[:, i], ACT.Sin).then_inc(s_trig, 1)
            for j in range(OWN):
                act.wait_ge(s_stage[j], 16)
                act.dma_start(merged_blocks[B * j:B * j + B, :], stage[:, j, :]).then_inc(s_init, 16)
            act.wait_ge(s_pre2, 1)
            act.copy(aow[:, :, :], ps_pre[:, 384:512].rearrange("p (c n) -> p c n", c=2)).then_inc(s_prec, 1)
            act.copy(wob[:, :, :], ps_wob[:, :].rearrange("p (c n) -> p c n", c=2)).then_inc(s_prec, 1)

            def phase1(h, u):
                t, k, p, r, n = at_step4(h, u, 2)
                if valid(t):
                    act.wait_ge(qkv_done, t + 1)
                    if reused(t):
                        act.wait_ge(prods_done, t - 1)
                        act.wait_ge(cross_done, 2 * (t - 1))
                    act.copy(kqs[:, p, :], ps_qkv[p][:, 0:384]).then_inc(kq_copied, 1)
                    if reused(t):
                        act.wait_ge(ss_done, t - 1)
                    act.activation(sq[:, p, :], ps_qkv[p][:, 0:384], ACT.Square).then_inc(sq_done, 1)
                    if not isinstance(t, int) or t >= RING:
                        act.wait_ge(s_scat[r], 16 * n)
                    act.copy(kvrow[:, r, 128:256], ps_qkv[p][:, 384:512]).then_inc(v_copied, 1)
                t, k, p, r, n = at_step4(h, u, 1)
                if valid(t):
                    act.wait_ge(xT_done, t + 1)
                    if reused(t):
                        act.wait_ge(y_done, t - 1)
                    act.copy(x1T[:, p], ps_xT[p][:, 0:256].rearrange("p (c n) -> p c n", c=2)
                             ).then_inc(xT_copied, 1)
                t, k, p, r, n = at_step4(h, u, 2)
                if valid(t):
                    act.wait_ge(y_done, t + 1)
                    act.copy(yall[:, bass.ds(t, 1), :].rearrange("p o n -> p (o n)"), ps_y[p][:, 0:D]
                             ).then_inc(y_copied, 1)
                    act.copy(zx[:, bass.ds(t, 1), :].rearrange("p o n -> p (o n)"), ps_y[p][0:E * R, D:D + 128]
                             ).then_inc(zx_copied, 1)
                t, k, p, r, n = at_step4(h, u, 3)
                if valid(t):
                    act.wait_ge(ss_done, t + 1)
                    if reused(t):
                        act.wait_ge(rinv_done, t - 1)
                    act.activation(rt[:, p, :], ss[:, p, :], ACT.Sqrt).then_inc(rt_done, 1)
                t, k, p, r, n = at_step4(h, u, 5)
                if valid(t):
                    act.wait_ge(qrT_done, t + 1)
                    act.copy(qT[:, bass.ds(t, 1), :].rearrange("p o n -> p (o n)"), qrT[:, p, :]).then_inc(qT_done, 1)

            steps(act, phase1, *P1)
            act.wait_ge(s_init, 16 * OWN)
            act.wait_ge(qT_done, NT)

            def queries(t, p):
                if reused(t):
                    act.wait_ge(sc_done, 3 * (t - 1))
                for b in range(NB):
                    only = con[:, COL["batch"][0] + b:COL["batch"][0] + b + 1]
                    act.activation(qbd[:, p, :, 32 * b:32 * b + 32],
                                   qT[:, bass.ds(t, 1), :].rearrange("p o (h c) -> p (o h) c", h=H),
                                   ACT.Copy, scale=only).then_inc(qbd_done, 1)

            queries(0, 0)
            queries(1, 1)
            act.wait_ge(s_pad, 2)

            def phase2(h, u):
                t, k, p, r, n = at_step4(h, u, 0)
                t2, k2, p2, _, _ = at_step4(h, u, 2)
                if valid(t2):
                    act.wait_ge(onT_done, t2 + 1)
                    act.copy(onT[:, :, :], ps_t[:, 0:256].rearrange("p (c n) -> p c n", c=2)
                             ).then_inc(onT_copied, 1)
                for i in range(3):
                    if valid(t):
                        if i == 0 and reused(t):
                            act.wait_ge(pT_done, 3 * (t - 1))
                        act.wait_ge(nmx_done, 3 * t + i + 1)
                        for j, hd in enumerate(HEADS[i]):
                            act.activation(prob[:, p, hd, 0:NK], ps_sc[i][:, j * NK:j * NK + NK], ACT.Exp,
                                           bias=nmx[:, p, hd:hd + 1], scale=SCALE,
                                           accum_out=den[:, p, hd:hd + 1]).then_inc(exp_done, 1)
                if valid(t):
                    act.wait_ge(s_own[r], 16 * (n + 1))
                    if reused(t):
                        act.wait_ge(pv_done, t - 1)
                    new = own[:, r, :].rearrange("p (f k g d) -> p f k g d", f=2, k=2, g=G)
                    for b in range(NB):
                        act.activation(vbd[:, p, 4:6, :, 32 * b:32 * b + 32], new[:, :, 1], ACT.Copy,
                                       scale=con[:, COL["batch"][0] + b:COL["batch"][0] + b + 1]).then_inc(vnew_done, 1)
                t1, _, p1, _, _ = at_step4(h, u, -1)
                if valid(t1) and reused(t1):
                    queries(t1, p1)

            steps(act, phase2, *P2R)

        @block.vector
        def _(ve):
            count = [0]

            def link(ins):
                count[0] += 1
                ins.then_inc(s_ix, 1)
                ve.wait_ge(s_ix, count[0])

            ve.wait_ge(s_small, 32)
            ve.wait_ge(s_con, 16)
            link(ve.tensor_copy(kvf, kv_i))
            link(ve.tensor_copy(tabf, tab_i))
            link(ve.tensor_scalar(slot0, kvf, 1.0 / BLOCK, -7.5 / BLOCK, ALU.mult, ALU.add))
            link(ve.tensor_scalar(slot0, slot0, MAGIC, None, ALU.add))
            link(ve.tensor_scalar(slot0, slot0, -MAGIC, None, ALU.add))
            link(ve.scalar_tensor_tensor(out=off0, in0=slot0, scalar=-float(BLOCK), in1=kvf,
                                         op0=ALU.mult, op1=ALU.add))
            link(ve.tensor_scalar(target, cc("span", B), slot0, None, ALU.add))
            ve.wait_ge(s_rowi, 16)
            link(ve.tensor_copy(w0_f[:, :], row_i[:, 1, :]))
            link(ve.tensor_scalar(w0_f[:, :], w0_f[:, :], float(TOK), cc("rowtok"), ALU.mult, ALU.add))
            ve.tensor_copy(w0_i[:, :], w0_f[:, :]).then_inc(s_w0i, 1)
            for i in range(SPAN):
                link(ve.scalar_tensor_tensor(out=pick, in0=cc("slot", B), scalar=target[:, i:i + 1], in1=tabf,
                                             op0=ALU.is_equal, op1=ALU.mult, accum_out=blk[:, i:i + 1]))
            link(ve.tensor_scalar(bits[:, 0:1], off0, 8.0, None, ALU.is_ge))
            link(ve.scalar_tensor_tensor(out=rest[:, 0:1], in0=bits[:, 0:1], scalar=-8.0, in1=off0,
                                         op0=ALU.mult, op1=ALU.add))
            link(ve.tensor_scalar(bits[:, 1:2], rest[:, 0:1], 4.0, None, ALU.is_ge))
            link(ve.scalar_tensor_tensor(out=rest[:, 1:2], in0=bits[:, 1:2], scalar=-4.0, in1=rest[:, 0:1],
                                         op0=ALU.mult, op1=ALU.add))
            link(ve.tensor_scalar(bits[:, 2:3], rest[:, 1:2], 2.0, None, ALU.is_ge))
            link(ve.scalar_tensor_tensor(out=bits[:, 3:4], in0=bits[:, 2:3], scalar=-2.0, in1=rest[:, 1:2],
                                         op0=ALU.mult, op1=ALU.add))
            ve.tensor_copy(blk_i[:, :], blk).then_inc(s_blk, 1)

            ve.wait_ge(s_rowi, 16)
            link(ve.tensor_copy(rowpos[:, :], row_i[:, 0, :]))
            link(ve.tensor_scalar(rowpos[:, :], rowpos[:, :], cc("rowtok"), None, ALU.add))
            link(ve.tensor_tensor(ang, rowpos[:, :].unsqueeze(2).broadcast_to([128, NT, half]),
                                  cc("inv").unsqueeze(1).broadcast_to([128, NT, half]), ALU.mult))
            c1 = float(np.float32(6.28125))
            c2 = float(np.float32(np.round((2 * np.pi - c1) * 2.0 ** 21) / 2.0 ** 21))
            c3 = float(np.float32(2 * np.pi - c1 - c2))
            for i in range(2):
                link(ve.tensor_scalar(turn, ang, 1.0 / (2 * PI), 0.25 * i, ALU.mult, ALU.add))
                link(ve.tensor_scalar(turn, turn, MAGIC, None, ALU.add))
                link(ve.tensor_scalar(turn, turn, -MAGIC, None, ALU.add))
                link(ve.scalar_tensor_tensor(out=redu[:, i], in0=turn, scalar=-c1, in1=ang, op0=ALU.mult, op1=ALU.add))
                link(ve.scalar_tensor_tensor(out=redu[:, i], in0=turn, scalar=-c2, in1=redu[:, i],
                                             op0=ALU.mult, op1=ALU.add))
                link(ve.scalar_tensor_tensor(out=redu[:, i], in0=turn, scalar=-c3, in1=redu[:, i],
                                             op0=ALU.mult, op1=ALU.add))
                link(ve.tensor_scalar(redu[:, i], redu[:, i], i * PI / 2, PI, ALU.add, ALU.min))
                link(ve.tensor_scalar(redu[:, i], redu[:, i], -PI, None, ALU.max))
            ve.engine_nop().then_inc(s_redu, 1)
            link(ve.tensor_scalar(posf[:, 1, :], cc("tok", B), rest[:, 1:2], None, ALU.add))
            link(ve.tensor_tensor(lim, rest[:, 1:2], kvf, ALU.subtract))
            link(ve.tensor_scalar(lim, lim, float(WINDOW), None, ALU.add))
            link(ve.tensor_scalar(posf[:, 0, :], posf[:, 1, :], 1.0, lim, ALU.add, ALU.max))

            link(ve.tensor_scalar(cidx, blk, 4.0, None, ALU.mult))
            link(ve.tensor_tensor(rows4[:, 0, :].rearrange("p (i f) -> p i f", f=4),
                                  cidx[:, 0:9].unsqueeze(2).broadcast_to([B, 9, 4]),
                                  cc("m4", B).rearrange("p (i f) -> p i f", f=4), ALU.add))

            link(ve.tensor_scalar(cover[:, 0, :], cc("m16", B)[:, 0:17], off0, None, ALU.is_ge))
            link(ve.tensor_scalar(cover[:, 2, :], cc("m16", B)[:, 0:17], off0, None, ALU.is_lt))
            link(ve.memset(cover[:, 1, :], 1.0))
            link(ve.memset(cover[:, :, 16:17], 1.0))
            ve.wait_ge(s_num, 16 * 5)
            link(ve.tensor_copy(adp_f[:, :], adp_i[:, :]))
            link(ve.tensor_scalar(zscale[:, :], adp_f[:, :], cc("adapter", E * R), scal[:, 0:1],
                                  ALU.is_equal, ALU.mult))
            ve.wait_ge(s_rope, 2)
            ve.wait_ge(s_trig, 2)
            for lo in range(2):
                for k, scl in enumerate((ksc, qsc, qsc)):
                    link(ve.scalar_tensor_tensor(
                        out=ropeS[:, :, lo, k, :], in0=trig[:, 0], scalar=2.0 * lo - 1.0,
                        in1=scl[:, half - half * lo:HD - half * lo].unsqueeze(1).broadcast_to([128, NT, half]),
                        op0=ALU.mult, op1=ALU.mult))
            def same_blocks():
                ve.wait_ge(s_blkr, 16)
                for j in range(OWN):
                    link(ve.tensor_scalar(eq[j], allblk, blk[:, BACK + j:BACK + j + 1], None, ALU.is_equal))
                for j in range(OWN):
                    a = COL["later"][0] + j * B * OWN
                    link(ve.tensor_tensor(el[j].rearrange("p (b i) -> p b i", i=OWN),
                                          eq[j].rearrange("p (b i) -> p b i", i=SPAN)[:, :, BACK:SPAN],
                                          con[0:B, a:a + B * OWN].rearrange("p (b i) -> p b i", i=OWN), ALU.mult))
                ve.engine_nop().then_inc(s_same, 1)

            def segments():
                ve.wait_ge(s_ipe, 1)
                link(ve.tensor_copy(dead, ps_idx[0:B, 0:51].rearrange("p (j n) -> p j n", j=OWN)))
                link(ve.tensor_scalar(canon_seg, dead[:, :, 16], 0.0, None, ALU.is_equal))
                link(ve.tensor_tensor(canon_b, canon_seg, cc("seg1", B), ALU.mult))
                ve.engine_nop().then_inc(s_canon, 1)

            def lists_of_rows():
                ve.wait_ge(s_ipe, 2)
                link(ve.tensor_copy(canon, ps_idx[0:B, 64:64 + SPAN]))
                link(ve.tensor_scalar(cmiss, canon, 0.0, BIG, ALU.is_equal, ALU.mult))
                link(ve.tensor_scalar(cidx, canon, 4.0, -4.0, ALU.mult, ALU.add))
                link(ve.tensor_tensor(cidx, cidx, cmiss, ALU.add))
                link(ve.tensor_tensor(rows4[:, 1, :].rearrange("p (i f) -> p i f", f=4),
                                      cidx[:, 0:9].unsqueeze(2).broadcast_to([B, 9, 4]),
                                      cc("m4", B).rearrange("p (i f) -> p i f", f=4), ALU.add))
                link(ve.tensor_scalar(cidx, canon, 8.0, -8.0, ALU.mult, ALU.add))
                link(ve.tensor_tensor(rows2.rearrange("p (i f) -> p i f", f=8),
                                      cidx[:, BACK:SPAN].unsqueeze(2).broadcast_to([B, OWN, 8]),
                                      cc("m8", B).rearrange("p (i f) -> p i f", f=8), ALU.add))
                link(ve.tensor_scalar(cidx, canon, 16.0, -16.0, ALU.mult, ALU.add))
                link(ve.tensor_tensor(rows1.rearrange("p (i f) -> p i f", f=16),
                                      cidx[:, BACK:SPAN].unsqueeze(2).broadcast_to([B, OWN, 16]),
                                      cc("m16", B).rearrange("p (i f) -> p i f", f=16), ALU.add))
                link(ve.tensor_scalar(dead, dead, 1.0, BIG, ALU.is_ge, ALU.mult))
                link(ve.tensor_tensor(rows1.rearrange("p (i f) -> p i f", f=16),
                                      rows1.rearrange("p (i f) -> p i f", f=16), dead[:, :, 0:16], ALU.add))

            def shifted_lists():
                link(ve.memset(idxf[:, :, :], BIG))

                def shift(dst, tmp, src, by, bit):
                    n = dst.shape[-1]
                    s0 = src[:, :, 0:n] if len(src.shape) == 3 else src[:, 0:n]
                    s1 = src[:, :, by:by + n] if len(src.shape) == 3 else src[:, by:by + n]
                    tm = tmp[:, :, 0:n] if len(src.shape) == 3 else tmp[:, 0:n]
                    link(ve.tensor_tensor(tm, s1, s0, ALU.subtract))
                    link(ve.scalar_tensor_tensor(out=dst, in0=tm, scalar=bits[:, bit:bit + 1], in1=s0,
                                                 op0=ALU.mult, op1=ALU.add))

                shift(rows4b[:, :, 0:33], tmp4, rows4, 2, 0)
                shift(idxf[:, 0:2, :], tmp4, rows4b, 1, 1)
                shift(rows2b[:, 0:20], tmp2, rows2, 4, 0)
                shift(idxf[:, 2, 0:Q2], tmp2, rows2b, 2, 1)
                shift(rows1b[:, 0:39], tmp1, rows1, 8, 0)
                shift(rows1[:, 0:35], tmp1, rows1b, 4, 1)
                shift(rows1b[:, 0:33], tmp1, rows1, 2, 2)
                shift(idxf[:, 3, :], tmp1, rows1b, 1, 3)
                link(ve.tensor_tensor(spread, lists.unsqueeze(2).broadcast_to([B, 6, NB, TOK]),
                                      cc("place", B).unsqueeze(1).unsqueeze(3).broadcast_to([B, 6, NB, TOK]), ALU.mult))
                ve.engine_nop().then_inc(s_lists, 1)

            def rows_of_tiles():
                ve.wait_ge(s_ipe, 3)
                link(ve.tensor_copy(idx[:, :, :], ps_idx[:, 128:192].rearrange("p (k t) -> p k t", k=4)))
                link(ve.tensor_copy(pos3[:, :, :], ps_idx[:, 192:224].rearrange("p (k t) -> p k t", k=2)))
                ve.engine_nop().then_inc(s_rows, 1)

            AFTER = {0: same_blocks, 1: segments, 2: lists_of_rows, 3: shifted_lists, 4: rows_of_tiles}

            def phase1(h, u):
                t, k, p, r, n = at_step4(h, u, 0)
                if valid(t):
                    if isinstance(t, int) and t == 0:
                        ve.wait_ge(s_zero, ZEROED)
                    if isinstance(t, int) and t in (0, 4):
                        ve.wait_ge(s_w0[t // 4], 64)
                    if isinstance(t, int) and t == 7:
                        ve.wait_ge(s_w0[2], 64)
                        ve.wait_ge(s_w0[3], 64)
                    if reused(t):
                        ve.wait_ge(xT_done, t - 1)
                    for b in range(NB):
                        rows = slice(32 * b, 32 * b + 32)
                        ve.tensor_tensor(w0i[rows, p, rows], w0c[rows, bass.ds(t, 1), :].rearrange("p o n -> p (o n)"),
                                         ident[rows, rows], ALU.add).then_inc(w0i_done, 1)
                t, k, p, r, n = at_step4(h, u, 3)
                if valid(t):
                    ve.wait_ge(sq_done, t + 1)
                    if reused(t):
                        ve.wait_ge(rt_done, t - 1)
                    ve.tensor_reduce(ss[:, p, :], sq[:, p, :].rearrange("p (a n d) -> p n a d", a=2, d=half), AX_XY,
                                     ALU.add).then_inc(kT_part, 1)
                    ve.wait_ge(kq_copied, t + 1)
                    sn = ropeS[:, bass.ds(t, 1)].rearrange("p o a k d -> p (o a k) d")
                    for lo in range(2):
                        ve.tensor_tensor(
                            ropeB[:, p, 192 * lo:192 * lo + 192].rearrange("p (k n d) -> p k n d", k=3, d=half),
                            kqs[:, p, 192 - 192 * lo:384 - 192 * lo].rearrange("p (k n d) -> p k n d", k=3, d=half),
                            sn[:, 3 * lo:3 * lo + 3].unsqueeze(2).broadcast_to([128, 3, G, half]),
                            ALU.mult).then_inc(cross_done, 1)
                        if lo == 0:
                            ve.wait_ge(kT_part, t + 1)
                            ve.tensor_scalar(ss[:, p, :], ss[:, p, :], 1.0 / HD, EPS, ALU.mult, ALU.add
                                             ).then_inc(ss_done, 1)
                t, k, p, r, n = at_step4(h, u, 4)
                if valid(t):
                    ve.wait_ge(prods_done, t + 1)
                    ve.wait_ge(cross_done, 2 * (t + 1))
                    ve.tensor_tensor(rsum[:, p, :], ropeA[:, p, :], ropeB[:, p, :], ALU.add).then_inc(rsum_done, 1)
                    ve.wait_ge(rt_done, t + 1)
                    ve.reciprocal(rinv[:, p, :], rt[:, p, :]).then_inc(rinv_done, 1)
                    ve.wait_ge(rsum_done, t + 1)
                    ve.wait_ge(rinv_done, t + 1)
                    if not isinstance(t, int) or t >= RING:
                        ve.wait_ge(s_scat[r], 16 * n)
                    halves = rsum[:, p, :].rearrange("p (a n d) -> p a n d", a=2, d=half)
                    ve.tensor_tensor(qrot[:, p, :].rearrange("p (n a d) -> p a n d", a=2, d=half),
                                     halves[:, :, G:12, :],
                                     rinv[:, p, G:12].unsqueeze(1).unsqueeze(3).broadcast_to([128, 2, H, half]),
                                     ALU.mult).then_inc(qrot_done, 1)
                    ve.tensor_tensor(kvrow[:, r, 0:128].rearrange("p (n a d) -> p a n d", a=2, d=half),
                                     halves[:, :, 0:G, :],
                                     rinv[:, p, 0:G].unsqueeze(1).unsqueeze(3).broadcast_to([128, 2, G, half]),
                                     ALU.mult).then_inc(krow_done, 1)
                    ve.wait_ge(qrot_done, t + 1)
                    if reused(t):
                        ve.wait_ge(qT_done, t - 1)
                    ve.transpose(qrT[:, p, :], qrot[:, p, :]).then_inc(qrT_done, 1)
                if isinstance(h, int) and 4 * h + u in AFTER:
                    AFTER[4 * h + u]()

            steps(ve, phase1, *P1)

            def keys(t, p, r, n):
                ve.wait_ge(s_merge[r], 16 * (n + 1))
                ve.wait_ge(s_own[r], 16 * (n + 1))
                if reused(t):
                    ve.wait_ge(sc_done, 3 * (t - 1))
                old = kvb[:, r, :].rearrange("p (f k g d) -> p f k g d", f=4, k=2, g=G)
                new = own[:, r, :].rearrange("p (f k g d) -> p f k g d", f=2, k=2, g=G)
                ve.transpose(kT[:, p, :, 0:NKB].rearrange("p g (f r) -> p f g r", f=4), old[:, :, 0])
                ve.transpose(kT[:, p, :, NKB:NKB + 32], new[:, 0, 0]).then_inc(kT_part, 1)
                ve.wait_ge(kT_part, NT + t + 1)
                ve.transpose(kT[:, p, :, NKB + Q2:NKB + Q2 + 32], new[:, 1, 0]).then_inc(kT_done, 1)

            def values(t, p, r, n):
                if reused(t):
                    ve.wait_ge(pv_done, t - 1)
                old = kvb[:, r, :].rearrange("p (f k g d) -> p f k g d", f=4, k=2, g=G)
                for b in range(NB):
                    ve.tensor_scalar(vbd[:, p, 0:4, :, 32 * b:32 * b + 32], old[:, :, 1],
                                     con[:, COL["batch"][0] + b:COL["batch"][0] + b + 1], None,
                                     ALU.mult).then_inc(vold_done, 1)

            keys(0, 0, 0, 0)
            keys(1, 1, 1, 0)
            ve.wait_ge(s_pad, 2)

            def maxima(t, p, i):
                a, n = HEADS[i][0], len(HEADS[i])
                ve.wait_ge(sc_done, 3 * t + i + 1)
                ve.tensor_reduce(mx[:, p, a:a + n], ps_sc[i][:, 0:n * NK].rearrange("p (n k) -> p n k", n=n),
                                 AX_X, ALU.max).then_inc(mx_done, 1)

            def negated(t, p, i):
                a, n = HEADS[i][0], len(HEADS[i])
                ve.wait_ge(mx_done, 3 * t + i + 1)
                ve.tensor_scalar(nmx[:, p, a:a + n], mx[:, p, a:a + n], -SCALE, None, ALU.mult).then_inc(nmx_done, 1)

            def phase2(h, u):
                t, k, p, r, n = at_step4(h, u, 0)
                t2, k2, p2, _, _ = at_step4(h, u, 2)
                if valid(t2):
                    ve.wait_ge(pv_done, t2 + 1)
                    ve.transpose(oraw[:, :], ps_o[:, 0:256]).then_inc(oraw_done, 1)
                    ve.wait_ge(oraw_done, t2 + 1)
                    ve.wait_ge(rden_done, t2 + 1)
                    ve.tensor_tensor(onrm[:, :].rearrange("p (n d) -> p n d", d=HD),
                                     oraw[:, :].rearrange("p (n d) -> p n d", d=HD),
                                     rden[:, p2, :].unsqueeze(2).broadcast_to([128, H, HD]),
                                     ALU.mult).then_inc(onrm_done, 1)
                if valid(t):
                    maxima(t, p, 0)
                    maxima(t, p, 1)
                    negated(t, p, 0)
                if valid(t2):
                    ve.wait_ge(z_done, t2 + 1)
                    ve.tensor_tensor(zs[:, :], ps_z, zx[:, bass.ds(t2, 1), :].rearrange("p o n -> p (o n)"),
                                     ALU.add).then_inc(zs_done, 1)
                if valid(t):
                    negated(t, p, 1)
                    maxima(t, p, 2)
                if valid(t2):
                    ve.wait_ge(zs_done, t2 + 1)
                    ve.tensor_tensor(zm[:, :].rearrange("p (b c) -> p b c", b=NB),
                                     zs[:, :].rearrange("p (b c) -> p b c", b=NB),
                                     zscale[:, bass.ds(t2 * NB, NB)].unsqueeze(2).broadcast_to([E * R, NB, TOK]),
                                     ALU.mult).then_inc(zm_done, 1)
                if valid(t):
                    negated(t, p, 2)
                if valid(t):
                    values(t, p, r, n)
                if valid(t2):
                    ve.wait_ge(l2_done, t2 + 1)
                    ve.tensor_tensor(x3s[:, p2, :], yall[:, bass.ds(t2, 1), :].rearrange("p o n -> p (o n)"),
                                     ps_l2, ALU.add).then_inc(x3_done, 1)
                t1, _, p1, r1, n1 = at_step4(h, u, -1)
                if valid(t1) and reused(t1):
                    keys(t1, p1, r1, n1)
                if valid(t):
                    if reused(t):
                        ve.wait_ge(pv_done, t - 1)
                    ve.wait_ge(exp_done, H * (t + 1))
                    for f0, f1, a in ((0, 4, 0), (4, 5, NKB), (5, 6, NKB + Q2)):
                        ve.transpose(pT[:, p, f0:f1, :].rearrange("p f (h c) -> p h f c", h=H),
                                     prob[:, p, :, a:a + 32 * (f1 - f0)].rearrange("p h (f c) -> p h f c", c=32)
                                     ).then_inc(pT_done, 1)
                    ve.reciprocal(rden[:, p, :], den[:, p, :]).then_inc(rden_done, 1)
                if valid(t2):
                    ve.wait_ge(l3_done, t2 + 1)
                    if reused(t2):
                        ve.wait_ge(s_out[p2], 16 * k2)
                    ve.tensor_tensor(x4s[:, p2, :], x3s[:, p2, :], ps_l3, ALU.add).then_inc(x4_done, 1)

            steps(ve, phase2, *P2R)

        @block.tensor
        def _(pe):
            pe.wait_ge(s_w, 16 * 7)
            for m in range(2):
                for c in range(2):
                    pe.matmul(ps_pre[:, 64 * m:64 * m + 64], wt_sb[:, c, 128 * m:128 * m + 128], at_sb[:, c, :],
                              start=(c == 0), stop=(c == 1))
            for c in range(2):
                mm = pe.matmul(ps_pre[0:E * R, 128:384], bt_sb[:, c, :], wp_sb[:, c, :], start=(c == 0), stop=(c == 1))
            mm.then_inc(s_pre, 1)
            pe.wait_ge(s_wb, 2)
            for m in range(2):
                for c in range(2):
                    pe.matmul(ps_wob[:, D * m:D * m + D], wo_rows[:, c, 128 * m:128 * m + 128], wbase_sb[:, c, :],
                              start=(c == 0), stop=(c == 1))
            pe.wait_ge(s_prec, 3)
            for m in range(2):
                for c in range(2):
                    mm = pe.matmul(ps_pre[:, 384 + 64 * m:448 + 64 * m], wo_rows[:, c, 128 * m:128 * m + 128],
                                   aw[:, c, :], start=(c == 0), stop=(c == 1))
            mm.then_inc(s_pre2, 1)

            def dead_tokens():
                pe.wait_ge(s_same, 1)
                for i in range(OWN):
                    for j in range(OWN):
                        mm = pe.matmul(ps_idx[0:B, 17 * i:17 * i + 17],
                                       el[j].rearrange("p (b i) -> p i b", i=OWN)[:, i], cover[:, j, :],
                                       start=(j == 0), stop=(j == OWN - 1))
                mm.then_inc(s_ipe, 1)

            def canonical():
                pe.wait_ge(s_canon, 1)
                for i in range(SPAN):
                    for j in range(OWN):
                        mm = pe.matmul(ps_idx[0:B, 64 + i:65 + i], eq[j].rearrange("p (b i) -> p i b", i=SPAN)[:, i],
                                       canon_b[:, j:j + 1], start=(j == 0), stop=(j == OWN - 1))
                mm.then_inc(s_ipe, 1)

            def tiles():
                pe.wait_ge(s_lists, 1)
                for kind in range(6):
                    mm = pe.matmul(ps_idx[:, 128 + NT * kind:128 + NT * kind + NT],
                                   spread[:, kind].rearrange("p b r -> p (b r)"), cc("tile", B), start=True, stop=True)
                mm.then_inc(s_ipe, 1)

            INDEX = {1: dead_tokens, 2: canonical, 4: tiles}

            def phase1(h, u):
                t, k, p, r, n = at_step4(h, u, 1)
                if valid(t):
                    pe.wait_ge(s_x[r], 16 * (n + 1))
                    pe.wait_ge(w0i_done, NB * (t + 1))
                    if reused(t):
                        pe.wait_ge(xT_copied, t - 1)
                    for c in range(2):
                        mm = pe.matmul(ps_xT[p][:, 128 * c:128 * c + 128], xin[:, r, 128 * c:128 * c + 128],
                                       w0i[:, p, :], start=True, stop=True)
                    mm.then_inc(xT_done, 1)
                if isinstance(h, int) and 4 * h + u in INDEX:
                    INDEX[4 * h + u]()
                t, k, p, r, n = at_step4(h, u, 2)
                if valid(t):
                    pe.wait_ge(xT_copied, t + 1)
                    if reused(t):
                        pe.wait_ge(kq_copied, t - 1)
                        pe.wait_ge(sq_done, t - 1)
                        pe.wait_ge(v_copied, t - 1)
                    for c in range(2):
                        mm = pe.matmul(ps_qkv[p][:, :], x1T[:, p, c, :], wqkv_sb[:, c, :], start=(c == 0), stop=(c == 1))
                    mm.then_inc(qkv_done, 1)
                    if isinstance(t, int) and t < 2:
                        pe.wait_ge(s_prec, 5)
                    if reused(t):
                        pe.wait_ge(y_copied, t - 1)
                        pe.wait_ge(zx_copied, t - 1)
                    for c in range(2):
                        pe.matmul(ps_y[p][:, 0:D], x1T[:, p, c, :], wbase_sb[:, c, :], start=(c == 0), stop=(c == 1))
                    for c in range(2):
                        mm = pe.matmul(ps_y[p][0:E * R, D:D + 128], aw[:, c, :], x1T[:, p, c, :],
                                       start=(c == 0), stop=(c == 1))
                    mm.then_inc(y_done, 1)

            steps(pe, phase1, *P1)

            pe.wait_ge(kq_copied, NT)
            pe.wait_ge(sq_done, NT)
            pe.wait_ge(v_copied, NT)
            pe.wait_ge(y_copied, NT)
            pe.wait_ge(zx_copied, NT)

            def scores(t, p, i):
                if i == 0:
                    pe.wait_ge(kT_done, t + 1)
                    pe.wait_ge(qbd_done, NB * (t + 1))
                    pe.wait_ge(mask_done, 2 * (t + 1))
                if not isinstance(t, int) or t >= 1:
                    pe.wait_ge(exp_done, H * t - H + HEADS[i][-1] + 1)
                n = len(HEADS[i])
                pe.matmul(ps_sc[i][:, 0:n * NK], identb[:, :],
                          mask[:, p, :].unsqueeze(1).broadcast_to([128, n, NK]), start=True, stop=False,
                          skip_group_check=True)
                for j, hd in enumerate(HEADS[i]):
                    mm = pe.matmul(ps_sc[i][:, j * NK:j * NK + NK], qbd[:, p, hd, :], kT[:, p, hd // GSZ, 0:NK],
                                   start=False, stop=(j == n - 1), skip_group_check=True)
                mm.then_inc(sc_done, 1)

            def weighted(t, p, groups):
                if groups[0] == 0:
                    pe.wait_ge(pT_done, 3 * (t + 1))
                    pe.wait_ge(vold_done, NB * (t + 1))
                    pe.wait_ge(vnew_done, NB * (t + 1))
                    if not isinstance(t, int) or t >= 1:
                        pe.wait_ge(oraw_done, t)
                for g in groups:
                    for f in range(6):
                        mm = pe.matmul(ps_o[:, 64 * g:64 * g + 64], vbd[:, p, f, g, :], pT[:, p, f, 64 * g:64 * g + 64],
                                       start=(f == 0), stop=(f == 5))
                if groups[-1] == G - 1:
                    mm.then_inc(pv_done, 1)

            def phase2(h, u):
                t, k, p = at_step(h, u, 0)
                t1, k1, p1 = at_step(h, u, 1)
                t2, k2, p2 = at_step(h, u, 2)
                if valid(t):
                    scores(t, p, 0)
                if valid(t2):
                    pe.wait_ge(onrm_done, t2 + 1)
                    for c in range(2):
                        mm = pe.transpose(ps_t[:, 128 * c:128 * c + 128], onrm[:, 128 * c:128 * c + 128], ident)
                    mm.then_inc(onT_done, 1)
                if valid(t):
                    scores(t, p, 1)
                if valid(t2):
                    pe.wait_ge(onT_copied, t2 + 1)
                    if not isinstance(t2, int) or t2 >= 1:
                        pe.wait_ge(zs_done, t2)
                        pe.wait_ge(x3_done, t2)
                    for c in range(2):
                        mm = pe.matmul(ps_z, aow[:, c, :], onT[:, c, :], start=(c == 0), stop=(c == 1))
                    mm.then_inc(z_done, 1)
                if valid(t):
                    scores(t, p, 2)
                if valid(t2):
                    for c in range(2):
                        pe.matmul(ps_l2, onT[:, c, :], wob[:, c, :], start=(c == 0), stop=False)
                if valid(t1):
                    weighted(t1, p1, [0])
                if valid(t2):
                    pe.wait_ge(zm_done, t2 + 1)
                    pe.matmul(ps_l2, zm[:, :], bw[:, :], start=False, stop=True).then_inc(l2_done, 1)
                if valid(t1):
                    weighted(t1, p1, [1])
                    weighted(t1, p1, [2])
                if valid(t2):
                    pe.wait_ge(x3_done, t2 + 1)
                    pe.wait_ge(s_w3[p2], 64 * (k2 + 1))
                    if not isinstance(t2, int) or t2 >= 1:
                        pe.wait_ge(x4_done, t2)
                    pe.matmul(ps_l3, w3bd[:, p2, :], x3s[:, p2, :], start=True, stop=True).then_inc(l3_done, 1)
                if valid(t1):
                    weighted(t1, p1, [3])

            steps(pe, phase2, *P2)


def kernel(**inputs):
    import concourse.bacc as _bacc
    from concourse.bass_utils import run_bass_kernel_spmd as _run

    a = {k: np.asarray(v) for k, v in inputs.items()}
    kb, vb = a["L1_cond_k_blocks"], a["L1_cond_v_blocks"]
    pool = np.stack([kb.transpose(0, 2, 1, 3), vb.transpose(0, 2, 1, 3)], axis=2).reshape(NPOOL * BLOCK, ROW)
    arrays = {
        "x": a["x"].reshape(B * TOK, D),
        "table": a["itok_Bx257_0_4111"],
        "kv_lens": a["itok_B_37_3939"].reshape(B, 1),
        "of_rows": np.repeat(np.concatenate([a["itok_B_37_3939"].reshape(NT, NB).T,
                                             a["itok_B_1_198"].reshape(NT, NB).T], axis=1), TOK, axis=0),
        "adapter": a["itok_B_0_3"].reshape(1, B),
        "subject": a["itok_B_0_7"].reshape(1, B),
        "w0": a["L0_cond_weights"],
        "wqkv": np.concatenate([
            np.concatenate([a["L1_cond_Wk"], a["L1_cond_Wq"]], axis=0).reshape(G + H, 2, HD // 2, D)
            .transpose(1, 0, 2, 3).reshape((G + H) * HD, D), a["L1_cond_Wv"]], axis=0).T,
        "wo": a["L1_cond_Wo"],
        "qscale": a["L1_cond_q_norm_scale"].reshape(1, HD),
        "kscale": a["L1_cond_k_norm_scale"].reshape(1, HD),
        "pool": pool,
        "wbase": a["L2_cond_W_base"].T,
        "wt": a["L2_cond_Wt"],
        "at": a["L2_cond_A"].reshape(E * R, D).T,
        "bt": a["L2_cond_B_w"].transpose(1, 0, 2).reshape(D, E * R),
        "wp": a["L2_cond_Wp"].T,
        "scaling": np.repeat(a["L2_cond_scaling"], R).reshape(E * R, 1),
        "w3": a["L3_cond_weights"],
        "consts": constants(),
    }
    nc = _bacc.Bacc("TRN2", target_bir_lowering=False, num_devices=1)
    arrays = {f"in_{k}": np.ascontiguousarray(v) for k, v in arrays.items()}
    args = [nc.dram_tensor(k, v.shape, mybir.dt.from_np(v.dtype), kind="ExternalInput").ap()
            for k, v in arrays.items()]
    out = nc.dram_tensor("out", (B * TOK, D), F32, kind="ExternalOutput").ap()
    build(nc, *args, out)
    r = _run(nc, [arrays], core_ids=[0])
    return r.results[0]["out"].reshape(B, TOK, D)
```
